# Optimizing a Trainium2 kernel written in Bass

```python
import numpy as np
import jax
import jax.numpy as jnp

def _softmax(x, axis=-1):
    return jax.nn.softmax(x, axis=axis)

def _gelu(x):
    return jax.nn.gelu(x, approximate=True)

def _silu(x):
    return jax.nn.silu(x)

def _sigmoid(x):
    return jax.nn.sigmoid(x)

def _layernorm(x, axis=-1, eps=1e-05):
    m = jnp.mean(x, axis=axis, keepdims=True)
    v = jnp.var(x, axis=axis, keepdims=True)
    return (x - m) / jnp.sqrt(v + eps)

def _scatter_add(tgt, idx, src, axis=0):
    return tgt.at[idx].add(src)

def _segment_sum(src, seg, n):
    return jax.ops.segment_sum(src, seg, n)
kernel_name = 'mk_vit_tower_postln_d1_tok_img512_r4_a0223d'

def setup_inputs(seed: int=0):
    np.random.seed(seed)
    _w = jnp.asarray

    def _rec_inputs():
        import jax
        import jax.numpy as jnp
        _rk = jax.random.key(seed)
        x = 7.57192e-06 + 1.00007 * jax.random.normal(jax.random.fold_in(_rk, 1), (128, 3, 224, 224), jnp.float32)
        return x
    x = _rec_inputs()

    def _L0_tok_setup():
        import jax, jax.numpy as jnp
        import numpy as np
        DEPTH = 4
        HEADS = 8
        DIM = 128
        HID = 256
        P = 16
        IMG = 224
        GRID = IMG // P
        NPATCH = GRID * GRID
        NTOK = NPATCH + 1
        BATCH = 64
        EPS = 1e-05

        def layernorm(x, w, b):
            mu = jnp.mean(x, axis=-1, keepdims=True)
            var = jnp.mean(jnp.square(x - mu), axis=-1, keepdims=True)
            return (x - mu) * jax.lax.rsqrt(var + EPS) * w + b
        key = jax.random.key(seed)
        ks = jax.random.split(key, 12)
        s = 0.02
        inp = {'x': jax.random.normal(ks[0], (BATCH, 3, IMG, IMG), jnp.float32), 'conv_w': jax.random.normal(ks[1], (3 * P * P, DIM), jnp.float32) * s, 'conv_b': jnp.zeros((DIM,), jnp.float32), 'cls_token': jax.random.normal(ks[2], (1, 1, DIM), jnp.float32) * s, 'pos_embed': jax.random.normal(ks[3], (1, NTOK, DIM), jnp.float32) * s, 'ln1_w': jnp.ones((DEPTH, DIM), jnp.float32), 'ln1_b': jnp.zeros((DEPTH, DIM), jnp.float32), 'qkv_w': jax.random.normal(ks[4], (DEPTH, DIM, 3 * DIM), jnp.float32) * s, 'qkv_b': jnp.zeros((DEPTH, 3 * DIM), jnp.float32), 'proj_w': jax.random.normal(ks[5], (DEPTH, DIM, DIM), jnp.float32) * s, 'proj_b': jnp.zeros((DEPTH, DIM), jnp.float32), 'ln2_w': jnp.ones((DEPTH, DIM), jnp.float32), 'ln2_b': jnp.zeros((DEPTH, DIM), jnp.float32), 'fc1_w': jax.random.normal(ks[6], (DEPTH, DIM, HID), jnp.float32) * s, 'fc1_b': jnp.zeros((DEPTH, HID), jnp.float32), 'fc2_w': jax.random.normal(ks[7], (DEPTH, HID, DIM), jnp.float32) * s, 'fc2_b': jnp.zeros((DEPTH, DIM), jnp.float32), 'norm_w': jnp.ones((DIM,), jnp.float32), 'norm_b': jnp.zeros((DIM,), jnp.float32)}
        return inp
    _L0_tok_all = _L0_tok_setup()
    _L0_tok_in = {k: v for k, v in _L0_tok_all.items() if k in ('conv_w', 'conv_b', 'cls_token', 'pos_embed', 'ln1_w', 'ln1_b', 'qkv_w', 'qkv_b', 'proj_w', 'proj_b', 'ln2_w', 'ln2_b', 'fc1_w', 'fc1_b', 'fc2_w', 'fc2_b', 'norm_w', 'norm_b')}
    del _L0_tok_all

    def _L0_attn_setup():
        import jax, jax.numpy as jnp
        import numpy as np
        import math
        D_MODEL = 128
        D_STATE = 64
        CHUNK = 4
        NC = D_MODEL // CHUNK
        B_SZ, L_SEQ = (8, 1024)

        def _layernorm(x, g, b, eps=1e-05):
            mu = jnp.mean(x, axis=-1, keepdims=True)
            var = jnp.mean((x - mu) ** 2, axis=-1, keepdims=True)
            return (x - mu) * jax.lax.rsqrt(var + eps) * g + b
        key = jax.random.key(seed)
        ks = jax.random.split(key, 10)
        x = jax.random.normal(ks[0], (B_SZ, L_SEQ, D_MODEL), dtype=jnp.float32)
        ln_gamma = jnp.ones((D_MODEL,), jnp.float32)
        ln_beta = jnp.zeros((D_MODEL,), jnp.float32)
        Win = jax.random.normal(ks[1], (D_MODEL, D_MODEL), jnp.float32) / math.sqrt(D_MODEL)
        bin_ = jnp.zeros((D_MODEL,), jnp.float32)
        Wout = jax.random.normal(ks[2], (D_MODEL, D_MODEL), jnp.float32) / math.sqrt(D_MODEL)
        bout = jnp.zeros((D_MODEL,), jnp.float32)
        Lambda_re = -0.5 * jnp.ones((NC, D_STATE), jnp.float32)
        Lambda_im = jnp.broadcast_to(jnp.arange(D_STATE, dtype=jnp.float32) * 2.0 * math.pi / D_STATE, (NC, D_STATE))
        Bmat = jax.random.normal(ks[3], (NC, D_STATE), jnp.float32)
        C_re = jax.random.normal(ks[4], (NC, D_STATE), jnp.float32)
        C_im = jax.random.normal(ks[5], (NC, D_STATE), jnp.float32)
        Dvec = jax.random.normal(ks[6], (NC,), jnp.float32)
        return {'x': x, 'ln_gamma': ln_gamma, 'ln_beta': ln_beta, 'Win': Win, 'bin_': bin_, 'Wout': Wout, 'bout': bout, 'Lambda_re': Lambda_re, 'Lambda_im': Lambda_im, 'Bmat': Bmat, 'C_re': C_re, 'C_im': C_im, 'Dvec': Dvec}
    _L0_attn_all = _L0_attn_setup()
    _L0_attn_in = {k: v for k, v in _L0_attn_all.items() if k in ('ln_gamma', 'ln_beta', 'Win', 'bin_', 'Wout', 'bout', 'Lambda_re', 'Lambda_im', 'Bmat', 'C_re', 'C_im', 'Dvec')}
    del _L0_attn_all

    def _L0_ffn_setup():
        import jax, jax.numpy as jnp
        import numpy as np
        B, N, D, E = (8, 2048, 128, 8)
        H = 2 * D
        key = jax.random.key(seed)
        ks = jax.random.split(key, 7)
        s = 0.02
        return {'x': jax.random.normal(ks[0], (B, N, D), dtype=jnp.float32), 'W1': jax.random.normal(ks[1], (E, D, H), dtype=jnp.float32) * s, 'b1': jnp.zeros((E, H), dtype=jnp.float32), 'W2': jax.random.normal(ks[2], (E, H, D), dtype=jnp.float32) * s, 'b2': jnp.zeros((E, D), dtype=jnp.float32), 'Wg': jax.random.normal(ks[3], (D, E), dtype=jnp.float32) * s, 'bg': jnp.zeros((E,), dtype=jnp.float32)}
    _L0_ffn_all = _L0_ffn_setup()
    _L0_ffn_in = {k: v for k, v in _L0_ffn_all.items() if k in ('W1', 'b1', 'W2', 'b2', 'Wg', 'bg')}
    del _L0_ffn_all
    return {'x': x, 'L0_tok_conv_w': _L0_tok_in['conv_w'], 'L0_tok_conv_b': _L0_tok_in['conv_b'], 'L0_tok_cls_token': _L0_tok_in['cls_token'], 'L0_tok_pos_embed': _L0_tok_in['pos_embed'], 'L0_tok_ln1_w': _L0_tok_in['ln1_w'], 'L0_tok_ln1_b': _L0_tok_in['ln1_b'], 'L0_tok_qkv_w': _L0_tok_in['qkv_w'], 'L0_tok_qkv_b': _L0_tok_in['qkv_b'], 'L0_tok_proj_w': _L0_tok_in['proj_w'], 'L0_tok_proj_b': _L0_tok_in['proj_b'], 'L0_tok_ln2_w': _L0_tok_in['ln2_w'], 'L0_tok_ln2_b': _L0_tok_in['ln2_b'], 'L0_tok_fc1_w': _L0_tok_in['fc1_w'], 'L0_tok_fc1_b': _L0_tok_in['fc1_b'], 'L0_tok_fc2_w': _L0_tok_in['fc2_w'], 'L0_tok_fc2_b': _L0_tok_in['fc2_b'], 'L0_tok_norm_w': _L0_tok_in['norm_w'], 'L0_tok_norm_b': _L0_tok_in['norm_b'], 'L0_attn_ln_gamma': _L0_attn_in['ln_gamma'], 'L0_attn_ln_beta': _L0_attn_in['ln_beta'], 'L0_attn_Win': _L0_attn_in['Win'], 'L0_attn_bin_': _L0_attn_in['bin_'], 'L0_attn_Wout': _L0_attn_in['Wout'], 'L0_attn_bout': _L0_attn_in['bout'], 'L0_attn_Lambda_re': _L0_attn_in['Lambda_re'], 'L0_attn_Lambda_im': _L0_attn_in['Lambda_im'], 'L0_attn_Bmat': _L0_attn_in['Bmat'], 'L0_attn_C_re': _L0_attn_in['C_re'], 'L0_attn_C_im': _L0_attn_in['C_im'], 'L0_attn_Dvec': _L0_attn_in['Dvec'], 'L0_ffn_W1': _L0_ffn_in['W1'], 'L0_ffn_b1': _L0_ffn_in['b1'], 'L0_ffn_W2': _L0_ffn_in['W2'], 'L0_ffn_b2': _L0_ffn_in['b2'], 'L0_ffn_Wg': _L0_ffn_in['Wg'], 'L0_ffn_bg': _L0_ffn_in['bg']}

def reference(x, L0_tok_conv_w, L0_tok_conv_b, L0_tok_cls_token, L0_tok_pos_embed, L0_tok_ln1_w, L0_tok_ln1_b, L0_tok_qkv_w, L0_tok_qkv_b, L0_tok_proj_w, L0_tok_proj_b, L0_tok_ln2_w, L0_tok_ln2_b, L0_tok_fc1_w, L0_tok_fc1_b, L0_tok_fc2_w, L0_tok_fc2_b, L0_tok_norm_w, L0_tok_norm_b, L0_attn_ln_gamma, L0_attn_ln_beta, L0_attn_Win, L0_attn_bin_, L0_attn_Wout, L0_attn_bout, L0_attn_Lambda_re, L0_attn_Lambda_im, L0_attn_Bmat, L0_attn_C_re, L0_attn_C_im, L0_attn_Dvec, L0_ffn_W1, L0_ffn_b1, L0_ffn_W2, L0_ffn_b2, L0_ffn_Wg, L0_ffn_bg):
    import jax
    import jax.numpy as jnp

    def _L0_tok_ref(x, conv_w, conv_b, cls_token, pos_embed, ln1_w, ln1_b, qkv_w, qkv_b, proj_w, proj_b, ln2_w, ln2_b, fc1_w, fc1_b, fc2_w, fc2_b, norm_w, norm_b):
        import jax, jax.numpy as jnp
        import numpy as np
        DEPTH = 4
        HEADS = 8
        DIM = 128
        HID = 256
        P = 16
        IMG = 224
        GRID = IMG // P
        NPATCH = GRID * GRID
        NTOK = NPATCH + 1
        BATCH = 64
        EPS = 1e-05

        def layernorm(x, w, b):
            mu = jnp.mean(x, axis=-1, keepdims=True)
            var = jnp.mean(jnp.square(x - mu), axis=-1, keepdims=True)
            return (x - mu) * jax.lax.rsqrt(var + EPS) * w + b
        B = x.shape[0]
        hd = DIM // HEADS
        scale = hd ** (-0.5)
        patches = x.reshape(B, 3, GRID, P, GRID, P)
        patches = patches.transpose(0, 2, 4, 1, 3, 5).reshape(B, NPATCH, 3 * P * P)
        tok = patches @ conv_w + conv_b
        cls = jnp.broadcast_to(cls_token, (B, 1, DIM))
        h = jnp.concatenate([cls, tok], axis=1) + pos_embed
        for i in range(DEPTH):
            y = layernorm(h, ln1_w[i], ln1_b[i])
            qkv = (y @ qkv_w[i] + qkv_b[i]).reshape(B, NTOK, 3, HEADS, hd)
            qkv = qkv.transpose(2, 0, 3, 1, 4)
            q, k, v = (qkv[0], qkv[1], qkv[2])
            attn = jax.nn.softmax(jnp.einsum('bhnd,bhmd->bhnm', q, k) * scale, axis=-1)
            o = jnp.einsum('bhnm,bhmd->bhnd', attn, v)
            o = o.transpose(0, 2, 1, 3).reshape(B, NTOK, DIM)
            h = h + (o @ proj_w[i] + proj_b[i])
            y = layernorm(h, ln2_w[i], ln2_b[i])
            y = jax.nn.gelu(y @ fc1_w[i] + fc1_b[i], approximate=False)
            h = h + (y @ fc2_w[i] + fc2_b[i])
        return layernorm(h, norm_w, norm_b)

    def _L0_attn_ref(x, ln_gamma, ln_beta, Win, bin_, Wout, bout, Lambda_re, Lambda_im, Bmat, C_re, C_im, Dvec):
        import jax, jax.numpy as jnp
        import numpy as np
        import math
        D_MODEL = 128
        D_STATE = 64
        CHUNK = 4
        NC = D_MODEL // CHUNK
        B_SZ, L_SEQ = (8, 1024)

        def _layernorm(x, g, b, eps=1e-05):
            mu = jnp.mean(x, axis=-1, keepdims=True)
            var = jnp.mean((x - mu) ** 2, axis=-1, keepdims=True)
            return (x - mu) * jax.lax.rsqrt(var + eps) * g + b
        Bsz, L, Dm = x.shape
        nc, n = Lambda_re.shape
        cs = Dm // nc
        z = _layernorm(x, ln_gamma, ln_beta)
        z = z @ Win + bin_
        omega = jnp.arange(L, dtype=jnp.float32)
        Lam = Lambda_re + 1j * Lambda_im
        expo = jnp.exp(Lam[:, :, None] * omega[None, None])
        CB = (C_re + 1j * C_im) * Bmat
        k = jnp.real(jnp.einsum('cn,cnl->cl', CB, expo))
        k2 = jnp.concatenate([k, k[:, ::-1]], axis=1)
        kf = jnp.fft.rfft(k2, n=2 * L, axis=1)
        u = z.reshape(Bsz, L, nc, cs)
        uf = jnp.fft.rfft(u, n=2 * L, axis=1)
        yf = uf * kf.T[None, :, :, None]
        y = jnp.fft.irfft(yf, n=2 * L, axis=1)[:, :L]
        y = y + u * Dvec[None, None, :, None]
        y = y.reshape(Bsz, L, Dm)
        y = y @ Wout + bout
        y = jax.nn.gelu(y, approximate=False)
        return x + y

    def _L0_ffn_ref(x, W1, b1, W2, b2, Wg, bg):
        import jax, jax.numpy as jnp
        import numpy as np
        B, N, D, E = (8, 2048, 128, 8)
        H = 2 * D
        Bs, Ns, Ds = x.shape
        xf = x.reshape(Bs * Ns, Ds)
        logits = xf @ Wg + bg
        idx = jnp.argmax(logits, axis=-1)
        out = jnp.zeros_like(xf)
        num_experts = W1.shape[0]
        for e in range(num_experts):
            h = jax.nn.relu(xf @ W1[e] + b1[e])
            y = h @ W2[e] + b2[e]
            out = jnp.where((idx == e)[:, None], y, out)
        return out.reshape(Bs, Ns, Ds)
    h = _L0_tok_ref(x, L0_tok_conv_w, L0_tok_conv_b, L0_tok_cls_token, L0_tok_pos_embed, L0_tok_ln1_w, L0_tok_ln1_b, L0_tok_qkv_w, L0_tok_qkv_b, L0_tok_proj_w, L0_tok_proj_b, L0_tok_ln2_w, L0_tok_ln2_b, L0_tok_fc1_w, L0_tok_fc1_b, L0_tok_fc2_w, L0_tok_fc2_b, L0_tok_norm_w, L0_tok_norm_b)
    h = _layernorm(h + _L0_attn_ref(h, L0_attn_ln_gamma, L0_attn_ln_beta, L0_attn_Win, L0_attn_bin_, L0_attn_Wout, L0_attn_bout, L0_attn_Lambda_re, L0_attn_Lambda_im, L0_attn_Bmat, L0_attn_C_re, L0_attn_C_im, L0_attn_Dvec), axis=-1)
    h = _layernorm(h + _L0_ffn_ref(h, L0_ffn_W1, L0_ffn_b1, L0_ffn_W2, L0_ffn_b2, L0_ffn_Wg, L0_ffn_bg), axis=-1)
    return h

_drawn_inputs = setup_inputs


def setup_inputs(seed=0):
    import zlib

    import numpy as np

    out = dict(_drawn_inputs(seed))
    spreads = {'L0_tok_conv_b': (0.0, 0.1),
     'L0_tok_ln1_w': (1.0, 0.6),
     'L0_tok_ln1_b': (0.0, 0.31),
     'L0_tok_qkv_b': (0.0, 0.1),
     'L0_tok_proj_b': (0.0, 0.1),
     'L0_tok_ln2_w': (1.0, 0.2),
     'L0_tok_ln2_b': (0.0, 0.336),
     'L0_tok_fc1_b': (0.0, 0.1),
     'L0_tok_fc2_b': (0.0, 0.1),
     'L0_tok_norm_w': (1.0, 0.2),
     'L0_tok_norm_b': (0.0, 0.1),
     'L0_attn_ln_gamma': (1.0, 0.2),
     'L0_attn_ln_beta': (0.0, 0.1),
     'L0_attn_bin_': (0.0, 0.1),
     'L0_attn_bout': (0.0, 0.541),
     'L0_attn_Lambda_re': (-0.5, 0.2),
     'L0_ffn_b1': (0.0, 0.349),
     'L0_ffn_b2': (0.0, 0.1),
     'L0_ffn_bg': (0.0, 0.1)}
    factors = {'L0_tok_cls_token': 8.0}
    for name, (base, spread) in spreads.items():
        noise = np.random.default_rng([zlib.crc32(name.encode()), seed]).standard_normal(out[name].shape)
        drawn = base * np.exp(spread * noise) if base else spread * noise
        out[name] = jnp.asarray(drawn.astype(out[name].dtype))
    for name, factor in factors.items():
        out[name] = (out[name] * factor).astype(out[name].dtype)
    return out
```

```python
from contextlib import ExitStack

import concourse.bass as bass
from concourse import mybir

F32 = mybir.dt.float32
F16 = mybir.dt.float16
BF16 = mybir.dt.bfloat16
ALU = mybir.AluOpType
ACT = mybir.ActivationFunctionType
AX_X = mybir.AxisListType.X

P = 128
TOK = 197
PATCH = TOK - 1
IMG = 2
N = IMG * TOK
DEPTH = 4
HEADS = 8
HD = P // HEADS
KCH = 6
EXPERTS = 8
TILES = ((0, 128), (128, TOK - 128))
LAST0 = TOK - 128
EPS = 1e-5
CHUNKS = 32
CW = P // CHUNKS
GEN = 2 * TOK - 1
STATE = 64
CG = CHUNKS // 2
NEG = -1e30
ONE_ROW = 96


def shift(it, per, k):
    return it * per + k


class Banks:

    def __init__(self, steps):
        self.use, count = {}, [0, 0]
        for n, step in enumerate(steps):
            b = n % 2
            self.use[step] = (b, count[b])
            count[b] += 1
        self.per = count


LAYER_STEPS = ("xc1", "var1", "q", "k", "v", "neg", "den0", "den1", "proj", "xc2", "var2", "fc1a", "fc1b", "fc2")
VIT_STEPS = ([("emb",)] + [(l, s) for l in range(DEPTH) for s in LAYER_STEPS]
             + [("end", s) for s in ("xcn", "varn", "xcz", "varz", "u")])
TAIL_STEPS = ([("yT",), ("out",), ("xc",), ("var",), ("logit",), ("hotT",)]
              + [("exp", e, j) for e in range(EXPERTS) for j in range(2)]
              + [("xcf",), ("varf",), ("back",)])


def build(nc, x, conv, convb, clsc, posT, qkv, qkvb, projp, projn, projb, ln1, fc1, fc1b, fc2, fc2b, ln2,
          normwb, attg, win, binb, wout, boutc, lre, lim, bm, cre, cim, dvec, w1, b1c, w2, b2, wg, bgb,
          om, ident, cen, mean, dsel, esel, rank, anti, out):
    B = out.shape[0]
    PAIRS = B // IMG
    GRP = B // 4 if B >= 8 else B
    GROUPS = B // GRP

    with ExitStack() as ctx:
        def sb(name, shape, dt=F32):
            return ctx.enter_context(nc.sbuf_tensor(name, shape, dt))

        def sem(name):
            return ctx.enter_context(nc.semaphore(name))

        split_dram = nc.dram_tensor("split_dram", (2, 2, HEADS, HD, N), F16).ap()
        gen_dram = nc.dram_tensor("gen_dram", (CHUNKS, GEN), F32).ap()
        u_dram = nc.dram_tensor("u_dram", (TOK, B, P), F32).ap()
        y_dram = nc.dram_tensor("y_dram", (TOK, B, P), F32).ap()
        ho_dram = nc.dram_tensor("ho_dram", (PAIRS, P, N), F32).ap()

        psA = ctx.enter_context(nc.psum_tensor("psA", [P, 2, 2, 512], F32))
        psD = ctx.enter_context(nc.psum_tensor("psD", [P, 2, 512], F32))
        psO = ctx.enter_context(nc.psum_tensor("psO", [P, 2, 512], F32))

        const_in = sem("const_in")

        conv_s = sb("conv_s", [P, KCH, P])
        qkv_s = sb("qkv_s", [P, DEPTH, 3 * P])
        projp_s = sb("projp_s", [P, DEPTH, 2, P])
        fc1_s = sb("fc1_s", [P, DEPTH, 2 * P])
        fc2_s = sb("fc2_s", [P, DEPTH, 2, P])
        win_s = sb("win_s", [P, P])
        wout_s = sb("wout_s", [P, P])
        cen_s = sb("cen_s", [P, P])
        mean_s = sb("mean_s", [P, P])
        dsel_s = sb("dsel_s", [P, P])
        id_s = sb("id_s", [P, P])
        pos_s = sb("pos_s", [P, TOK])
        binb_s = sb("binb_s", [P, P])
        vecs = {}
        for nm_, src in (("convb", convb), ("clsc", clsc), ("qkvb", qkvb), ("projb", projb), ("ln1", ln1),
                         ("fc1b", fc1b), ("fc2b", fc2b), ("ln2", ln2), ("normwb", normwb), ("attg", attg),
                         ("boutc", boutc), ("lre", lre), ("lim", lim), ("bm", bm), ("cre", cre), ("cim", cim),
                         ("b1c", b1c)):
            vecs[nm_] = (sb(nm_ + "_s", [P, src.shape[1]]), src)
        convb_s, clsc_s, qkvb_s, projb_s, ln1_s, fc1b_s, fc2b_s, ln2_s, normwb_s, attg_s, boutc_s, lre_s, lim_s, \
            bm_s, cre_s, cim_s, b1c_s = [vecs[k][0] for k in vecs]
        loads = [(conv_s, conv), (qkv_s, qkv), (projp_s, projp), (fc1_s, fc1), (fc2_s, fc2), (win_s, win),
                 (wout_s, wout), (cen_s, cen), (mean_s, mean), (dsel_s, dsel), (id_s, ident), (pos_s, posT),
                 (binb_s, binb)] + list(vecs.values())
        bias_s = sb("bias_s", [P, DEPTH, 6])
        eps_s = sb("eps_s", [P, 1])

        with ExitStack() as pre:
            def psb(name, shape, dt=F32):
                return pre.enter_context(nc.sbuf_tensor(name, shape, dt))
            projn_s = psb("projn_s", [P, DEPTH, P])
            om_s = psb("om_s", [P, GEN])
            dvec_s = psb("dvec_s", [CHUNKS, 1])
            cb = psb("cb", [P, 2, CG])
            lw = psb("lw", [P, 2, CG * CHUNKS])
            ang = psb("ang", [P, GEN])
            turn = psb("turn", [P, GEN])
            red = psb("red", [P, GEN])
            red2 = psb("red2", [P, GEN])
            dec = psb("dec", [P, GEN])
            sn = psb("sn", [P, GEN])
            hs = psb("hs", [P, GEN])
            cs = psb("cs", [P, GEN])
            ec = psb("ec", [P, 2, GEN])
            es = psb("es", [P, 2, GEN])
            gen = psb("gen", [CHUNKS, GEN])
            pre_loads = [(projn_s, projn), (om_s, om), (dvec_s, dvec)]

            fold = pre.enter_context(nc.semaphore("fold"))
            shifts_full = pre.enter_context(nc.semaphore("shifts_full"))
            vshift = pre.enter_context(nc.semaphore("vshift"))
            proj_full = pre.enter_context(nc.semaphore("proj_full"))
            winfull = pre.enter_context(nc.semaphore("winfull"))
            chain = pre.enter_context(nc.semaphore("chain"))
            reduced = pre.enter_context(nc.semaphore("reduced"))
            waves = pre.enter_context(nc.semaphore("waves"))
            damped = pre.enter_context(nc.semaphore("damped"))
            summed = pre.enter_context(nc.semaphore("summed"))
            gen_out = pre.enter_context(nc.semaphore("gen_out"))
            gen_done = pre.enter_context(nc.semaphore("gen_done"))
            n_const = 16 * (len(loads) + len(pre_loads))
            blk = pre.enter_context(nc.Block())

            @blk.sync
            def _(sp):
                for t, src in loads + pre_loads:
                    sp.dma_start(t[:], src).then_inc(const_in, 16)
                sp.wait_ge(gen_done, 1)
                sp.dma_start(gen_dram, gen[:, :]).then_inc(gen_out, 16)
                sp.wait_ge(gen_out, 16)

            @blk.tensor
            def _(pe):
                pe.wait_ge(const_in, n_const)
                for l in range(DEPTH):
                    for j in range(3):
                        pe.matmul(psD[:, 0, 8 * l + j:8 * l + j + 1], qkv_s[:, l, j * P:(j + 1) * P],
                                  ln1_s[:, DEPTH + l:DEPTH + l + 1], start=True, stop=True)
                    for j in range(2):
                        last = pe.matmul(psD[:, 0, 8 * l + 3 + j:8 * l + 4 + j], fc1_s[:, l, j * P:(j + 1) * P],
                                         ln2_s[:, DEPTH + l:DEPTH + l + 1], start=True, stop=True)
                last = pe.matmul(psD[:, 0, 128:256], attg_s[:, 1:2].to_broadcast([P, P]), win_s[:, :],
                                 start=True, stop=True)
                last.then_inc(shifts_full, 1)
                pe.wait_ge(vshift, 1)
                for l in range(DEPTH):
                    last = pe.matmul(psD[:, 1, l:l + 1], projn_s[:, l, :], bias_s[:, l, 2:3], start=True, stop=True)
                last.then_inc(proj_full, 1)
                for g in range(CG):
                    pe.wait_ge(damped, 2 * (g + 1))
                    pe.matmul(psA[0:CHUNKS, 0, 0, 0:GEN], lw[:, 0, g * CHUNKS:(g + 1) * CHUNKS], ec[:, g % 2, :],
                              start=(g == 0), stop=False)
                    pe.matmul(psA[0:CHUNKS, 0, 0, 0:GEN], lw[:, 1, g * CHUNKS:(g + 1) * CHUNKS], es[:, g % 2, :],
                              start=False, stop=(g == CG - 1)).then_inc(summed, 1)

            @blk.scalar
            def _(act):
                act.wait_ge(const_in, n_const)
                for g in range(CG):
                    if g >= 1:
                        act.wait_ge(damped, 2 * g)
                    act.activation(dec[:, :], om_s[:, :], ACT.Exp, scale=lre_s[:, g:g + 1]).then_inc(waves, 1)
                    act.wait_ge(reduced, g + 1)
                    act.activation(sn[:, :], red2[:, :], ACT.Sin).then_inc(waves, 1)
                    act.activation(hs[:, :], red2[:, :], ACT.Sin, scale=0.5).then_inc(waves, 1)

            @blk.vector
            def _(dve):
                steps = [0]

                def then(ins):
                    steps[0] += 1
                    ins.then_inc(chain, 1)
                    dve.wait_ge(chain, steps[0])

                dve.memset(eps_s[:, :], EPS)
                then(dve.memset(lw[:, :, :], 0.0))
                dve.wait_ge(const_in, n_const)
                dve.tensor_scalar(pos_s[:, 1:TOK], pos_s[:, 1:TOK], convb_s[:, 0:1], None, ALU.add)
                dve.tensor_tensor(pos_s[:, 0:1], pos_s[:, 0:1], clsc_s[:, 0:1], ALU.add)
                dve.wait_ge(shifts_full, 1)
                sv = psD[:, 0, 0:8 * DEPTH].rearrange("p (l k) -> p l k", k=8)
                dve.tensor_tensor(bias_s[:, :, 0:3], sv[:, :, 0:3],
                                  qkvb_s[:, :].rearrange("p (l k) -> p l k", k=3), ALU.add)
                dve.tensor_tensor(bias_s[:, :, 3:5], sv[:, :, 3:5],
                                  fc1b_s[:, :].rearrange("p (l k) -> p l k", k=2), ALU.add)
                then(dve.tensor_tensor(binb_s[:, :], psD[:, 0, 128:256], binb_s[:, :], ALU.add))
                dve.tensor_scalar(bias_s[:, :, 0:1], bias_s[:, :, 0:1], float(HD) ** -0.5, None,
                                  ALU.mult).then_inc(vshift, 1)
                for l in range(DEPTH):
                    dve.tensor_scalar(qkv_s[:, l, P:], qkv_s[:, l, P:], ln1_s[:, l:l + 1], None, ALU.mult)
                    dve.tensor_scalar(qkv_s[:, l, 0:P], qkv_s[:, l, 0:P], ln1_s[:, l:l + 1], float(HD) ** -0.5,
                                      ALU.mult, ALU.mult)
                    dve.tensor_scalar(fc1_s[:, l, :], fc1_s[:, l, :], ln2_s[:, l:l + 1], None, ALU.mult)
                dve.tensor_scalar(win_s[:, :], win_s[:, :], attg_s[:, 0:1], None, ALU.mult)
                dve.wait_ge(proj_full, 1)
                dve.tensor_tensor(bias_s[:, :, 5], psD[:, 1, 0:DEPTH], projb_s[:, :], ALU.add)
                dve.tensor_tensor(cb[:, 0, :], cre_s[:, :], bm_s[:, :], ALU.mult)
                then(dve.tensor_tensor(cb[:, 1, :], cim_s[:, :], bm_s[:, :], ALU.mult))
                for i in range(2):
                    r = slice(STATE * i, STATE * (i + 1))
                    dve.tensor_scalar(lw[r, 0, i::CHUNKS + 2], cb[r, 0, :], 1.0, None, ALU.mult)
                    then(dve.tensor_scalar(lw[r, 1, i::CHUNKS + 2], cb[r, 1, :], -1.0, None, ALU.mult))
                for g in range(CG):
                    then(dve.tensor_scalar(ang[:, :], om_s[:, :], lim_s[:, g:g + 1], None, ALU.mult))
                    then(dve.tensor_scalar(turn[:, :], ang[:, :], TURNS, MAGIC, ALU.mult, ALU.add))
                    then(dve.tensor_scalar(turn[:, :], turn[:, :], MAGIC, None, ALU.subtract))
                    then(dve.scalar_tensor_tensor(out=red[:, :], in0=turn[:, :], scalar=-PI2[0], in1=ang[:, :],
                                                  op0=ALU.mult, op1=ALU.add))
                    then(dve.scalar_tensor_tensor(out=red[:, :], in0=turn[:, :], scalar=-PI2[1], in1=red[:, :],
                                                  op0=ALU.mult, op1=ALU.add))
                    then(dve.scalar_tensor_tensor(out=red[:, :], in0=turn[:, :], scalar=-PI2[2], in1=red[:, :],
                                                  op0=ALU.mult, op1=ALU.add))
                    dve.tensor_scalar(red2[:, :], red[:, :], PI_BELOW, -PI_BELOW, ALU.min,
                                      ALU.max).then_inc(reduced, 1)
                    dve.wait_ge(waves, 3 * (g + 1))
                    then(dve.scalar_tensor_tensor(out=cs[:, :], in0=hs[:, :], scalar=-2.0, in1=hs[:, :],
                                                  op0=ALU.mult, op1=ALU.mult))
                    if g >= 2:
                        dve.wait_ge(summed, g - 1)
                    dve.scalar_tensor_tensor(out=ec[:, g % 2, :], in0=cs[:, :], scalar=1.0, in1=dec[:, :],
                                             op0=ALU.add, op1=ALU.mult).then_inc(damped, 1)
                    dve.tensor_tensor(es[:, g % 2, :], sn[:, :], dec[:, :], ALU.mult).then_inc(damped, 1)
                dve.wait_ge(summed, CG)
                then(dve.tensor_copy(gen[:, :], psA[0:CHUNKS, 0, 0, 0:GEN]))
                dve.tensor_tensor(gen[:, TOK - 1:TOK], gen[:, TOK - 1:TOK], dvec_s[:, :],
                                  ALU.add).then_inc(gen_done, 1)

        with ExitStack() as st:
            def ssb(name, shape, dt=F32):
                return st.enter_context(nc.sbuf_tensor(name, shape, dt))

            def ssem(name):
                return st.enter_context(nc.semaphore(name))

            patches = ssb("patches", [P, KCH, IMG * PATCH])
            h = ssb("h", [P, N])
            sq = ssb("sq", [P, N])
            lnv = ssb("lnv", [P, N])
            rstd = ssb("rstd", [P, N])
            y = ssb("y", [P, N])
            qsp = ssb("qsp", [P, 2, N], F16)
            ksp = ssb("ksp", [P, 2, N], F16)
            qst = ssb("qst", [P, HEADS, N], F16)
            kst = ssb("kst", [P, HEADS, N], F16)
            vals = ssb("vals", [P, IMG, 2, HEADS, 2 * HD])
            nmax = ssb("nmax", [P, IMG, 2, HEADS])
            nmT = ssb("nmT", [HEADS, N], F16)
            prob = ssb("prob", [P, 4, 4, TOK])
            osb = ssb("osb", [P, 2, N])
            rden = ssb("rden", [P, 2, N])
            on = ssb("on", [P, 2, N])
            gl = ssb("gl", [P, 2, N])
            ho = ssb("ho", [P, N])
            usb = ssb("usb", [P, IMG, 2, P])

            patches_in = ssem("patches_in")
            full = [ssem(f"dense_full{b}") for b in range(2)]
            evac = [ssem(f"dense_evac{b}") for b in range(2)]
            set_up = ssem("set_up")
            cls_done = ssem("cls_done")
            sq_done = ssem("sq_done")
            rstd_done = ssem("rstd_done")
            hi_done = ssem("hi_done")
            v_half = ssem("v_half")
            split_out = ssem("split_out")
            stacks_in = ssem("stacks_in")
            scores_full = ssem("scores_full")
            max_done = ssem("max_done")
            neg_in = ssem("neg_in")
            exp_done = ssem("exp_done")
            pv_done = ssem("pv_done")
            o_copied = ssem("o_copied")
            rden_done = ssem("rden_done")
            gelu_done = ssem("gelu_done")
            ho_done = ssem("ho_done")
            ho_out = ssem("ho_out")
            u_half = ssem("u_half")
            u_out = ssem("u_out")
            banks = Banks(VIT_STEPS)

            def ready(eng, it, step):
                b, k = banks.use[step]
                eng.wait_ge(full[b], shift(it, banks.per[b], k + 1))
                return psD[:, b, :]

            def result(eng, it, step):
                b, k = banks.use[step]
                eng.wait_ge(evac[b], shift(it, banks.per[b], k + 1))

            def free(pe, it, step):
                b, k = banks.use[step]
                pe.wait_ge(evac[b], shift(it, banks.per[b], k))
                return psD[:, b, :]

            def fulls(ins, step):
                ins.then_inc(full[banks.use[step][0]], 1)

            def evacs(ins, step):
                ins.then_inc(evac[banks.use[step][0]], 1)

            LNS = 2 * DEPTH + 2
            blk = st.enter_context(nc.Block())

            @blk.sync
            def _(sp):
                sp.dma_start(patches[:, :, :], x[0]).then_inc(patches_in, 16)
                with sp.Fori(0, PAIRS) as it:
                    for l in range(DEPTH):
                        if l == 1:
                            ready(sp, it, ("emb",))
                            sp.dma_start(patches[:, :, :], x[bass.ds(it + 1, 1)].rearrange("a p k n -> (a p) k n")).then_inc(patches_in, 16)
                        result(sp, it, (l, "q"))
                        sp.dma_start(split_dram[0].rearrange("s h d n -> (h d) s n"), qsp[:, :, :]).then_inc(split_out, 16)
                        result(sp, it, (l, "k"))
                        sp.dma_start(split_dram[1].rearrange("s h d n -> (h d) s n"), ksp[:, :, :]).then_inc(split_out, 16)
                        sp.wait_ge(split_out, shift(it, 32 * DEPTH, 32 * (l + 1)))
                        for r, s in enumerate((0, 0, 1, 1)):
                            sp.dma_start(qst[HD * r:HD * (r + 1), :, :],
                                         split_dram[0, s].rearrange("h d n -> d h n")).then_inc(stacks_in, 16)
                        for r, s in enumerate((0, 1, 0, 1)):
                            sp.dma_start(kst[HD * r:HD * (r + 1), :, :],
                                         split_dram[1, s].rearrange("h d n -> d h n")).then_inc(stacks_in, 16)
                        result(sp, it, (l, "neg"))
                        sp.dma_start(qst[ONE_ROW:ONE_ROW + 1, :, :], nmT[:, :]).then_inc(neg_in, 16)
                    sp.wait_ge(ho_done, it + 1)
                    sp.dma_start(ho_dram[bass.ds(it, 1)].rearrange("a p n -> (a p) n"), ho[:, :]).then_inc(ho_out, 16)
                    result(sp, it, ("end", "u"))
                    sp.wait_ge(u_half, it + 1)
                    for t, (t0, tn) in enumerate(TILES):
                        sp.dma_start(u_dram[t0:t0 + tn, bass.ds(IMG * it, IMG), :], usb[0:tn, :, t, :]).then_inc(u_out, 16)
                sp.wait_ge(ho_out, 16 * PAIRS)
                sp.wait_ge(u_out, 32 * PAIRS)
                sp.wait_ge(patches_in, 16 * (PAIRS + 1))

            def norm_pe(pe, it, xc, var, n, moving):
                fulls(pe.matmul(free(pe, it, xc)[:, 0:N], cen_s[:, :], moving, start=True, stop=True), xc)
                pe.wait_ge(sq_done, shift(it, LNS, n + 1))
                fulls(pe.matmul(free(pe, it, var)[:, 0:N], mean_s[:, :], sq[:, :], start=True, stop=True), var)

            @blk.tensor
            def _(pe):
                pe.wait_ge(set_up, 4)

                def scores(it, l, n):
                    slot = n % 2
                    if n < 8:
                        if n >= 2:
                            pe.wait_ge(max_done, shift(it, 8 * DEPTH, 8 * l + n - 1))
                        else:
                            pe.wait_ge(exp_done, shift(it, 8 * DEPTH, 8 * l))
                        b, t, g = n // 4, n // 2 % 2, n % 2
                        out_st, mov, rows = qst, kst, ONE_ROW
                    else:
                        if n >= 10:
                            pe.wait_ge(exp_done, shift(it, 8 * DEPTH, 8 * l + n - 9))
                        b, g, t = (n - 8) // 4, (n - 8) // 2 % 2, n % 2
                        out_st, mov, rows = kst, qst, ONE_ROW + 1
                    t0, tn = TILES[t]
                    for j in range(4):
                        last = pe.matmul(psA[0:tn, slot, j // 2, (j % 2) * TOK:(j % 2 + 1) * TOK],
                                         out_st[0:rows, 4 * g + j, b * TOK + t0:b * TOK + t0 + tn],
                                         mov[0:rows, 4 * g + j, b * TOK:(b + 1) * TOK], start=True, stop=True)
                    last.then_inc(scores_full, 1)

                def weighted(it, l, p):
                    b, g = p // 2, p % 2
                    pe.wait_ge(exp_done, shift(it, 8 * DEPTH, 8 * l + 2 * p + 2))
                    for t, (t0, tn) in enumerate(TILES):
                        for j in range(4):
                            last = pe.matmul(psO[32 * j:32 * j + 32, g, b * TOK:(b + 1) * TOK],
                                             vals[0:tn, b, t, 4 * g + j, :], prob[0:tn, (2 * p + t) % 4, j, :],
                                             start=(t == 0), stop=(t == 1))
                    last.then_inc(pv_done, 1)

                with pe.Fori(0, PAIRS) as it:
                    pe.wait_ge(patches_in, shift(it, 16, 16))
                    ps = free(pe, it, ("emb",))
                    for k in range(KCH):
                        last = pe.matmul(ps[:, 0:IMG * PATCH], conv_s[:, k, :], patches[:, k, :],
                                         start=(k == 0), stop=(k == KCH - 1))
                    fulls(last, ("emb",))
                    pe.wait_ge(cls_done, it + 1)
                    for l in range(DEPTH):
                        result(pe, it, ("emb",) if l == 0 else (l - 1, "fc2"))
                        norm_pe(pe, it, (l, "xc1"), (l, "var1"), 2 * l, h[:, :])
                        result(pe, it, (l, "xc1"))
                        for j, s in enumerate("qk"):
                            fulls(pe.matmul(free(pe, it, (l, s))[:, 0:N], qkv_s[:, l, j * P:(j + 1) * P], y[:, :],
                                            start=True, stop=True), (l, s))
                        ps = free(pe, it, (l, "v"))
                        for b in range(IMG):
                            for t, (t0, tn) in enumerate(TILES):
                                last = pe.matmul(ps[0:tn, (2 * b + t) * P:(2 * b + t + 1) * P],
                                                 y[:, b * TOK + t0:b * TOK + t0 + tn], qkv_s[:, l, 2 * P:],
                                                 start=True, stop=True)
                        fulls(last, (l, "v"))
                        pe.wait_ge(stacks_in, shift(it, 128 * DEPTH, 128 * (l + 1)))
                        for n in range(8):
                            scores(it, l, n)
                        pe.wait_ge(max_done, shift(it, 8 * DEPTH, 8 * (l + 1)))
                        ps = free(pe, it, (l, "neg"))
                        for b in range(IMG):
                            for t, (t0, tn) in enumerate(TILES):
                                c0 = b * TOK + t0
                                last = pe.matmul(ps[0:HEADS, c0:c0 + tn], nmax[0:tn, b, t, :], id_s[0:tn, 0:tn],
                                                 start=True, stop=True)
                        fulls(last, (l, "neg"))
                        pe.wait_ge(neg_in, shift(it, 16 * DEPTH, 16 * (l + 1)))
                        result(pe, it, (l, "v"))
                        pe.wait_ge(v_half, shift(it, DEPTH, l + 1))
                        pe.wait_ge(o_copied, shift(it, 2 * DEPTH, 2 * l))
                        for p in range(4):
                            scores(it, l, 8 + 2 * p)
                            scores(it, l, 9 + 2 * p)
                            if p:
                                weighted(it, l, p - 1)
                        weighted(it, l, 3)
                        for g in range(2):
                            s = (l, f"den{g}")
                            pe.wait_ge(o_copied, shift(it, 2 * DEPTH, 2 * l + g + 1))
                            fulls(pe.matmul(free(pe, it, s)[:, 0:N], dsel_s[:, :], osb[:, g, :],
                                            start=True, stop=True), s)
                        ps = free(pe, it, (l, "proj"))
                        for g in range(2):
                            result(pe, it, (l, f"den{g}"))
                            last = pe.matmul(ps[:, 0:N], projp_s[:, l, g, :], on[:, g, :], start=(g == 0), stop=(g == 1))
                        fulls(last, (l, "proj"))
                        result(pe, it, (l, "proj"))
                        norm_pe(pe, it, (l, "xc2"), (l, "var2"), 2 * l + 1, h[:, :])
                        result(pe, it, (l, "xc2"))
                        for j, s in enumerate(("fc1a", "fc1b")):
                            fulls(pe.matmul(free(pe, it, (l, s))[:, 0:N], fc1_s[:, l, j * P:(j + 1) * P], y[:, :],
                                            start=True, stop=True), (l, s))
                        ps = free(pe, it, (l, "fc2"))
                        for j, s in enumerate(("fc1a", "fc1b")):
                            result(pe, it, (l, s))
                            last = pe.matmul(ps[:, 0:N], fc2_s[:, l, j, :], gl[:, j, :], start=(j == 0), stop=(j == 1))
                        fulls(last, (l, "fc2"))
                    result(pe, it, (DEPTH - 1, "fc2"))
                    norm_pe(pe, it, ("end", "xcn"), ("end", "varn"), 2 * DEPTH, h[:, :])
                    pe.wait_ge(ho_done, it + 1)
                    norm_pe(pe, it, ("end", "xcz"), ("end", "varz"), 2 * DEPTH + 1, ho[:, :])
                    result(pe, it, ("end", "xcz"))
                    ps = free(pe, it, ("end", "u"))
                    for b in range(IMG):
                        for t, (t0, tn) in enumerate(TILES):
                            last = pe.matmul(ps[0:tn, (2 * b + t) * P:(2 * b + t + 1) * P],
                                             y[:, b * TOK + t0:b * TOK + t0 + tn], win_s[:, :], start=True, stop=True)
                    fulls(last, ("end", "u"))

            @blk.scalar
            def _(act):
                act.wait_ge(set_up, 4)

                def norm(it, xc, var, n):
                    act.activation(sq[:, :], ready(act, it, xc)[:, 0:N], ACT.Square).then_inc(sq_done, 1)
                    evacs(act.activation(lnv[:, :], ready(act, it, var)[:, 0:N], ACT.Ln, bias=eps_s[:, 0:1]), var)
                    result(act, it, var)
                    act.activation(rstd[:, :], lnv[:, :], ACT.Exp, scale=-0.5).then_inc(rstd_done, 1)

                with act.Fori(0, PAIRS) as it:
                    for l in range(DEPTH):
                        norm(it, (l, "xc1"), (l, "var1"), 2 * l)
                        for j, (s, t) in enumerate((("q", qsp), ("k", ksp))):
                            ps = ready(act, it, (l, s))
                            if l:
                                act.wait_ge(split_out, shift(it, 32 * DEPTH, 32 * l))
                            act.activation(t[:, 0, :], ps[:, 0:N], ACT.Identity,
                                           bias=bias_s[:, l, j:j + 1]).then_inc(hi_done, 1)
                        for n in range(8):
                            g, t = n // 2 % 2, n % 2
                            tn = TILES[t][1]
                            act.wait_ge(scores_full, shift(it, 16 * DEPTH, 16 * l + 8 + n + 1))
                            if n >= 4:
                                act.wait_ge(pv_done, shift(it, 4 * DEPTH, 4 * l + n // 2 - 1))
                            act.activation(prob[0:tn, n % 4, :, :].rearrange("p (a c) n -> p a c n", c=2),
                                           psA[0:tn, n % 2, :, 0:2 * TOK].rearrange("p a (c n) -> p a c n", c=2),
                                           ACT.Exp).then_inc(exp_done, 1)
                        norm(it, (l, "xc2"), (l, "var2"), 2 * l + 1)
                        for j, s in enumerate(("fc1a", "fc1b")):
                            evacs(act.activation(gl[:, j, :], ready(act, it, (l, s))[:, 0:N], ACT.Gelu,
                                                 bias=bias_s[:, l, 3 + j:4 + j]), (l, s))
                    norm(it, ("end", "xcn"), ("end", "varn"), 2 * DEPTH)
                    norm(it, ("end", "xcz"), ("end", "varz"), 2 * DEPTH + 1)

            @blk.vector
            def _(dve):
                dve.memset(qst[:, :, :], 0.0).then_inc(set_up, 1)
                dve.memset(kst[:, :, :], 0.0).then_inc(set_up, 1)
                dve.wait_ge(set_up, 2)
                dve.memset(kst[ONE_ROW:ONE_ROW + 1, :, :], 1.0).then_inc(set_up, 1)
                dve.memset(vals[:, :, :, :, :], 1.0).then_inc(set_up, 1)
                dve.wait_ge(set_up, 4)

                def norm(it, xc, n):
                    ps = ready(dve, it, xc)
                    dve.wait_ge(rstd_done, shift(it, LNS, n + 1))
                    evacs(dve.tensor_tensor(y[:, :], ps[:, 0:N], rstd[:, :], ALU.mult), xc)

                with dve.Fori(0, PAIRS) as it:
                    ps = ready(dve, it, ("emb",))
                    hv = h[:, :].rearrange("p (b t) -> p b t", b=IMG)
                    for b in range(IMG):
                        last = dve.tensor_copy(hv[:, b, 0:1], pos_s[:, 0:1])
                    last.then_inc(cls_done, 1)
                    for b in range(IMG):
                        last = dve.tensor_tensor(hv[:, b, 1:TOK], ps[:, b * PATCH:(b + 1) * PATCH], pos_s[:, 1:TOK], ALU.add)
                    evacs(last, ("emb",))
                    for l in range(DEPTH):
                        norm(it, (l, "xc1"), 2 * l)
                        for j, (s, t) in enumerate((("q", qsp), ("k", ksp))):
                            ps = ready(dve, it, (l, s))
                            dve.wait_ge(hi_done, shift(it, 2 * DEPTH, 2 * l + j + 1))
                            evacs(dve.scalar_tensor_tensor(out=t[:, 1, :], in0=ps[:, 0:N], scalar=bias_s[:, l, j:j + 1],
                                                           in1=t[:, 0, :], op0=ALU.add, op1=ALU.subtract), (l, s))
                        ps = ready(dve, it, (l, "v"))
                        for t, (t0, tn) in enumerate(TILES):
                            pv = ps.rearrange("p (b t h d) -> p b t h d", b=IMG, t=2, h=HEADS)
                            for b in range(IMG):
                                last = dve.tensor_copy(vals[0:tn, b, t, :, 0:HD], pv[0:tn, b, t, :, :])
                            if t == 0:
                                last.then_inc(v_half, 1)
                        evacs(last, (l, "v"))
                        for n in range(8):
                            b, t, g = n // 4, n // 2 % 2, n % 2
                            tn = TILES[t][1]
                            dve.wait_ge(scores_full, shift(it, 16 * DEPTH, 16 * l + n + 1))
                            dve.tensor_reduce(nmax[0:tn, b, t, 4 * g:4 * g + 4].rearrange("p (a c) -> p a c", c=2),
                                              psA[0:tn, n % 2, :, 0:2 * TOK].rearrange("p a (c n) -> p a c n", c=2),
                                              AX_X, ALU.max, negate=True).then_inc(max_done, 1)
                        evacs(dve.tensor_copy(nmT[:, :], ready(dve, it, (l, "neg"))[0:HEADS, 0:N]), (l, "neg"))
                        for g in range(2):
                            dve.wait_ge(pv_done, shift(it, 4 * DEPTH, 4 * l + g + 3))
                            dve.tensor_copy(osb[:, g, :], psO[:, g, 0:N]).then_inc(o_copied, 1)
                        for g in range(2):
                            s = (l, f"den{g}")
                            dve.reciprocal(rden[:, g, :], ready(dve, it, s)[:, 0:N]).then_inc(rden_done, 1)
                            dve.wait_ge(rden_done, shift(it, 2 * DEPTH, 2 * l + g + 1))
                            evacs(dve.tensor_tensor(on[:, g, :], osb[:, g, :], rden[:, g, :], ALU.mult), s)
                        evacs(dve.scalar_tensor_tensor(out=h[:, :], in0=ready(dve, it, (l, "proj"))[:, 0:N],
                                                       scalar=bias_s[:, l, 5:6], in1=h[:, :], op0=ALU.add,
                                                       op1=ALU.add), (l, "proj"))
                        norm(it, (l, "xc2"), 2 * l + 1)
                        evacs(dve.scalar_tensor_tensor(out=h[:, :], in0=ready(dve, it, (l, "fc2"))[:, 0:N],
                                                       scalar=fc2b_s[:, l:l + 1], in1=h[:, :], op0=ALU.add,
                                                       op1=ALU.add), (l, "fc2"))
                    norm(it, ("end", "xcn"), 2 * DEPTH)
                    result(dve, it, ("end", "xcn"))
                    dve.wait_ge(ho_out, shift(it, 16, 0))
                    dve.tensor_scalar(ho[:, :], y[:, :], normwb_s[:, 0:1], normwb_s[:, 1:2], ALU.mult,
                                      ALU.add).then_inc(ho_done, 1)
                    norm(it, ("end", "xcz"), 2 * DEPTH + 1)
                    ps = ready(dve, it, ("end", "u"))
                    dve.wait_ge(u_out, shift(it, 32, 0))
                    pv = ps.rearrange("p (b t d) -> p b t d", b=IMG, t=2)
                    for t, (t0, tn) in enumerate(TILES):
                        for b in range(IMG):
                            last = dve.tensor_tensor(usb[0:tn, b, t, :], pv[0:tn, b, t, :], binb_s[0:tn, :], ALU.add)
                        if t == 0:
                            last.then_inc(u_half, 1)
                    evacs(last, ("end", "u"))

        with ExitStack() as st:
            def ssb(name, shape, dt=F32):
                return st.enter_context(nc.sbuf_tensor(name, shape, dt))

            def ssem(name):
                return st.enter_context(nc.semaphore(name))

            toep = [ssb(f"toep{t}", [tn, CHUNKS, TOK]) for t, (t0, tn) in enumerate(TILES)]
            uin = [ssb(f"uin{t}", [tn, GRP, P]) for t, (t0, tn) in enumerate(TILES)]
            yout = [ssb(f"yout{t}", [tn, GRP, P]) for t, (t0, tn) in enumerate(TILES)]
            toep_in = ssem("toep_in")
            uin_in = ssem("uin_in")
            conv_full = ssem("conv_full")
            conv_act = ssem("conv_act")
            conv_dve = ssem("conv_dve")
            yout_out = ssem("yout_out")
            CB = 4
            STEPS = 2 * CHUNKS // CB
            blk = st.enter_context(nc.Block())

            @blk.sync
            def _(sp):
                for t, (t0, tn) in enumerate(TILES):
                    g0 = gen_dram[:, :]
                    src = bass.AP(tensor=g0.tensor, offset=t0, ap=[[1, tn], [GEN, CHUNKS], [1, TOK]])
                    sp.dma_start(toep[t][:, :, :], src).then_inc(toep_in, 16)
                with sp.Fori(0, GROUPS) as it:
                    sp.wait_ge(conv_full, shift(it, STEPS, 0))
                    for t, (t0, tn) in enumerate(TILES):
                        sp.dma_start(uin[t][:, :, :], u_dram[t0:t0 + tn, bass.ds(GRP * it, GRP), :]).then_inc(uin_in, 16)
                    for t, (t0, tn) in enumerate(TILES):
                        sp.wait_ge(conv_act, shift(it, STEPS // 2, STEPS // 4 * (t + 1)))
                        sp.wait_ge(conv_dve, shift(it, STEPS // 2, STEPS // 4 * (t + 1)))
                        sp.dma_start(y_dram[t0:t0 + tn, bass.ds(GRP * it, GRP), :], yout[t][:, :, :]).then_inc(yout_out, 16)
                sp.wait_ge(yout_out, 32 * GROUPS)

            @blk.tensor
            def _(pe):
                pe.wait_ge(toep_in, 32)
                with pe.Fori(0, GROUPS) as it:
                    pe.wait_ge(uin_in, shift(it, 32, 32))
                    for n in range(STEPS):
                        t, c0 = n // (STEPS // 2), n % (STEPS // 2) * CB
                        t0, tn = TILES[t]
                        pe.wait_ge((conv_act, conv_dve)[n % 2], shift(it, STEPS // 2, n // 2))
                        for c in range(CB):
                            for s, (s0, sn) in enumerate(TILES):
                                last = pe.matmul(psD[0:tn, n % 2, c * GRP * CW:(c + 1) * GRP * CW],
                                                 toep[s][:, c0 + c, t0:t0 + tn],
                                                 uin[s][:, :, CW * (c0 + c):CW * (c0 + c + 1)],
                                                 start=(s == 0), stop=(s == 1))
                        last.then_inc(conv_full, 1)

            def conv_view(n):
                t, c0 = n // (STEPS // 2), n % (STEPS // 2) * CB
                tn = TILES[t][1]
                dst = yout[t][:, :, CW * c0:CW * (c0 + CB)].rearrange("p b (c r) -> p c b r", c=CB)
                src = psD[0:tn, n % 2, 0:CB * GRP * CW].rearrange("p (c b r) -> p c b r", c=CB, r=CW)
                return dst, src

            @blk.scalar
            def _(act):
                with act.Fori(0, GROUPS) as it:
                    act.wait_ge(yout_out, shift(it, 32, 0))
                    for n in range(0, STEPS, 2):
                        dst, src = conv_view(n)
                        act.wait_ge(conv_full, shift(it, STEPS, n + 1))
                        act.activation(dst, src, ACT.Copy).then_inc(conv_act, 1)

            @blk.vector
            def _(dve):
                with dve.Fori(0, GROUPS) as it:
                    dve.wait_ge(yout_out, shift(it, 32, 0))
                    for n in range(1, STEPS, 2):
                        dst, src = conv_view(n)
                        dve.wait_ge(conv_full, shift(it, STEPS, n + 1))
                        dve.tensor_copy(dst, src).then_inc(conv_dve, 1)

        with ExitStack() as st:
            def ssb(name, shape, dt=F32):
                return st.enter_context(nc.sbuf_tensor(name, shape, dt))

            def ssem(name):
                return st.enter_context(nc.semaphore(name))

            w1_s = ssb("w1_s", [P, EXPERTS, 2 * P])
            w2_s = ssb("w2_s", [P, EXPERTS, 2, P])
            b2_s = ssb("b2_s", [EXPERTS, P])
            wg_s = ssb("wg_s", [P, EXPERTS])
            bgb_s = ssb("bgb_s", [P, EXPERTS])
            esel_s = ssb("esel_s", [EXPERTS, EXPERTS, P])
            closed = ssb("closed", [EXPERTS, EXPERTS, P], BF16)
            rank_s = ssb("rank_s", [P, EXPERTS])
            anti_s = ssb("anti_s", [P, P])
            yin = ssb("yin", [P, IMG, 2, P])
            hoin = ssb("hoin", [P, N])
            yT = ssb("yT", [P, N])
            gel = ssb("gel", [P, N])
            h2 = ssb("h2", [P, N])
            sq = ssb("sq3", [P, N])
            lnv = ssb("lnv3", [P, N])
            rstd = ssb("rstd3", [P, N])
            h3 = ssb("h3", [P, N])
            logit = ssb("logit", [P, IMG, 2, EXPERTS])
            top = ssb("top", [P, IMG, 2])
            cand = ssb("cand", [P, IMG, 2, EXPERTS])
            first = ssb("first", [P, IMG, 2])
            hot = ssb("hot", [P, IMG, 2, EXPERTS])
            hotT = ssb("hotT", [EXPERTS, N])
            hotb = ssb("hotb", [EXPERTS, N], BF16)
            hid = ssb("hid", [P, 4, N])
            h4 = ssb("h4", [P, N])
            yf = ssb("yf", [P, N])
            osb3 = ssb("osb3", [P, IMG, 2, P])

            w_in = ssem("w_in")
            rows_in = ssem("rows_in")
            full = [ssem(f"tail_full{b}") for b in range(2)]
            evac = [ssem(f"tail_evac{b}") for b in range(2)]
            closed_done = ssem("closed_done")
            yT_half = ssem("yT_half")
            h2_done = ssem("h2_done")
            sq_done = ssem("sq3_done")
            rstd_done = ssem("rstd3_done")
            route = ssem("route")
            hot_done = ssem("hot_done")
            hotb_done = ssem("hotb_done")
            moe_full = ssem("moe_full")
            w2_done = ssem("w2_done")
            h4_done = ssem("h4_done")
            back_half = ssem("back_half")
            out_done = ssem("out_done")
            banks = Banks(TAIL_STEPS)
            wl = [(w1_s, w1), (w2_s, w2), (b2_s, b2), (wg_s, wg), (bgb_s, bgb), (esel_s, esel), (rank_s, rank), (anti_s, anti)]

            def ready(eng, it, step):
                b, k = banks.use[step]
                eng.wait_ge(full[b], shift(it, banks.per[b], k + 1))
                return psD[:, b, :]

            def result(eng, it, step):
                b, k = banks.use[step]
                eng.wait_ge(evac[b], shift(it, banks.per[b], k + 1))

            def free(pe, it, step):
                b, k = banks.use[step]
                pe.wait_ge(evac[b], shift(it, banks.per[b], k))
                return psD[:, b, :]

            def fulls(ins, step):
                ins.then_inc(full[banks.use[step][0]], 1)

            def evacs(ins, step):
                ins.then_inc(evac[banks.use[step][0]], 1)

            FULL = ((0, 128), (LAST0, 128))
            MOE = 2 * EXPERTS
            blk = st.enter_context(nc.Block())

            @blk.sync
            def _(sp):
                for t, src in wl:
                    sp.dma_start(t[:], src).then_inc(w_in, 16)

                with sp.Fori(0, PAIRS) as it:
                    sp.wait_ge(h2_done, it)
                    for t, (t0, tn) in enumerate(TILES):
                        sp.dma_start(yin[0:tn, :, t, :], y_dram[t0:t0 + tn, bass.ds(IMG * it, IMG), :]).then_inc(rows_in, 16)
                    sp.dma_start(hoin[:, :], ho_dram[bass.ds(it, 1)].rearrange("a p n -> (a p) n")).then_inc(rows_in, 16)
                    sp.wait_ge(back_half, it + 1)
                    result(sp, it, ("back",))
                    for t, (t0, tn) in enumerate(TILES):
                        sp.dma_start(out[bass.ds(IMG * it, IMG), t0:t0 + tn, :].rearrange("b t d -> t b d"),
                                     osb3[0:tn, :, t, :]).then_inc(out_done, 16)
                sp.wait_ge(out_done, 32 * PAIRS)

            @blk.tensor
            def _(pe):
                pe.wait_ge(w_in, 16 * len(wl))
                pe.wait_ge(closed_done, 1)

                def norm_pe(it, xc, var, n, moving):
                    fulls(pe.matmul(free(pe, it, xc)[:, 0:N], cen_s[:, :], moving, start=True, stop=True), xc)
                    pe.wait_ge(sq_done, shift(it, 2, n + 1))
                    fulls(pe.matmul(free(pe, it, var)[:, 0:N], mean_s[:, :], sq[:, :], start=True, stop=True), var)

                def project(it, n):
                    result(pe, it, ("exp", n // 2, n % 2))
                    pe.matmul(psO[:, 0, 0:N], w2_s[:, n // 2, n % 2, :], hid[:, n % 4, :], start=(n == 0),
                              stop=False).then_inc(w2_done, 1)

                with pe.Fori(0, PAIRS) as it:
                    pe.wait_ge(rows_in, shift(it, 48, 48))
                    ps = free(pe, it, ("yT",))
                    for b in range(IMG):
                        for t, (t0, tn) in enumerate(TILES):
                            c0 = (b + 1) * TOK - t0 - tn
                            last = pe.matmul(ps[:, c0:c0 + tn], yin[0:tn, b, t, :], anti_s[0:tn, P - tn:P],
                                             start=True, stop=True)
                    fulls(last, ("yT",))
                    result(pe, it, ("yT",))
                    fulls(pe.matmul(free(pe, it, ("out",))[:, 0:N], wout_s[:, :], yT[:, :], start=True, stop=True), ("out",))
                    pe.wait_ge(h2_done, it + 1)
                    norm_pe(it, ("xc",), ("var",), 0, h2[:, :])
                    result(pe, it, ("xc",))
                    ps = free(pe, it, ("logit",))
                    for b in range(IMG):
                        for t, (t0, tn) in enumerate(FULL):
                            c0 = b * TOK + t0
                            last = pe.matmul(ps[:, (2 * b + t) * EXPERTS:(2 * b + t + 1) * EXPERTS], h3[:, c0:c0 + tn],
                                             wg_s[:, :], start=True, stop=True)
                    fulls(last, ("logit",))
                    pe.wait_ge(hot_done, it + 1)
                    ps = free(pe, it, ("hotT",))
                    for b in range(IMG):
                        for t, (t0, tn) in enumerate(FULL):
                            c0 = b * TOK + t0
                            last = pe.matmul(ps[0:EXPERTS, c0:c0 + tn], hot[:, b, t, :], id_s[:, :], start=True, stop=True)
                    fulls(last, ("hotT",))
                    result(pe, it, ("hotT",))
                    pe.wait_ge(hotb_done, it + 1)
                    for n in range(MOE):
                        e, j = n // 2, n % 2
                        ps = free(pe, it, ("exp", e, j))
                        pe.matmul(ps[:, 0:N], w1_s[:, e, j * P:(j + 1) * P], h3[:, :], start=True, stop=False)
                        fulls(pe.matmul(ps[:, 0:N], closed[:, e, :], hotb[:, :], start=False, stop=True), ("exp", e, j))
                        if n:
                            project(it, n - 1)
                    project(it, MOE - 1)
                    pe.matmul(psO[:, 0, 0:N], b2_s[:, :], hotT[:, :], start=False, stop=True).then_inc(moe_full, 1)
                    pe.wait_ge(h4_done, it + 1)
                    norm_pe(it, ("xcf",), ("varf",), 1, h4[:, :])
                    result(pe, it, ("xcf",))
                    ps = free(pe, it, ("back",))
                    for b in range(IMG):
                        for t, (t0, tn) in enumerate(TILES):
                            c0 = b * TOK + t0
                            last = pe.matmul(ps[0:tn, (2 * b + t) * P:(2 * b + t + 1) * P], yf[:, c0:c0 + tn],
                                             id_s[:, :], start=True, stop=True)
                    fulls(last, ("back",))

            @blk.scalar
            def _(act):
                act.wait_ge(w_in, 16 * len(wl))

                def norm(it, xc, var, n):
                    act.activation(sq[:, :], ready(act, it, xc)[:, 0:N], ACT.Square).then_inc(sq_done, 1)
                    evacs(act.activation(lnv[:, :], ready(act, it, var)[:, 0:N], ACT.Ln, bias=eps_s[:, 0:1]), var)
                    result(act, it, var)
                    act.activation(rstd[:, :], lnv[:, :], ACT.Exp, scale=-0.5).then_inc(rstd_done, 1)

                with act.Fori(0, PAIRS) as it:
                    evacs(act.activation(gel[:, :], ready(act, it, ("out",))[:, 0:N], ACT.Gelu,
                                         bias=boutc_s[:, 0:1]), ("out",))
                    norm(it, ("xc",), ("var",), 0)
                    for n in range(0, MOE, 2):
                        e, j = n // 2, n % 2
                        ps = ready(act, it, ("exp", e, j))
                        act.wait_ge(w2_done, shift(it, MOE, max(n - 3, 0)))
                        evacs(act.activation(hid[:, n % 4, :], ps[:, 0:N], ACT.Relu,
                                             bias=b1c_s[:, n:n + 1]), ("exp", e, j))
                    norm(it, ("xcf",), ("varf",), 1)

            @blk.vector
            def _(dve):
                dve.wait_ge(w_in, 16 * len(wl))
                dve.tensor_scalar(closed[:, :, :], esel_s[:, :, :], NEG, None, ALU.mult).then_inc(closed_done, 1)
                dve.wait_ge(closed_done, 1)
                with dve.Fori(0, PAIRS) as it:
                    evacs(dve.tensor_copy(yT[:, :], ready(dve, it, ("yT",))[:, 0:N]), ("yT",))
                    result(dve, it, ("out",))
                    dve.scalar_tensor_tensor(out=h2[:, :], in0=hoin[:, :], scalar=2.0, in1=gel[:, :], op0=ALU.mult,
                                             op1=ALU.add).then_inc(h2_done, 1)
                    ps = ready(dve, it, ("xc",))
                    dve.wait_ge(rstd_done, shift(it, 2, 1))
                    evacs(dve.tensor_tensor(h3[:, :], ps[:, 0:N], rstd[:, :], ALU.mult), ("xc",))
                    ps = ready(dve, it, ("logit",))
                    step = [0]

                    def then(ins):
                        step[0] += 1
                        ins.then_inc(route, 1)
                        dve.wait_ge(route, shift(it, 3, step[0]))

                    lg = logit[:, :, :, :].rearrange("p b t e -> p (b t) e")
                    tp = top[:, :, :].rearrange("p b t -> p (b t)")
                    cd = cand[:, :, :, :].rearrange("p b t e -> p (b t) e")
                    fi = first[:, :, :].rearrange("p b t -> p (b t)")
                    ht = hot[:, :, :, :].rearrange("p b t e -> p (b t) e")
                    sh = [P, 2 * IMG, EXPERTS]
                    evacs(dve.tensor_tensor(lg, ps[:, 0:2 * IMG * EXPERTS].rearrange("p (t e) -> p t e", e=EXPERTS),
                                            bgb_s[:, :].unsqueeze(1).to_broadcast(sh), ALU.add), ("logit",))
                    result(dve, it, ("logit",))
                    then(dve.tensor_reduce(tp, lg, AX_X, ALU.max))
                    then(dve.tensor_tensor(cd, lg, tp.unsqueeze(2).to_broadcast(sh), ALU.is_equal))
                    dve.tensor_tensor(cd, cd, rank_s[:, :].unsqueeze(1).to_broadcast(sh), ALU.mult).then_inc(route, 1)
                    dve.wait_ge(route, shift(it, 3, 3))
                    dve.tensor_reduce(fi, cd, AX_X, ALU.max).then_inc(yT_half, 1)
                    dve.wait_ge(yT_half, it + 1)
                    dve.tensor_tensor(ht, cd, fi.unsqueeze(2).to_broadcast(sh), ALU.is_equal).then_inc(hot_done, 1)
                    ps = ready(dve, it, ("hotT",))
                    dve.tensor_copy(hotb[:, :], ps[0:EXPERTS, 0:N]).then_inc(hotb_done, 1)
                    evacs(dve.tensor_copy(hotT[:, :], ps[0:EXPERTS, 0:N]), ("hotT",))
                    for n in range(1, MOE, 2):
                        e, j = n // 2, n % 2
                        ps = ready(dve, it, ("exp", e, j))
                        dve.wait_ge(w2_done, shift(it, MOE, max(n - 3, 0)))
                        evacs(dve.tensor_scalar(hid[:, n % 4, :], ps[:, 0:N], b1c_s[:, n:n + 1], 0.0, ALU.add,
                                                ALU.max), ("exp", e, j))
                    dve.wait_ge(moe_full, it + 1)
                    dve.tensor_tensor(h4[:, :], psO[:, 0, 0:N], h3[:, :], ALU.add).then_inc(h4_done, 1)
                    ps = ready(dve, it, ("xcf",))
                    dve.wait_ge(rstd_done, shift(it, 2, 2))
                    evacs(dve.tensor_tensor(yf[:, :], ps[:, 0:N], rstd[:, :], ALU.mult), ("xcf",))
                    ps = ready(dve, it, ("back",))
                    dve.wait_ge(out_done, shift(it, 32, 0))
                    pv = ps.rearrange("p (b t d) -> p b t d", b=IMG, t=2)
                    for t, (t0, tn) in enumerate(TILES):
                        for b in range(IMG):
                            last = dve.tensor_copy(osb3[0:tn, b, t, :], pv[0:tn, b, t, :])
                        if t == 0:
                            last.then_inc(back_half, 1)
                    evacs(last, ("back",))


TURNS = 0.15915494309189535
MAGIC = 12582912.0
PI2 = (6.28125, 0.0019350051879882812, 3.0199159819567e-07)
PI_BELOW = 3.1415925

_INS = ["x", "conv", "convb", "clsc", "posT", "qkv", "qkvb", "projp", "projn", "projb", "ln1", "fc1", "fc1b", "fc2",
        "fc2b", "ln2", "normwb", "attg", "win", "binb", "wout", "boutc", "lre", "lim", "bm", "cre", "cim", "dvec",
        "w1", "b1c", "w2", "b2", "wg", "bgb", "om", "ident", "cen", "mean", "dsel", "esel", "rank", "anti"]


def layouts(i, np):
    L, D = DEPTH, P
    v = {k.replace("L0_", ""): np.asarray(a) for k, a in i.items()}
    a = {}
    x = v["x"]
    b = x.shape[0]
    xp = x.reshape(b // 2, 2, 3, 14, 16, 14, 16).transpose(0, 2, 4, 6, 1, 3, 5).reshape(b // 2, KCH, D, 2 * PATCH)
    xp = xp.transpose(0, 2, 1, 3)
    a["x"] = np.concatenate([xp, xp[:1]], axis=0)
    a["conv"] = v["tok_conv_w"].reshape(KCH, D, D).transpose(1, 0, 2)
    a["convb"] = v["tok_conv_b"][:, None]
    a["clsc"] = v["tok_cls_token"].reshape(D, 1)
    a["posT"] = v["tok_pos_embed"][0].T
    a["qkv"] = v["tok_qkv_w"].transpose(1, 0, 2)
    a["qkvb"] = v["tok_qkv_b"].reshape(L * 3, D).T
    pj = v["tok_proj_w"]
    pp = np.zeros((L, 2, 4, 32, D), pj.dtype)
    pp[:, :, :, :HD] = pj.reshape(L, 2, 4, HD, D)
    a["projp"] = pp.reshape(L, 2, D, D).transpose(2, 0, 1, 3)
    a["projn"] = pj.transpose(1, 0, 2)
    a["projb"] = v["tok_proj_b"].T
    a["ln1"] = np.concatenate([v["tok_ln1_w"], v["tok_ln1_b"]]).T
    a["ln2"] = np.concatenate([v["tok_ln2_w"], v["tok_ln2_b"]]).T
    a["fc1"] = v["tok_fc1_w"].transpose(1, 0, 2)
    a["fc1b"] = v["tok_fc1_b"].reshape(L * 2, D).T
    a["fc2"] = v["tok_fc2_w"].reshape(L, 2, D, D).transpose(2, 0, 1, 3)
    a["fc2b"] = v["tok_fc2_b"].T
    a["normwb"] = np.stack([v["tok_norm_w"], v["tok_norm_b"]], 1)
    a["attg"] = np.stack([v["attn_ln_gamma"], v["attn_ln_beta"]], 1)
    a["win"] = v["attn_Win"]
    a["binb"] = np.broadcast_to(v["attn_bin_"], (D, D))
    a["wout"] = v["attn_Wout"]
    a["boutc"] = v["attn_bout"][:, None]
    for n, k in (("lre", "attn_Lambda_re"), ("lim", "attn_Lambda_im"), ("bm", "attn_Bmat"), ("cre", "attn_C_re"),
                 ("cim", "attn_C_im")):
        a[n] = v[k].reshape(CG, D).T
    a["dvec"] = v["attn_Dvec"][:, None]
    a["w1"] = v["ffn_W1"].transpose(1, 0, 2)
    a["b1c"] = v["ffn_b1"].reshape(2 * EXPERTS, D).T
    a["w2"] = v["ffn_W2"].reshape(EXPERTS, 2, D, D).transpose(2, 0, 1, 3)
    a["b2"] = v["ffn_b2"]
    a["wg"] = v["ffn_Wg"]
    a["bgb"] = np.broadcast_to(v["ffn_bg"], (D, EXPERTS))
    f = np.float32
    j = (TOK - 1) - np.arange(GEN)
    a["om"] = np.broadcast_to(np.where(j >= 0, j, -j - 1).astype(f), (D, GEN))
    a["ident"] = np.eye(D, dtype=f)
    a["anti"] = np.eye(D, dtype=f)[::-1]
    a["cen"] = (np.eye(D) - 1.0 / D).astype(f)
    a["mean"] = np.full((D, D), 1.0 / D, f)
    r = np.arange(D)
    a["dsel"] = (r[:, None] == (r // 32 * 32 + HD)[None, :]).astype(f)
    a["esel"] = np.broadcast_to((1 - np.eye(EXPERTS))[:, :, None], (EXPERTS, EXPERTS, D)).astype(f)
    a["rank"] = np.broadcast_to(np.arange(EXPERTS, 0, -1).astype(f), (D, EXPERTS))
    return {k: np.ascontiguousarray(a[k]) for k in _INS}


def kernel(**inputs):
    import numpy as np
    import concourse.bacc as bacc
    from concourse.bass_utils import run_bass_kernel_spmd

    arrays = layouts(inputs, np)
    batch = inputs["x"].shape[0]
    nc = bacc.Bacc("TRN2", target_bir_lowering=False, num_devices=1)
    args = {k: nc.dram_tensor(k, a.shape, mybir.dt.from_np(a.dtype), kind="ExternalInput").ap()
            for k, a in arrays.items()}
    args["out"] = nc.dram_tensor("out", (batch, TOK, P), F32, kind="ExternalOutput").ap()
    build(nc, **args)
    r = run_bass_kernel_spmd(nc, [arrays], core_ids=[0])
    return r.results[0]["out"]
```

```python
from contextlib import ExitStack

import concourse.bass as bass
from concourse import mybir

F32 = mybir.dt.float32
F16 = mybir.dt.float16
BF16 = mybir.dt.bfloat16
ALU = mybir.AluOpType
ACT = mybir.ActivationFunctionType
AX_X = mybir.AxisListType.X

P = 128
TOK = 197
PATCH = TOK - 1
IMG = 2
N = IMG * TOK
DEPTH = 4
HEADS = 8
HD = P // HEADS
KCH = 6
EXPERTS = 8
TILES = ((0, 128), (128, TOK - 128))
LAST0 = TOK - 128
EPS = 1e-5
CHUNKS = 32
CW = P // CHUNKS
GEN = 2 * TOK - 1
STATE = 64
CG = CHUNKS // 2
NEG = -1e30
ONE_ROW = 96


FIRST = 1


def shift(it, per, k):
    return it * per + k + FIRST


def start(nc, sems):
    with nc.Block() as blk:
        @blk.gpsimd
        def _(pool):
            for sem in sems:
                pool.sem_inc(sem, FIRST)


class Banks:

    def __init__(self, steps):
        self.use, count = {}, [0, 0]
        for n, step in enumerate(steps):
            b = n % 2
            self.use[step] = (b, count[b])
            count[b] += 1
        self.per = count


ROUNDS = 2 * DEPTH
NORM_SET = "natural_log_exp_and_others"


def timed(*parts):
    out = [(t0 + (t1 - t0) * (n + 0.5) / len(steps), k, step) for k, (t0, t1, steps) in enumerate(parts)
           for n, step in enumerate(steps)]
    return [step for _, _, step in sorted(out, key=lambda x: x[:2])]


def of(p, *steps):
    return [(step, p) for step in steps]


def probs(p):
    return [("c", p, 0), ("c", p, 1), ("c", p, 2), ("c", p, 3), ("w", p, 0), ("c", p, 4), ("c", p, 5), ("w", p, 1),
            ("c", p, 6), ("c", p, 7), ("w", p, 2), ("o", p, 0), ("w", p, 3), ("o", p, 1)]


def maxima(p):
    return [("b", p, n) for n in range(8)]


FIRST_HALF = ("sq1", "var1", "y1", "q", "k", "v")
END = ("sqn", "varn", "ho", "xcz", "varz", "yz", "u")
TO_MLP = ("den", "on", "proj", "sq2", "var2", "y2")
MLP = [(step, p) for step in ("fc1", "gelu", "fc2") for p in range(2)]


def one_round(first, a):
    return timed((a[0], a[1], of(0, *first)), (a[2], a[3], of(1, *first)),
                 (a[4], a[5], probs(0)), (a[5], a[6], probs(1)),
                 (a[7], a[8], of(0, *TO_MLP)), (a[9], a[10], of(1, *TO_MLP)), (a[11], a[12], MLP),
                 (a[13], a[14], maxima(0)), (a[15], a[15], of(0, "neg")),
                 (a[14], a[16], maxima(1)), (a[17], a[17], of(1, "neg")))


ORDER = one_round(FIRST_HALF, (0.03, 0.32, 0.14, 0.44, 0.0, 0.27, 0.56, 0.3, 0.64, 0.6, 0.86, 0.84, 1.0, 0.45, 0.72,
                               0.76, 0.97, 0.99))
ORDER_END = one_round(END + ("emb",) + FIRST_HALF,
                      (0.02, 0.47, 0.05, 0.57, 0.0, 0.3, 0.56, 0.5, 0.72, 0.68, 0.88, 0.86, 1.0, 0.56, 0.78,
                       0.8, 0.97, 0.99))
BODY = [(r, x) for r in range(ROUNDS) for x in (ORDER_END if r < 2 else ORDER)]
LAST_0 = timed((0.02, 0.5, of(0, *END)), (0.05, 0.55, of(1, *END)), (0.0, 0.3, probs(0)), (0.3, 0.6, probs(1)),
               (0.4, 0.7, of(0, *TO_MLP)), (0.65, 0.85, of(1, *TO_MLP)), (0.86, 1.0, MLP))
LAST_1 = timed((0.0, 0.9, of(0, *END)), (0.1, 1.0, of(1, *END)))
LAST = [(0, x) for x in LAST_0] + [(1, x) for x in LAST_1]

DENSE = {"varn": ("varn",), "xcz": ("xcz",), "varz": ("varz",), "u": ("u",), "emb": ("emb",), "var1": ("var1",),
         "q": ("q",), "k": ("k",), "v": ("v",), "den": ("den0", "den1"), "proj": ("proj",),
         "var2": ("var2",), "fc1": ("fc1a", "fc1b"), "neg": ("neg",), "fc2": ("fc2",)}
COUNTED = {
    "sq": {"sqn": 1, "xcz": 1, "sq1": 1, "sq2": 1},
    "rstd": {"varn": 1, "varz": 1, "var1": 1, "var2": 1},
    "y": {"ho": 1, "yz": 1, "y1": 1, "y2": 1},
    "hi": {"q": 1, "k": 1},
    "v": {"v": 1},
    "split": {"k": 32},
    "stacks": {"k": 128},
    "b": {"b": 1},
    "c": {"c": 1},
    "w": {"w": 1},
    "o": {"o": 1},
    "neg": {"neg": 16},
    "rden": {"den": 2},
    "on": {"on": 1},
    "ho": {"ho": 1},
    "ho_out": {"ho": 16},
    "u": {"u": 1},
    "u_out": {"u": 32},
    "cls": {"emb": 1},
}


BY_PAIR = ("split", "stacks", "neg", "ho_out", "u_out")


def dense(steps):
    return [(r, d, x[1]) for r, x in steps for d in DENSE.get(x[0], ())]


def counts(steps):
    out = {}
    for name, adds in COUNTED.items():
        total, at = [0, 0], {}
        for r, x in steps:
            p = x[1] if name in BY_PAIR else 0
            total[p] += adds.get(x[0], 0)
            at[(r, x)] = total[p]
        out[name] = (at, total[0])
    return out


TAIL_FRONT = ("yT", "out", "h2", "xc", "var", "h3", "logit", "route", "hotT")
TAIL_BACK = ("h4", "xcf", "varf", "yf", "back")
TAIL_USES = ("yT", "out", "xc", "var", "logit", "hotT", "xcf", "varf", "back")


def experts(q):
    n = 2 * EXPERTS
    out = []
    for k in range(n + 2):
        out += [("exp", q, k)] * (k < n) + [("w2", q, k - 2)] * (k >= 2)
    return out + [("b2", q)]


def tail_half(q, *chain):
    return [("half", q)] + timed((0.0, 1.0, experts(q)), (0.0, 1.0, of(1 - q, *chain)))


TAIL_FIRST = of(0, *TAIL_FRONT) + tail_half(0, *TAIL_FRONT)
TAIL_BODY = tail_half(1, *(TAIL_BACK + TAIL_FRONT)) + tail_half(0, *(TAIL_BACK + TAIL_FRONT))
TAIL_LAST = tail_half(1, *TAIL_BACK) + [("half", 0)] + of(1, *TAIL_BACK)
TAIL_BANK = {x: x[2] % 2 for x in TAIL_BODY if x[0] == "exp"}
TAIL_BANK.update({x: 2 + n % 2 for n, x in enumerate(x for x in TAIL_BODY if x[0] in TAIL_USES)})
TAIL_COUNTED = {"h2": {"h2": 1}, "sq": {"xc": 1, "xcf": 1}, "rstd": {"var": 1, "varf": 1}, "route": {"route": 5},
                "w2": {"w2": 1}, "moe": {"b2": 1}, "h4": {"h4": 1}, "back": {"back": 1}}


def tail_count(steps):
    adds = {name: (lambda x, by=by: by.get(x[0], 0)) for name, by in TAIL_COUNTED.items()}
    for b in range(4):
        adds[b] = lambda x, b=b: int(TAIL_BANK.get(x) == b)
    for q in range(2):
        adds[f"rows{q}"] = lambda x, q=q: 48 * (x == ("yT", q))
        adds[f"out{q}"] = lambda x, q=q: 32 * (x == ("back", q))
    out = {}
    for name, add in adds.items():
        total, at = 0, {}
        for x in steps:
            total += add(x)
            at[x] = total
        out[name] = (at, total)
    return out


def build(nc, x, conv, convb, clsc, posT, qkv, qkvb, projp, projn, projb, ln1, fc1, fc1b, fc2, fc2b, ln2,
          normwb, attg, win, binb, wout, boutc, lre, lim, bm, cre, cim, dvec, w1, b1c, w2, b2, wg, bgb,
          om, ident, cen, mean, gsel, esel, rank, anti, out):
    B = out.shape[0]
    PAIRS = B // IMG
    GRP = B // 4 if B >= 8 else B
    GROUPS = B // GRP

    with ExitStack() as ctx:
        def sb(name, shape, dt=F32):
            return ctx.enter_context(nc.sbuf_tensor(name, shape, dt))

        def sem(name):
            return ctx.enter_context(nc.semaphore(name))

        split_dram = nc.dram_tensor("split_dram", (2, 2, 2, HEADS, HD, N), F16).ap()
        gen_dram = nc.dram_tensor("gen_dram", (CHUNKS, GEN), F32).ap()
        u_dram = nc.dram_tensor("u_dram", (TOK, B + 4 * IMG, P), F32).ap()
        y_dram = nc.dram_tensor("y_dram", (TOK, B, P), F32).ap()
        ho_dram = nc.dram_tensor("ho_dram", (PAIRS + 4, P, N), F32).ap()

        psA = ctx.enter_context(nc.psum_tensor("psA", [P, 2, 2, 512], F32))
        psD = ctx.enter_context(nc.psum_tensor("psD", [P, 2, 512], F32))
        psO = ctx.enter_context(nc.psum_tensor("psO", [P, 2, 512], F32))

        const_in = sem("const_in")

        conv_s = sb("conv_s", [P, KCH, P])
        qkv_s = sb("qkv_s", [P, DEPTH, 3 * P])
        projp_s = sb("projp_s", [P, DEPTH, 2, P])
        fc1_s = sb("fc1_s", [P, DEPTH, 2 * P])
        fc2_s = sb("fc2_s", [P, DEPTH, 2, P])
        win_s = sb("win_s", [P, P])
        wout_s = sb("wout_s", [P, P])
        cen_s = sb("cen_s", [P, P])
        mean_s = sb("mean_s", [P, P])
        gsel_s = sb("gsel_s", [P, P])
        id_s = sb("id_s", [P, P])
        pos_s = sb("pos_s", [P, TOK])
        binb_s = sb("binb_s", [P, P])
        vecs = {}
        for nm_, src in (("convb", convb), ("clsc", clsc), ("qkvb", qkvb), ("projb", projb), ("ln1", ln1),
                         ("fc1b", fc1b), ("fc2b", fc2b), ("ln2", ln2), ("normwb", normwb), ("attg", attg),
                         ("boutc", boutc), ("lre", lre), ("lim", lim), ("bm", bm), ("cre", cre), ("cim", cim),
                         ("b1c", b1c)):
            vecs[nm_] = (sb(nm_ + "_s", [P, src.shape[1]]), src)
        convb_s, clsc_s, qkvb_s, projb_s, ln1_s, fc1b_s, fc2b_s, ln2_s, normwb_s, attg_s, boutc_s, lre_s, lim_s, \
            bm_s, cre_s, cim_s, b1c_s = [vecs[k][0] for k in vecs]
        loads = [(conv_s, conv), (qkv_s, qkv), (projp_s, projp), (fc1_s, fc1), (fc2_s, fc2), (win_s, win),
                 (wout_s, wout), (cen_s, cen), (mean_s, mean), (gsel_s, gsel), (id_s, ident), (pos_s, posT),
                 (binb_s, binb)] + list(vecs.values())
        bias_s = sb("bias_s", [P, DEPTH, 6])
        eps_s = sb("eps_s", [P, 1])

        with ExitStack() as pre:
            def psb(name, shape, dt=F32):
                return pre.enter_context(nc.sbuf_tensor(name, shape, dt))
            projn_s = psb("projn_s", [P, DEPTH, P])
            om_s = psb("om_s", [P, GEN])
            dvec_s = psb("dvec_s", [CHUNKS, 1])
            cb = psb("cb", [P, 2, CG])
            lw = psb("lw", [P, 2, CG * CHUNKS])
            ang = psb("ang", [P, GEN])
            turn = psb("turn", [P, GEN])
            red = psb("red", [P, GEN])
            red2 = psb("red2", [P, GEN])
            dec = psb("dec", [P, GEN])
            sn = psb("sn", [P, GEN])
            hs = psb("hs", [P, GEN])
            cs = psb("cs", [P, GEN])
            ec = psb("ec", [P, 2, GEN])
            es = psb("es", [P, 2, GEN])
            gen = psb("gen", [CHUNKS, GEN])
            wsum = psb("wsum", [P, KCH + 4 * DEPTH])
            pre_loads = [(projn_s, projn), (om_s, om), (dvec_s, dvec)]

            fold = pre.enter_context(nc.semaphore("fold"))
            shifts_full = pre.enter_context(nc.semaphore("shifts_full"))
            vshift = pre.enter_context(nc.semaphore("vshift"))
            bias_done = pre.enter_context(nc.semaphore("bias_done"))
            centred = pre.enter_context(nc.semaphore("centred"))
            proj_full = pre.enter_context(nc.semaphore("proj_full"))
            winfull = pre.enter_context(nc.semaphore("winfull"))
            chain = pre.enter_context(nc.semaphore("chain"))
            reduced = pre.enter_context(nc.semaphore("reduced"))
            waves = pre.enter_context(nc.semaphore("waves"))
            damped = pre.enter_context(nc.semaphore("damped"))
            summed = pre.enter_context(nc.semaphore("summed"))
            gen_out = pre.enter_context(nc.semaphore("gen_out"))
            gen_done = pre.enter_context(nc.semaphore("gen_done"))
            n_const = 16 * (len(loads) + len(pre_loads))
            blk = pre.enter_context(nc.Block())

            @blk.sync
            def _(sp):
                for t, src in loads + pre_loads:
                    sp.dma_start(t[:], src).then_inc(const_in, 16)
                sp.wait_ge(gen_done, 1)
                sp.dma_start(gen_dram, gen[:, :]).then_inc(gen_out, 16)
                sp.wait_ge(gen_out, 16)

            @blk.tensor
            def _(pe):
                pe.wait_ge(const_in, n_const)
                for l in range(DEPTH):
                    for j in range(3):
                        pe.matmul(psD[:, 0, 8 * l + j:8 * l + j + 1], qkv_s[:, l, j * P:(j + 1) * P],
                                  ln1_s[:, DEPTH + l:DEPTH + l + 1], start=True, stop=True)
                    for j in range(2):
                        last = pe.matmul(psD[:, 0, 8 * l + 3 + j:8 * l + 4 + j], fc1_s[:, l, j * P:(j + 1) * P],
                                         ln2_s[:, DEPTH + l:DEPTH + l + 1], start=True, stop=True)
                last = pe.matmul(psD[:, 0, 128:256], attg_s[:, 1:2].to_broadcast([P, P]), win_s[:, :],
                                 start=True, stop=True)
                last.then_inc(shifts_full, 1)
                pe.wait_ge(vshift, 1)
                for l in range(DEPTH):
                    last = pe.matmul(psD[:, 1, l:l + 1], projn_s[:, l, :], bias_s[:, l, 2:3], start=True, stop=True)
                last.then_inc(proj_full, 1)
                pe.wait_ge(bias_done, 1)
                pe.matmul(psD[:, 1, 8:8 + TOK], cen_s[:, :], pos_s[:, :], start=True, stop=True)
                pe.matmul(psD[:, 1, 256:256 + DEPTH], cen_s[:, :], bias_s[:, :, 5], start=True, stop=True)
                pe.matmul(psD[:, 1, 260:260 + DEPTH], cen_s[:, :], fc2b_s[:, :], start=True,
                          stop=True).then_inc(centred, 1)
                for g in range(CG):
                    pe.wait_ge(damped, 2 * (g + 1))
                    pe.matmul(psA[0:CHUNKS, 0, 0, 0:GEN], lw[:, 0, g * CHUNKS:(g + 1) * CHUNKS], ec[:, g % 2, :],
                              start=(g == 0), stop=False)
                    pe.matmul(psA[0:CHUNKS, 0, 0, 0:GEN], lw[:, 1, g * CHUNKS:(g + 1) * CHUNKS], es[:, g % 2, :],
                              start=False, stop=(g == CG - 1)).then_inc(summed, 1)

            @blk.scalar
            def _(act):
                act.wait_ge(const_in, n_const)
                for g in range(CG):
                    if g >= 1:
                        act.wait_ge(damped, 2 * g)
                    act.activation(dec[:, :], om_s[:, :], ACT.Exp, scale=lre_s[:, g:g + 1]).then_inc(waves, 1)
                    act.wait_ge(reduced, g + 1)
                    act.activation(sn[:, :], red2[:, :], ACT.Sin).then_inc(waves, 1)
                    act.activation(hs[:, :], red2[:, :], ACT.Sin, scale=0.5).then_inc(waves, 1)

            @blk.vector
            def _(dve):
                steps = [0]

                def then(ins):
                    steps[0] += 1
                    ins.then_inc(chain, 1)
                    dve.wait_ge(chain, steps[0])

                dve.memset(eps_s[:, :], EPS)
                then(dve.memset(lw[:, :, :], 0.0))
                dve.wait_ge(const_in, n_const)
                dve.tensor_scalar(pos_s[:, 1:TOK], pos_s[:, 1:TOK], convb_s[:, 0:1], None, ALU.add)
                dve.tensor_tensor(pos_s[:, 0:1], pos_s[:, 0:1], clsc_s[:, 0:1], ALU.add)
                dve.wait_ge(shifts_full, 1)
                sv = psD[:, 0, 0:8 * DEPTH].rearrange("p (l k) -> p l k", k=8)
                dve.tensor_tensor(bias_s[:, :, 0:3], sv[:, :, 0:3],
                                  qkvb_s[:, :].rearrange("p (l k) -> p l k", k=3), ALU.add)
                dve.tensor_tensor(bias_s[:, :, 3:5], sv[:, :, 3:5],
                                  fc1b_s[:, :].rearrange("p (l k) -> p l k", k=2), ALU.add)
                then(dve.tensor_tensor(binb_s[:, :], psD[:, 0, 128:256], binb_s[:, :], ALU.add))
                dve.tensor_scalar(bias_s[:, :, 0:1], bias_s[:, :, 0:1], float(HD) ** -0.5, None,
                                  ALU.mult).then_inc(vshift, 1)
                for l in range(DEPTH):
                    dve.tensor_scalar(qkv_s[:, l, P:], qkv_s[:, l, P:], ln1_s[:, l:l + 1], None, ALU.mult)
                    dve.tensor_scalar(qkv_s[:, l, 0:P], qkv_s[:, l, 0:P], ln1_s[:, l:l + 1], float(HD) ** -0.5,
                                      ALU.mult, ALU.mult)
                    dve.tensor_scalar(fc1_s[:, l, :], fc1_s[:, l, :], ln2_s[:, l:l + 1], None, ALU.mult)
                dve.tensor_scalar(win_s[:, :], win_s[:, :], attg_s[:, 0:1], None, ALU.mult)
                dve.wait_ge(proj_full, 1)
                dve.tensor_tensor(bias_s[:, :, 5], psD[:, 1, 0:DEPTH], projb_s[:, :], ALU.add).then_inc(bias_done, 1)
                parts = [(conv_s[:, :, :], KCH), (projp_s[:, :, :, :].rearrange("p l g n -> p (l g) n"), 2 * DEPTH),
                         (fc2_s[:, :, :, :].rearrange("p l j n -> p (l j) n"), 2 * DEPTH)]
                k0 = 0
                for w, k in parts:
                    last = dve.tensor_reduce(wsum[:, k0:k0 + k], w, AX_X, ALU.add)
                    k0 += k
                then(last)
                then(dve.tensor_scalar(wsum[:, :], wsum[:, :], 1.0 / P, None, ALU.mult))
                k0 = 0
                for w, k in parts:
                    for i in range(k):
                        dve.tensor_scalar(w[:, i, :], w[:, i, :], wsum[:, k0 + i:k0 + i + 1], None, ALU.subtract)
                    k0 += k
                dve.wait_ge(centred, 1)
                dve.tensor_copy(pos_s[:, :], psD[:, 1, 8:8 + TOK])
                dve.tensor_copy(bias_s[:, :, 5], psD[:, 1, 256:256 + DEPTH])
                dve.tensor_copy(fc2b_s[:, :], psD[:, 1, 260:260 + DEPTH])
                dve.tensor_tensor(cb[:, 0, :], cre_s[:, :], bm_s[:, :], ALU.mult)
                then(dve.tensor_tensor(cb[:, 1, :], cim_s[:, :], bm_s[:, :], ALU.mult))
                for i in range(2):
                    r = slice(STATE * i, STATE * (i + 1))
                    dve.tensor_scalar(lw[r, 0, i::CHUNKS + 2], cb[r, 0, :], 1.0, None, ALU.mult)
                    then(dve.tensor_scalar(lw[r, 1, i::CHUNKS + 2], cb[r, 1, :], -1.0, None, ALU.mult))
                for g in range(CG):
                    then(dve.tensor_scalar(ang[:, :], om_s[:, :], lim_s[:, g:g + 1], None, ALU.mult))
                    then(dve.tensor_scalar(turn[:, :], ang[:, :], TURNS, MAGIC, ALU.mult, ALU.add))
                    then(dve.tensor_scalar(turn[:, :], turn[:, :], MAGIC, None, ALU.subtract))
                    then(dve.scalar_tensor_tensor(out=red[:, :], in0=turn[:, :], scalar=-PI2[0], in1=ang[:, :],
                                                  op0=ALU.mult, op1=ALU.add))
                    then(dve.scalar_tensor_tensor(out=red[:, :], in0=turn[:, :], scalar=-PI2[1], in1=red[:, :],
                                                  op0=ALU.mult, op1=ALU.add))
                    then(dve.scalar_tensor_tensor(out=red[:, :], in0=turn[:, :], scalar=-PI2[2], in1=red[:, :],
                                                  op0=ALU.mult, op1=ALU.add))
                    dve.tensor_scalar(red2[:, :], red[:, :], PI_BELOW, -PI_BELOW, ALU.min,
                                      ALU.max).then_inc(reduced, 1)
                    dve.wait_ge(waves, 3 * (g + 1))
                    then(dve.scalar_tensor_tensor(out=cs[:, :], in0=hs[:, :], scalar=-2.0, in1=hs[:, :],
                                                  op0=ALU.mult, op1=ALU.mult))
                    if g >= 2:
                        dve.wait_ge(summed, g - 1)
                    dve.scalar_tensor_tensor(out=ec[:, g % 2, :], in0=cs[:, :], scalar=1.0, in1=dec[:, :],
                                             op0=ALU.add, op1=ALU.mult).then_inc(damped, 1)
                    dve.tensor_tensor(es[:, g % 2, :], sn[:, :], dec[:, :], ALU.mult).then_inc(damped, 1)
                dve.wait_ge(summed, CG)
                then(dve.tensor_copy(gen[:, :], psA[0:CHUNKS, 0, 0, 0:GEN]))
                dve.tensor_tensor(gen[:, TOK - 1:TOK], gen[:, TOK - 1:TOK], dvec_s[:, :],
                                  ALU.add).then_inc(gen_done, 1)

        with ExitStack() as st:
            def ssb(name, shape, dt=F32):
                return st.enter_context(nc.sbuf_tensor(name, shape, dt))

            counted = []

            def ssem(name):
                counted.append(st.enter_context(nc.semaphore(name)))
                return counted[-1]

            def four(name, shape, dt=F32):
                return [[ssb(f"{name}{s}{p}", shape, dt) for p in range(2)] for s in range(2)]

            def two(name, shape, dt=F32):
                return [ssb(f"{name}{p}", shape, dt) for p in range(2)]

            h = four("h", [P, N])
            qst = four("qst", [P, HEADS, N], F16)
            kst = four("kst", [P, HEADS, N], F16)
            vals = four("vals", [P, IMG, 2, HEADS, 2 * HD])
            patches = two("patches", [P, KCH, IMG * PATCH])
            sq = two("sq", [P, N])
            lnv = two("lnv", [P, N])
            rstd = two("rstd", [P, N])
            y = two("y", [P, N])
            qsp = two("qsp", [P, 2, N], F16)
            ksp = two("ksp", [P, 2, N], F16)
            nmax = two("nmax", [P, IMG, 2, HEADS], F16)
            idh_s = ssb("idh_s", [P, P], F16)
            nmT = two("nmT", [HEADS, N], F16)
            prob = ssb("prob", [P, 4, 4, TOK])
            osb = two("osb", [P, 2, N])
            lden = two("lden", [P, 2, N])
            rden = two("rden", [P, 2, N])
            on = two("on", [P, 2, N])
            gl = two("gl", [P, 2, N])
            ho = two("ho", [P, N])
            usb = two("usb", [P, IMG, 2, P])

            patches_in = [ssem(f"patches_in{p}") for p in range(2)]
            full = [ssem(f"dense_full{b}") for b in range(2)]
            evac = [ssem(f"dense_evac{b}") for b in range(2)]
            set_up = st.enter_context(nc.semaphore("set_up"))
            cls_done = ssem("cls_done")
            sq_done = ssem("sq_done")
            rstd_done = ssem("rstd_done")
            y_done = ssem("y_done")
            hi_done = ssem("hi_done")
            v_parts = ssem("v_parts")
            split_out = [ssem(f"split_out{p}") for p in range(2)]
            stacks_in = [ssem(f"stacks_in{p}") for p in range(2)]
            keys_full = ssem("keys_full")
            max_done = ssem("max_done")
            neg_in = [ssem(f"neg_in{p}") for p in range(2)]
            probs_full = ssem("probs_full")
            exp_done = ssem("exp_done")
            pv_done = ssem("pv_done")
            o_copied = ssem("o_copied")
            rden_done = ssem("rden_done")
            on_done = ssem("on_done")
            ho_done = ssem("ho_done")
            ho_out = [ssem(f"ho_out{p}") for p in range(2)]
            u_parts = ssem("u_parts")
            u_out = [ssem(f"u_out{p}") for p in range(2)]
            sems = {"sq": sq_done, "rstd": rstd_done, "y": y_done, "hi": hi_done, "v": v_parts, "split": split_out,
                    "stacks": stacks_in, "b": max_done, "c": exp_done, "w": pv_done, "o": o_copied, "neg": neg_in,
                    "rden": rden_done, "on": on_done, "ho": ho_done, "ho_out": ho_out, "u": u_parts,
                    "u_out": u_out, "cls": cls_done}
            ITERS = PAIRS // 4
            body, last_part = Banks(dense(BODY)), Banks(dense(LAST))
            body_counts, last_counts = counts(BODY), counts(LAST)
            units = [[(r, x) for r, x in steps if x[0] in "bc"] for steps in (BODY, LAST)]

            class At:

                def __init__(self, it, last=False):
                    self.it, self.banks = it, last_part if last else body
                    self.counts = last_counts if last else body_counts
                    self.units = units[last]

                def slot(self, r, x):
                    return self.units.index((r, x)) % 2

                def bank(self, r, step, p, more):
                    b, k = self.banks.use[(r, step, p)]
                    return b, shift(self.it, body.per[b], k + more)

            def signal(name, step):
                return sems[name][step[1]] if name in BY_PAIR else sems[name]

            def wait(eng, at, name, r, step):
                eng.wait_ge(signal(name, step), shift(at.it, body_counts[name][1], at.counts[name][0][(r, step)]))

            def wait_before(eng, at, name, r, step, back=1):
                add = COUNTED[name][step[0]]
                k = at.counts[name][0][(r, step)] - back * add
                if k >= 0:
                    eng.wait_ge(signal(name, step), shift(at.it, body_counts[name][1], k))
                else:
                    eng.wait_ge(signal(name, step), shift(at.it, body_counts[name][1], 0))

            def wait_round(eng, at, name, r, step):
                if r:
                    wait(eng, at, name, r - 1, step)
                else:
                    eng.wait_ge(signal(name, step), shift(at.it, body_counts[name][1], 0))

            def ready(eng, at, r, step, p):
                b, v = at.bank(r, step, p, 1)
                eng.wait_ge(full[b], v)
                return psD[:, b, :]

            def result(eng, at, r, step, p):
                b, v = at.bank(r, step, p, 1)
                eng.wait_ge(evac[b], v)

            def free(pe, at, r, step, p, after=()):
                own, k = at.banks.use[(r, step, p)]
                need = {own: k}
                for d in after:
                    b, k = at.banks.use[(r, d, p)]
                    need[b] = max(need.get(b, 0), k + 1)
                for b, k in need.items():
                    pe.wait_ge(evac[b], shift(at.it, body.per[b], k))
                return psD[:, own, :]

            def fulls(ins, at, r, step, p):
                ins.then_inc(full[at.bank(r, step, p, 1)[0]], 1)

            def evacs(ins, at, r, step, p):
                ins.then_inc(evac[at.bank(r, step, p, 1)[0]], 1)

            def mlp_result(eng, at, r, p):
                if r:
                    result(eng, at, r - 1, "fc2", p)
                else:
                    for b in range(2):
                        eng.wait_ge(evac[b], shift(at.it, body.per[b], 0))

            def layer(r, second):
                return (r - second) // 2 % DEPTH

            SQUARE = {"varn": "sqn", "varz": "xcz", "var1": "sq1", "var2": "sq2"}
            start(nc, counted)
            blk = st.enter_context(nc.Block())

            @blk.sync
            def _(sp):
                ho_slots = ho_dram.rearrange("(i s) p n -> i s p n", s=4)
                u_slots = u_dram.rearrange("t (i s b) p -> t i s b p", s=4, b=IMG)
                x_next = x[2:].rearrange("(i s) p k n -> i s p k n", s=4)

                def ends(at, r, p):
                    wait(sp, at, "ho", r, ("ho", p))
                    sp.dma_start(ho_slots[bass.ds(at.it, 1), 2 * r + p].rearrange("a p n -> (a p) n"),
                                 ho[p][:, :]).then_inc(ho_out[p], 16)
                    for t, (t0, tn) in enumerate(TILES):
                        if t == 0:
                            wait(sp, at, "u", r, ("u", p))
                        else:
                            result(sp, at, r, "u", p)
                        sp.dma_start(u_slots[t0:t0 + tn, bass.ds(at.it, 1), 2 * r + p].rearrange("t a b p -> t (a b) p"),
                                     usb[p][0:tn, :, t, :]).then_inc(u_out[p], 16)

                for p in range(2):
                    sp.dma_start(patches[p][:, :, :], x[p]).then_inc(patches_in[p], 16)
                with sp.Fori(0, ITERS) as it:
                    at = At(it)
                    for r in range(ROUNDS):
                        if r < 2:
                            for p in range(2):
                                ends(at, r, p)
                            for p in range(2):
                                ready(sp, at, r, "emb", p)
                                sp.dma_start(patches[p][:, :, :],
                                             x_next[bass.ds(it, 1), 2 * r + p].rearrange("a p k n -> (a p) k n")
                                             ).then_inc(patches_in[p], 16)
                        for p in range(2):
                            for j, (step, part) in enumerate((("q", qsp[p]), ("k", ksp[p]))):
                                result(sp, at, r, step, p)
                                sp.dma_start(split_dram[p, j].rearrange("s h d n -> (h d) s n"),
                                             part[:, :, :]).then_inc(split_out[p], 16)
                            wait(sp, at, "split", r, ("k", p))
                            for q, part in enumerate((0, 0, 1, 1)):
                                sp.dma_start(qst[r % 2][p][HD * q:HD * (q + 1), :, :],
                                             split_dram[p, 0, part].rearrange("h d n -> d h n")).then_inc(stacks_in[p], 16)
                            for q, part in enumerate((0, 1, 0, 1)):
                                sp.dma_start(kst[r % 2][p][HD * q:HD * (q + 1), :, :],
                                             split_dram[p, 1, part].rearrange("h d n -> d h n")).then_inc(stacks_in[p], 16)
                        for p in range(2):
                            result(sp, at, r, "neg", p)
                            sp.dma_start(qst[r % 2][p][ONE_ROW:ONE_ROW + 1, :, :], nmT[p][:, :]).then_inc(neg_in[p], 16)
                at = At(ITERS, last=True)
                for r in range(2):
                    for p in range(2):
                        ends(at, r, p)
                for p in range(2):
                    sp.wait_ge(ho_out[p], shift(0, 0, 16 * (PAIRS // 2 + 2)))
                    sp.wait_ge(u_out[p], shift(0, 0, 32 * (PAIRS // 2 + 2)))
                    sp.wait_ge(patches_in[p], shift(0, 0, 16 * (PAIRS // 2 + 1)))

            @blk.tensor
            def _(pe):
                pe.wait_ge(set_up, 23)

                def scores(at, r, kind, p, n):
                    s = r % 2 if kind == "b" else 1 - r % 2
                    m = at.units.index((r, (kind, p, n)))
                    slot = at.slot(r, (kind, p, n))
                    if m >= 2:
                        r0, x0 = at.units[m - 2]
                        wait(pe, at, x0[0], r0, x0)
                    else:
                        pe.wait_ge(max_done, shift(at.it, body_counts["b"][1], 0))
                    if kind == "b":
                        b, t, g = n // 4, n // 2 % 2, n % 2
                        sta, mov, rows = qst[s][p], kst[s][p], ONE_ROW
                    else:
                        b, g, t = n // 4, n // 2 % 2, n % 2
                        sta, mov, rows = kst[s][p], qst[s][p], ONE_ROW + 1
                    t0, tn = TILES[t]
                    for j in range(4):
                        last = pe.matmul(psA[0:tn, slot, j // 2, (j % 2) * TOK:(j % 2 + 1) * TOK],
                                         sta[0:rows, 4 * g + j, b * TOK + t0:b * TOK + t0 + tn],
                                         mov[0:rows, 4 * g + j, b * TOK:(b + 1) * TOK], start=True, stop=True)
                    last.then_inc(keys_full if kind == "b" else probs_full, 1)

                def weighted(at, r, p, n):
                    b, g, s = n // 2, n % 2, 1 - r % 2
                    wait(pe, at, "c", r, ("c", p, 2 * n + 1))
                    if b == 0:
                        wait_before(pe, at, "o", r, ("o", p, g), 2)
                    for t, (t0, tn) in enumerate(TILES):
                        for j in range(4):
                            last = pe.matmul(psO[32 * j:32 * j + 32, g, b * TOK:(b + 1) * TOK],
                                             vals[s][p][0:tn, b, t, 4 * g + j, :], prob[0:tn, (2 * n + t) % 4, j, :],
                                             start=(t == 0), stop=(t == 1))
                    last.then_inc(pv_done, 1)

                def product(at, r, step, p, weights, moving, after=()):
                    ps = free(pe, at, r, step, p, after)
                    for i, (w, m) in enumerate(zip(weights, moving)):
                        last = pe.matmul(ps[:, 0:m.shape[1]], w, m, start=(i == 0), stop=(i == len(weights) - 1))
                    fulls(last, at, r, step, p)

                def by_token(at, r, step, p, weights):
                    ps = free(pe, at, r, step, p)
                    for b in range(IMG):
                        for t, (t0, tn) in enumerate(TILES):
                            last = pe.matmul(ps[0:tn, (2 * b + t) * P:(2 * b + t + 1) * P],
                                             y[p][:, b * TOK + t0:b * TOK + t0 + tn], weights, start=True, stop=True)
                    fulls(last, at, r, step, p)

                def play(at, r, steps):
                    l1, l2 = layer(r, 0), layer(r, 1)
                    for x in steps:
                        step, p = x[0], x[1]
                        if step in ("b", "c"):
                            if x[2] == 0 and step == "b":
                                wait(pe, at, "stacks", r, ("k", p))
                            elif x[2] == 0:
                                wait_round(pe, at, "neg", r, ("neg", p))
                            scores(at, r, step, p, x[2])
                        elif step == "w":
                            weighted(at, r, p, x[2])
                        elif step == "emb":
                            pe.wait_ge(patches_in[p], shift(at.it, 32, 16 * (r + 1)))
                            product(at, r, "emb", p, [conv_s[:, k, :] for k in range(KCH)],
                                    [patches[p][:, k, :] for k in range(KCH)])
                        elif step in SQUARE:
                            wait(pe, at, "sq", r, (SQUARE[step], p))
                            product(at, r, step, p, [mean_s[:, :]], [sq[p][:, :]])
                        elif step == "xcz":
                            wait(pe, at, "ho", r, ("ho", p))
                            product(at, r, "xcz", p, [cen_s[:, :]], [ho[p][:, :]])
                        elif step == "u":
                            wait(pe, at, "y", r, ("yz", p))
                            by_token(at, r, "u", p, win_s[:, :])
                        elif step in ("q", "k"):
                            wait(pe, at, "y", r, ("y1", p))
                            j = "qk".index(step)
                            product(at, r, step, p, [qkv_s[:, l1, j * P:(j + 1) * P]], [y[p][:, :]])
                        elif step == "v":
                            by_token(at, r, "v", p, qkv_s[:, l1, 2 * P:])
                        elif step == "den":
                            wait(pe, at, "o", r, ("o", p, 1))
                            for g in range(2):
                                product(at, r, f"den{g}", p, [gsel_s[:, :]], [osb[p][:, g, :]])
                        elif step == "proj":
                            wait(pe, at, "on", r, ("on", p))
                            product(at, r, "proj", p, [projp_s[:, l2, g, :] for g in range(2)],
                                    [on[p][:, g, :] for g in range(2)])
                        elif step == "fc1":
                            wait(pe, at, "y", r, ("y2", p))
                            for j, d in enumerate(("fc1a", "fc1b")):
                                product(at, r, d, p, [fc1_s[:, l2, j * P:(j + 1) * P]], [y[p][:, :]])
                        elif step == "neg":
                            wait(pe, at, "b", r, ("b", p, 7))
                            ps = free(pe, at, r, "neg", p)
                            for b in range(IMG):
                                for t, (t0, tn) in enumerate(TILES):
                                    c0 = b * TOK + t0
                                    last = pe.matmul(ps[0:HEADS, c0:c0 + tn], nmax[p][0:tn, b, t, :], idh_s[0:tn, 0:tn],
                                                     start=True, stop=True)
                            fulls(last, at, r, "neg", p)
                        elif step == "fc2":
                            product(at, r, "fc2", p, [fc2_s[:, l2, j, :] for j in range(2)],
                                    [gl[p][:, j, :] for j in range(2)], ("fc1a", "fc1b"))

                with pe.Fori(0, ITERS) as it:
                    for r in range(ROUNDS):
                        play(At(it), r, ORDER_END if r < 2 else ORDER)
                at = At(ITERS, last=True)
                play(at, 0, LAST_0)
                play(at, 1, LAST_1)

            @blk.scalar
            def _(act):
                act.preload_act_table_set(NORM_SET)
                act.wait_ge(set_up, 23)

                def square(p, source):
                    act.activation(sq[p][:, :], source, ACT.Square).then_inc(sq_done, 1)

                def inverse(at, r, step, p):
                    ps = ready(act, at, r, step, p)
                    evacs(act.activation(lnv[p][:, :], ps[:, 0:N], ACT.Ln, bias=eps_s[:, 0:1]), at, r, step, p)
                    result(act, at, r, step, p)
                    act.activation(rstd[p][:, :], lnv[p][:, :], ACT.Exp, scale=-0.5).then_inc(rstd_done, 1)

                def play(at, r, steps):
                    s, l1, l2 = r % 2, layer(r, 0), layer(r, 1)
                    for x in steps:
                        step, p = x[0], x[1]
                        if step == "c":
                            n = x[2]
                            tn = TILES[n % 2][1]
                            act.wait_ge(probs_full, shift(at.it, body_counts["c"][1], at.counts["c"][0][(r, x)]))
                            wait_before(act, at, "w", r, ("w", p, n // 2), 2)
                            act.activation(prob[0:tn, n % 4, :, :].rearrange("p (a c) n -> p a c n", c=2),
                                           psA[0:tn, at.slot(r, x), :, 0:2 * TOK].rearrange("p a (c n) -> p a c n", c=2),
                                           ACT.Exp).then_inc(exp_done, 1)
                        elif step == "sqn":
                            mlp_result(act, at, r, p)
                            square(p, h[s][p][:, :])
                        elif step == "xcz":
                            result(act, at, r, "xcz", p)
                            square(p, y[p][:, :])
                        elif step == "sq1":
                            if r < 2:
                                result(act, at, r, "emb", p)
                                wait(act, at, "cls", r, ("emb", p))
                            else:
                                mlp_result(act, at, r, p)
                            square(p, h[s][p][:, :])
                        elif step == "sq2":
                            result(act, at, r, "proj", p)
                            square(p, h[1 - s][p][:, :])
                        elif step in SQUARE:
                            inverse(at, r, step, p)
                        elif step in ("q", "k"):
                            j = "qk".index(step)
                            ps = ready(act, at, r, step, p)
                            wait_before(act, at, "split", r, ("k", p))
                            act.activation((qsp, ksp)[j][p][:, 0, :], ps[:, 0:N], ACT.Identity,
                                           bias=bias_s[:, l1, j:j + 1]).then_inc(hi_done, 1)
                        elif step == "den":
                            for g in range(2):
                                ps = ready(act, at, r, f"den{g}", p)
                                evacs(act.activation(lden[p][:, g, :], ps[:, 0:N], ACT.Ln), at, r, f"den{g}", p)
                            for g in range(2):
                                result(act, at, r, f"den{g}", p)
                                act.activation(rden[p][:, g, :], lden[p][:, g, :], ACT.Exp,
                                               scale=-1.0).then_inc(rden_done, 1)
                        elif step == "neg":
                            ps = ready(act, at, r, "neg", p)
                            wait_before(act, at, "neg", r, ("neg", p))
                            evacs(act.activation(nmT[p][:, :], ps[0:HEADS, 0:N], ACT.Copy), at, r, "neg", p)
                        elif step == "gelu":
                            for j, d in enumerate(("fc1a", "fc1b")):
                                ps = ready(act, at, r, d, p)
                                evacs(act.activation(gl[p][:, j, :], ps[:, 0:N], ACT.Gelu, bias=bias_s[:, l2, 3 + j:4 + j]),
                                      at, r, d, p)
                            if p == 1:
                                act.preload_act_table_set(NORM_SET)

                with act.Fori(0, ITERS) as it:
                    for r in range(ROUNDS):
                        play(At(it), r, ORDER_END if r < 2 else ORDER)
                at = At(ITERS, last=True)
                play(at, 0, LAST_0)
                play(at, 1, LAST_1)

            @blk.vector
            def _(dve):
                for s in range(2):
                    for p in range(2):
                        dve.memset(h[s][p][:, :], 0.0).then_inc(set_up, 1)
                        dve.memset(qst[s][p][:, :, :], 0.0).then_inc(set_up, 1)
                        dve.memset(kst[s][p][:, :, :], 0.0).then_inc(set_up, 1)
                        dve.memset(vals[s][p][:, :, :, :, :], 1.0).then_inc(set_up, 1)
                dve.wait_ge(set_up, 16)
                for s in range(2):
                    for p in range(2):
                        dve.memset(kst[s][p][ONE_ROW:ONE_ROW + 1, :, :], 1.0).then_inc(set_up, 1)
                for p in range(2):
                    dve.memset(nmax[p][:, :, :, :], 0.0).then_inc(set_up, 1)
                dve.tensor_copy(idh_s[:, :], id_s[:, :]).then_inc(set_up, 1)
                dve.wait_ge(set_up, 23)

                def scaled(at, r, step, p, source):
                    wait(dve, at, "rstd", r, ({"ho": "varn", "yz": "varz", "y1": "var1", "y2": "var2"}[step], p))
                    dve.tensor_tensor(y[p][:, :], source, rstd[p][:, :], ALU.mult).then_inc(y_done, 1)

                def add_to_h(at, r, s, step, p, bias):
                    ps = ready(dve, at, r, step, p)
                    evacs(dve.scalar_tensor_tensor(out=h[s][p][:, :], in0=ps[:, 0:N], scalar=bias, in1=h[s][p][:, :],
                                                   op0=ALU.add, op1=ALU.add), at, r, step, p)

                def play(at, r, steps):
                    s, l1, l2 = r % 2, layer(r, 0), layer(r, 1)
                    for x in steps:
                        step, p = x[0], x[1]
                        if step == "b":
                            n = x[2]
                            b, t, g = n // 4, n // 2 % 2, n % 2
                            tn = TILES[t][1]
                            dve.wait_ge(keys_full, shift(at.it, body_counts["b"][1], at.counts["b"][0][(r, x)]))
                            dve.tensor_reduce(nmax[p][0:tn, b, t, 4 * g:4 * g + 4].rearrange("p (a c) -> p a c", c=2),
                                              psA[0:tn, at.slot(r, x), :, 0:2 * TOK].rearrange("p a (c n) -> p a c n", c=2),
                                              AX_X, ALU.max, negate=True).then_inc(max_done, 1)
                        elif step == "o":
                            g = x[2]
                            wait(dve, at, "w", r, ("w", p, g + 2))
                            dve.tensor_copy(osb[p][:, g, :], psO[:, g, 0:N]).then_inc(o_copied, 1)
                        elif step == "emb":
                            ps = ready(dve, at, r, "emb", p)
                            hv = h[s][p][:, :].rearrange("p (b t) -> p b t", b=IMG)
                            for b in range(IMG):
                                last = dve.tensor_copy(hv[:, b, 0:1], pos_s[:, 0:1])
                            last.then_inc(cls_done, 1)
                            for b in range(IMG):
                                last = dve.tensor_tensor(hv[:, b, 1:TOK], ps[:, b * PATCH:(b + 1) * PATCH],
                                                         pos_s[:, 1:TOK], ALU.add)
                            evacs(last, at, r, "emb", p)
                        elif step == "ho":
                            mlp_result(dve, at, r, p)
                            scaled(at, r, "ho", p, h[s][p][:, :])
                            wait(dve, at, "y", r, ("ho", p))
                            wait_before(dve, at, "ho_out", r, ("ho", p))
                            dve.tensor_scalar(ho[p][:, :], y[p][:, :], normwb_s[:, 0:1], normwb_s[:, 1:2], ALU.mult,
                                              ALU.add).then_inc(ho_done, 1)
                        elif step == "xcz":
                            ps = ready(dve, at, r, "xcz", p)
                            evacs(dve.tensor_copy(y[p][:, :], ps[:, 0:N]), at, r, "xcz", p)
                        elif step == "yz":
                            scaled(at, r, "yz", p, y[p][:, :])
                        elif step == "u":
                            ps = ready(dve, at, r, "u", p)
                            wait_before(dve, at, "u_out", r, ("u", p))
                            pv = ps.rearrange("p (b t d) -> p b t d", b=IMG, t=2)
                            for t, (t0, tn) in enumerate(TILES):
                                for b in range(IMG):
                                    last = dve.tensor_tensor(usb[p][0:tn, b, t, :], pv[0:tn, b, t, :], binb_s[0:tn, :],
                                                             ALU.add)
                                if t == 0:
                                    last.then_inc(u_parts, 1)
                            evacs(last, at, r, "u", p)
                        elif step == "y1":
                            scaled(at, r, "y1", p, h[s][p][:, :])
                        elif step == "y2":
                            scaled(at, r, "y2", p, h[1 - s][p][:, :])
                        elif step in ("q", "k"):
                            j = "qk".index(step)
                            ps = ready(dve, at, r, step, p)
                            part = (qsp, ksp)[j][p]
                            wait(dve, at, "hi", r, x)
                            evacs(dve.scalar_tensor_tensor(out=part[:, 1, :], in0=ps[:, 0:N], scalar=bias_s[:, l1, j:j + 1],
                                                           in1=part[:, 0, :], op0=ALU.add, op1=ALU.subtract),
                                  at, r, step, p)
                        elif step == "v":
                            pv = ready(dve, at, r, "v", p).rearrange("p (b t h d) -> p b t h d", b=IMG, t=2, h=HEADS)
                            for t, (t0, tn) in enumerate(TILES):
                                for b in range(IMG):
                                    last = dve.tensor_copy(vals[s][p][0:tn, b, t, :, 0:HD], pv[0:tn, b, t, :, :])
                                if t == 0:
                                    last.then_inc(v_parts, 1)
                            evacs(last, at, r, "v", p)
                        elif step == "on":
                            wait(dve, at, "rden", r, ("den", p))
                            dve.tensor_tensor(on[p][:, :, :], osb[p][:, :, :], rden[p][:, :, :],
                                              ALU.mult).then_inc(on_done, 1)
                        elif step == "proj":
                            add_to_h(at, r, 1 - s, "proj", p, bias_s[:, l2, 5:6])
                        elif step == "fc2":
                            add_to_h(at, r, 1 - s, "fc2", p, fc2b_s[:, l2:l2 + 1])

                with dve.Fori(0, ITERS) as it:
                    for r in range(ROUNDS):
                        play(At(it), r, ORDER_END if r < 2 else ORDER)
                at = At(ITERS, last=True)
                play(at, 0, LAST_0)
                play(at, 1, LAST_1)

        with ExitStack() as st:
            def ssb(name, shape, dt=F32):
                return st.enter_context(nc.sbuf_tensor(name, shape, dt))

            counted = []

            def ssem(name):
                counted.append(st.enter_context(nc.semaphore(name)))
                return counted[-1]

            toep = [ssb(f"toep{t}", [tn, CHUNKS, TOK]) for t, (t0, tn) in enumerate(TILES)]
            uin = [ssb(f"uin{t}", [tn, GRP, P]) for t, (t0, tn) in enumerate(TILES)]
            yout = [ssb(f"yout{t}", [tn, GRP, P]) for t, (t0, tn) in enumerate(TILES)]
            toep_in = st.enter_context(nc.semaphore("toep_in"))
            uin_in = ssem("uin_in")
            conv_full = ssem("conv_full")
            conv_act = ssem("conv_act")
            conv_dve = ssem("conv_dve")
            yout_out = ssem("yout_out")
            CB = 4
            STEPS = 2 * CHUNKS // CB
            start(nc, counted)
            blk = st.enter_context(nc.Block())

            @blk.sync
            def _(sp):
                for t, (t0, tn) in enumerate(TILES):
                    g0 = gen_dram[:, :]
                    src = bass.AP(tensor=g0.tensor, offset=t0, ap=[[1, tn], [GEN, CHUNKS], [1, TOK]])
                    sp.dma_start(toep[t][:, :, :], src).then_inc(toep_in, 16)
                with sp.Fori(0, GROUPS) as it:
                    sp.wait_ge(conv_full, shift(it, STEPS, 0))
                    for t, (t0, tn) in enumerate(TILES):
                        sp.dma_start(uin[t][:, :, :], u_dram[t0:t0 + tn, bass.ds(GRP * it + 4 * IMG, GRP), :]).then_inc(uin_in, 16)
                    for t, (t0, tn) in enumerate(TILES):
                        sp.wait_ge(conv_act, shift(it, STEPS // 2, STEPS // 4 * (t + 1)))
                        sp.wait_ge(conv_dve, shift(it, STEPS // 2, STEPS // 4 * (t + 1)))
                        sp.dma_start(y_dram[t0:t0 + tn, bass.ds(GRP * it, GRP), :], yout[t][:, :, :]).then_inc(yout_out, 16)
                sp.wait_ge(yout_out, shift(GROUPS, 32, 0))

            @blk.tensor
            def _(pe):
                pe.wait_ge(toep_in, 32)
                with pe.Fori(0, GROUPS) as it:
                    pe.wait_ge(uin_in, shift(it, 32, 32))
                    for n in range(STEPS):
                        t, c0 = n // (STEPS // 2), n % (STEPS // 2) * CB
                        t0, tn = TILES[t]
                        pe.wait_ge((conv_act, conv_dve)[n % 2], shift(it, STEPS // 2, n // 2))
                        for c in range(CB):
                            for s, (s0, sn) in enumerate(TILES):
                                last = pe.matmul(psD[0:tn, n % 2, c * GRP * CW:(c + 1) * GRP * CW],
                                                 toep[s][:, c0 + c, t0:t0 + tn],
                                                 uin[s][:, :, CW * (c0 + c):CW * (c0 + c + 1)],
                                                 start=(s == 0), stop=(s == 1))
                        last.then_inc(conv_full, 1)

            def conv_view(n):
                t, c0 = n // (STEPS // 2), n % (STEPS // 2) * CB
                tn = TILES[t][1]
                dst = yout[t][:, :, CW * c0:CW * (c0 + CB)].rearrange("p b (c r) -> p c b r", c=CB)
                src = psD[0:tn, n % 2, 0:CB * GRP * CW].rearrange("p (c b r) -> p c b r", c=CB, r=CW)
                return dst, src

            @blk.scalar
            def _(act):
                with act.Fori(0, GROUPS) as it:
                    act.wait_ge(yout_out, shift(it, 32, 0))
                    for n in range(0, STEPS, 2):
                        dst, src = conv_view(n)
                        act.wait_ge(conv_full, shift(it, STEPS, n + 1))
                        act.activation(dst, src, ACT.Copy).then_inc(conv_act, 1)

            @blk.vector
            def _(dve):
                with dve.Fori(0, GROUPS) as it:
                    dve.wait_ge(yout_out, shift(it, 32, 0))
                    for n in range(1, STEPS, 2):
                        dst, src = conv_view(n)
                        dve.wait_ge(conv_full, shift(it, STEPS, n + 1))
                        dve.tensor_copy(dst, src).then_inc(conv_dve, 1)

        with ExitStack() as st:
            def ssb(name, shape, dt=F32):
                return st.enter_context(nc.sbuf_tensor(name, shape, dt))

            counted = []

            def ssem(name):
                counted.append(st.enter_context(nc.semaphore(name)))
                return counted[-1]

            def two(name, shape, dt=F32):
                return [ssb(f"{name}_{q}", shape, dt) for q in range(2)]

            w1_s = ssb("w1_s", [P, EXPERTS, 2 * P])
            w2_s = ssb("w2_s", [P, EXPERTS, 2, P])
            b2_s = ssb("b2_s", [EXPERTS, P])
            wg_s = ssb("wg_s", [P, EXPERTS])
            bgb_s = ssb("bgb_s", [P, EXPERTS])
            esel_s = ssb("esel_s", [EXPERTS, EXPERTS, P])
            closed = ssb("closed", [EXPERTS, EXPERTS, P], BF16)
            rank_s = ssb("rank_s", [P, EXPERTS])
            anti_s = ssb("anti_s", [P, P])
            yin = two("yin", [P, IMG, 2, P])
            hoin = two("hoin", [P, N])
            yT = two("yT", [P, N])
            gel = two("gel", [P, N])
            h2 = two("h2", [P, N])
            sq = two("sq3", [P, N])
            lnv = two("lnv3", [P, N])
            rstd = two("rstd3", [P, N])
            h3 = two("h3", [P, N])
            logit = two("logit", [P, 2 * IMG, EXPERTS])
            top = two("top", [P, 2 * IMG])
            cand = two("cand", [P, 2 * IMG, EXPERTS])
            first = two("first", [P, 2 * IMG])
            hot = two("hot", [P, 2 * IMG, EXPERTS])
            hotT = two("hotT", [EXPERTS, N])
            hotb = two("hotb", [EXPERTS, N], BF16)
            hid = ssb("hid", [P, 4, N])
            h4 = two("h4", [P, N])
            yf = two("yf", [P, N])
            osb3 = two("osb3", [P, IMG, 2, P])

            w_in = st.enter_context(nc.semaphore("w_in"))
            closed_done = st.enter_context(nc.semaphore("closed_done"))
            full = [ssem(f"tail_full{b}") for b in range(4)]
            evac = [ssem(f"tail_evac{b}") for b in range(4)]
            rows_in = [ssem(f"rows_in{q}") for q in range(2)]
            out_done = [ssem(f"out_done{q}") for q in range(2)]
            h2_done = ssem("h2_done")
            sq_done = ssem("sq3_done")
            rstd_done = ssem("rstd3_done")
            route = ssem("route")
            w2_done = ssem("w2_done")
            moe_full = ssem("moe_full")
            h4_done = ssem("h4_done")
            back_part = ssem("back_part")
            sems = {"h2": h2_done, "sq": sq_done, "rstd": rstd_done, "route": route, "w2": w2_done,
                    "moe": moe_full, "h4": h4_done, "back": back_part,
                    "rows0": rows_in[0], "rows1": rows_in[1], "out0": out_done[0], "out1": out_done[1]}
            wl = [(w1_s, w1), (w2_s, w2), (b2_s, b2), (wg_s, wg), (bgb_s, bgb), (esel_s, esel), (rank_s, rank), (anti_s, anti)]
            ITERS = PAIRS // 2 - 1
            banks = [psD[:, 0, :], psD[:, 1, :], psA[:, 0, 0, :], psA[:, 1, 0, :]]
            tail_counts = [tail_count(part) for part in (TAIL_FIRST, TAIL_BODY, TAIL_LAST)]

            class Part:

                def __init__(self, part, it):
                    self.counts, self.part, self.it = tail_counts[part], part, it

                def value(self, name, x, more=0):
                    k = self.counts[name][0][x] + more
                    if self.part == 0:
                        return shift(0, 0, k)
                    return shift(self.it, tail_counts[1][name][1], tail_counts[0][name][1] + k)

            def wait(eng, at, name, x, more=0):
                eng.wait_ge(sems[name], at.value(name, x, more))

            def ready(eng, at, x):
                b = TAIL_BANK[x]
                eng.wait_ge(full[b], at.value(b, x))
                return banks[b]

            def result(eng, at, x):
                b = TAIL_BANK[x]
                eng.wait_ge(evac[b], at.value(b, x))

            def free(pe, at, x):
                b = TAIL_BANK[x]
                pe.wait_ge(evac[b], at.value(b, x, -1))
                return banks[b]

            def fulls(ins, x):
                ins.then_inc(full[TAIL_BANK[x]], 1)

            def evacs(ins, x):
                ins.then_inc(evac[TAIL_BANK[x]], 1)

            FULL = ((0, 128), (LAST0, 128))
            start(nc, counted)
            blk = st.enter_context(nc.Block())

            @blk.sync
            def _(sp):
                for t, src in wl:
                    sp.dma_start(t[:], src).then_inc(w_in, 16)
                y_pairs = y_dram.rearrange("t (i s b) p -> t i s b p", s=2, b=IMG)
                ho_pairs = ho_dram.rearrange("(i s) p n -> i s p n", s=2)

                def load(q, y_rows, ho_rows):
                    for t, (t0, tn) in enumerate(TILES):
                        sp.dma_start(yin[q][0:tn, :, t, :],
                                     y_rows[t0:t0 + tn].rearrange("t a b p -> t (a b) p")).then_inc(rows_in[q], 16)
                    sp.dma_start(hoin[q][:, :], ho_rows.rearrange("a p n -> (a p) n")).then_inc(rows_in[q], 16)

                def store(at, q, out_rows):
                    for t, (t0, tn) in enumerate(TILES):
                        if t == 0:
                            wait(sp, at, "back", ("back", q))
                        else:
                            result(sp, at, ("back", q))
                        sp.dma_start(out_rows[:, t0:t0 + tn].rearrange("b t d -> t b d"),
                                     osb3[q][0:tn, :, t, :]).then_inc(out_done[q], 16)

                for q in range(2):
                    load(q, y_pairs[:, 0:1, q], ho_pairs[2:3, q])
                y_next, ho_next = y_pairs[:, 1:], ho_pairs[3:]
                with sp.Fori(0, ITERS) as it:
                    at = Part(1, it)
                    for q in range(2):
                        wait(sp, at, "h2", ("h2", q), -1)
                        load(q, y_next[:, bass.ds(it, 1), q], ho_next[bass.ds(it, 1), q])
                        store(at, q, out[bass.ds(2 * IMG * it + IMG * q, IMG)])
                at = Part(2, ITERS)
                for q in range(2):
                    store(at, q, out[2 * IMG * ITERS + IMG * q:2 * IMG * ITERS + IMG * (q + 1)])
                for q in range(2):
                    sp.wait_ge(out_done[q], shift(0, 0, 16 * PAIRS))

            @blk.tensor
            def _(pe):
                pe.wait_ge(w_in, 16 * len(wl))
                pe.wait_ge(closed_done, 1)

                def product(at, x, weights, moving):
                    fulls(pe.matmul(free(pe, at, x)[:, 0:N], weights, moving, start=True, stop=True), x)

                def play(at, steps):
                    for x in steps:
                        step, q = x[0], x[1]
                        if step == "yT":
                            pe.wait_ge(rows_in[q], at.value(f"rows{q}", x))
                            ps = free(pe, at, x)
                            for b in range(IMG):
                                for t, (t0, tn) in enumerate(TILES):
                                    c0 = (b + 1) * TOK - t0 - tn
                                    last = pe.matmul(ps[:, c0:c0 + tn], yin[q][0:tn, b, t, :], anti_s[0:tn, P - tn:P],
                                                     start=True, stop=True)
                            fulls(last, x)
                        elif step == "out":
                            result(pe, at, ("yT", q))
                            product(at, x, wout_s[:, :], yT[q][:, :])
                        elif step == "xc":
                            wait(pe, at, "h2", ("h2", q))
                            product(at, x, cen_s[:, :], h2[q][:, :])
                        elif step == "xcf":
                            wait(pe, at, "h4", ("h4", q))
                            product(at, x, cen_s[:, :], h4[q][:, :])
                        elif step in ("var", "varf"):
                            wait(pe, at, "sq", (("xc", "xcf")[step == "varf"], q))
                            product(at, x, mean_s[:, :], sq[q][:, :])
                        elif step == "logit":
                            result(pe, at, ("xc", q))
                            ps = free(pe, at, x)
                            for b in range(IMG):
                                for t, (t0, tn) in enumerate(FULL):
                                    c0 = b * TOK + t0
                                    last = pe.matmul(ps[:, (2 * b + t) * EXPERTS:(2 * b + t + 1) * EXPERTS],
                                                     h3[q][:, c0:c0 + tn], wg_s[:, :], start=True, stop=True)
                            fulls(last, x)
                        elif step == "hotT":
                            wait(pe, at, "route", ("route", q))
                            ps = free(pe, at, x)
                            for b in range(IMG):
                                for t, (t0, tn) in enumerate(FULL):
                                    c0 = b * TOK + t0
                                    last = pe.matmul(ps[0:EXPERTS, c0:c0 + tn], hot[q][:, 2 * b + t, :], id_s[:, :],
                                                     start=True, stop=True)
                            fulls(last, x)
                        elif step == "exp":
                            e, j = x[2] // 2, x[2] % 2
                            if x[2] == 0:
                                b = TAIL_BANK[("hotT", q)]
                                pe.wait_ge(evac[b], at.value(b, ("half", q)))
                            ps = free(pe, at, x)
                            pe.matmul(ps[:, 0:N], w1_s[:, e, j * P:(j + 1) * P], h3[q][:, :], start=True, stop=False)
                            fulls(pe.matmul(ps[:, 0:N], closed[:, e, :], hotb[q][:, :], start=False, stop=True), x)
                        elif step == "w2":
                            n = x[2]
                            if n == 0:
                                wait(pe, at, "h4", ("half", q))
                            result(pe, at, ("exp", q, n))
                            pe.matmul(psO[:, q, 0:N], w2_s[:, n // 2, n % 2, :], hid[:, n % 4, :], start=(n == 0),
                                      stop=False).then_inc(w2_done, 1)
                        elif step == "b2":
                            pe.matmul(psO[:, q, 0:N], b2_s[:, :], hotT[q][:, :], start=False,
                                      stop=True).then_inc(moe_full, 1)
                        elif step == "back":
                            result(pe, at, ("xcf", q))
                            ps = free(pe, at, x)
                            for b in range(IMG):
                                for t, (t0, tn) in enumerate(TILES):
                                    c0 = b * TOK + t0
                                    last = pe.matmul(ps[0:tn, (2 * b + t) * P:(2 * b + t + 1) * P],
                                                     yf[q][:, c0:c0 + tn], id_s[:, :], start=True, stop=True)
                            fulls(last, x)

                play(Part(0, 0), TAIL_FIRST)
                with pe.Fori(0, ITERS) as it:
                    play(Part(1, it), TAIL_BODY)
                play(Part(2, ITERS), TAIL_LAST)

            @blk.scalar
            def _(act):
                act.wait_ge(w_in, 16 * len(wl))
                act.preload_act_table_set(NORM_SET)

                def play(at, steps):
                    for x in steps:
                        step, q = x[0], x[1]
                        if step == "out":
                            evacs(act.activation(gel[q][:, :], ready(act, at, x)[:, 0:N], ACT.Gelu,
                                                 bias=boutc_s[:, 0:1]), x)
                            act.preload_act_table_set(NORM_SET)
                        elif step in ("xc", "xcf"):
                            act.activation(sq[q][:, :], ready(act, at, x)[:, 0:N], ACT.Square).then_inc(sq_done, 1)
                        elif step in ("var", "varf"):
                            evacs(act.activation(lnv[q][:, :], ready(act, at, x)[:, 0:N], ACT.Ln, bias=eps_s[:, 0:1]), x)
                            result(act, at, x)
                            act.activation(rstd[q][:, :], lnv[q][:, :], ACT.Exp, scale=-0.5).then_inc(rstd_done, 1)
                        elif step == "exp" and x[2] % 2 == 0:
                            n = x[2]
                            ps = ready(act, at, x)
                            wait(act, at, "w2", ("w2", q, 0), max(n - 3, 0) - 1)
                            evacs(act.activation(hid[:, n % 4, :], ps[:, 0:N], ACT.Relu, bias=b1c_s[:, n:n + 1]), x)

                play(Part(0, 0), TAIL_FIRST)
                with act.Fori(0, ITERS) as it:
                    play(Part(1, it), TAIL_BODY)
                play(Part(2, ITERS), TAIL_LAST)

            @blk.vector
            def _(dve):
                dve.wait_ge(w_in, 16 * len(wl))
                dve.tensor_scalar(closed[:, :, :], esel_s[:, :, :], NEG, None, ALU.mult).then_inc(closed_done, 1)
                dve.wait_ge(closed_done, 1)

                def play(at, steps):
                    for x in steps:
                        step, q = x[0], x[1]
                        if step == "yT":
                            evacs(dve.tensor_copy(yT[q][:, :], ready(dve, at, x)[:, 0:N]), x)
                        elif step == "h2":
                            result(dve, at, ("out", q))
                            dve.scalar_tensor_tensor(out=h2[q][:, :], in0=hoin[q][:, :], scalar=2.0, in1=gel[q][:, :],
                                                     op0=ALU.mult, op1=ALU.add).then_inc(h2_done, 1)
                        elif step == "h3":
                            wait(dve, at, "rstd", ("var", q))
                            evacs(dve.tensor_tensor(h3[q][:, :], ready(dve, at, ("xc", q))[:, 0:N], rstd[q][:, :],
                                                    ALU.mult), ("xc", q))
                        elif step == "route":
                            ps = ready(dve, at, ("logit", q))
                            lg, tp, cd, fi = logit[q][:, :, :], top[q][:, :], cand[q][:, :, :], first[q][:, :]
                            sh = [P, 2 * IMG, EXPERTS]
                            evacs(dve.tensor_tensor(lg, ps[:, 0:2 * IMG * EXPERTS].rearrange("p (t e) -> p t e", e=EXPERTS),
                                                    bgb_s[:, :].unsqueeze(1).to_broadcast(sh), ALU.add), ("logit", q))
                            result(dve, at, ("logit", q))
                            dve.tensor_reduce(tp, lg, AX_X, ALU.max).then_inc(route, 1)
                            wait(dve, at, "route", x, -4)
                            dve.tensor_tensor(cd, lg, tp.unsqueeze(2).to_broadcast(sh), ALU.is_equal).then_inc(route, 1)
                            wait(dve, at, "route", x, -3)
                            dve.tensor_tensor(cd, cd, rank_s[:, :].unsqueeze(1).to_broadcast(sh), ALU.mult).then_inc(route, 1)
                            wait(dve, at, "route", x, -2)
                            dve.tensor_reduce(fi, cd, AX_X, ALU.max).then_inc(route, 1)
                            wait(dve, at, "route", x, -1)
                            dve.tensor_tensor(hot[q][:, :, :], cd, fi.unsqueeze(2).to_broadcast(sh),
                                              ALU.is_equal).then_inc(route, 1)
                        elif step == "hotT":
                            ps = ready(dve, at, x)
                            dve.tensor_copy(hotb[q][:, :], ps[0:EXPERTS, 0:N])
                            evacs(dve.tensor_copy(hotT[q][:, :], ps[0:EXPERTS, 0:N]), x)
                        elif step == "exp" and x[2] % 2 == 1:
                            n = x[2]
                            ps = ready(dve, at, x)
                            wait(dve, at, "w2", ("w2", q, 0), max(n - 3, 0) - 1)
                            evacs(dve.tensor_scalar(hid[:, n % 4, :], ps[:, 0:N], b1c_s[:, n:n + 1], 0.0, ALU.add,
                                                    ALU.max), x)
                        elif step == "h4":
                            wait(dve, at, "moe", ("half", 1 - q))
                            dve.tensor_tensor(h4[q][:, :], psO[:, q, 0:N], h3[q][:, :], ALU.add).then_inc(h4_done, 1)
                        elif step == "yf":
                            wait(dve, at, "rstd", ("varf", q))
                            evacs(dve.tensor_tensor(yf[q][:, :], ready(dve, at, ("xcf", q))[:, 0:N], rstd[q][:, :],
                                                    ALU.mult), ("xcf", q))
                        elif step == "back":
                            ps = ready(dve, at, x)
                            dve.wait_ge(out_done[q], at.value(f"out{q}", x, -32))
                            pv = ps.rearrange("p (b t d) -> p b t d", b=IMG, t=2)
                            for t, (t0, tn) in enumerate(TILES):
                                for b in range(IMG):
                                    last = dve.tensor_copy(osb3[q][0:tn, b, t, :], pv[0:tn, b, t, :])
                                if t == 0:
                                    last.then_inc(back_part, 1)
                            evacs(last, x)

                play(Part(0, 0), TAIL_FIRST)
                with dve.Fori(0, ITERS) as it:
                    play(Part(1, it), TAIL_BODY)
                play(Part(2, ITERS), TAIL_LAST)

TURNS = 0.15915494309189535
MAGIC = 12582912.0
PI2 = (6.28125, 0.0019350051879882812, 3.0199159819567e-07)
PI_BELOW = 3.1415925

_INS = ["x", "conv", "convb", "clsc", "posT", "qkv", "qkvb", "projp", "projn", "projb", "ln1", "fc1", "fc1b", "fc2",
        "fc2b", "ln2", "normwb", "attg", "win", "binb", "wout", "boutc", "lre", "lim", "bm", "cre", "cim", "dvec",
        "w1", "b1c", "w2", "b2", "wg", "bgb", "om", "ident", "cen", "mean", "gsel", "esel", "rank", "anti"]


def layouts(i, np):
    L, D = DEPTH, P
    v = {k.replace("L0_", ""): np.asarray(a) for k, a in i.items()}
    a = {}
    x = v["x"]
    b = x.shape[0]
    xp = x.reshape(b // 2, 2, 3, 14, 16, 14, 16).transpose(0, 2, 4, 6, 1, 3, 5).reshape(b // 2, KCH, D, 2 * PATCH)
    xp = xp.transpose(0, 2, 1, 3)
    a["x"] = np.concatenate([xp, xp[:2]], axis=0)
    a["conv"] = v["tok_conv_w"].reshape(KCH, D, D).transpose(1, 0, 2)
    a["convb"] = v["tok_conv_b"][:, None]
    a["clsc"] = v["tok_cls_token"].reshape(D, 1)
    a["posT"] = v["tok_pos_embed"][0].T
    a["qkv"] = v["tok_qkv_w"].transpose(1, 0, 2)
    a["qkvb"] = v["tok_qkv_b"].reshape(L * 3, D).T
    pj = v["tok_proj_w"]
    pp = np.zeros((L, 2, 4, 32, D), pj.dtype)
    pp[:, :, :, :HD] = pj.reshape(L, 2, 4, HD, D)
    a["projp"] = pp.reshape(L, 2, D, D).transpose(2, 0, 1, 3)
    a["projn"] = pj.transpose(1, 0, 2)
    a["projb"] = v["tok_proj_b"].T
    a["ln1"] = np.concatenate([v["tok_ln1_w"], v["tok_ln1_b"]]).T
    a["ln2"] = np.concatenate([v["tok_ln2_w"], v["tok_ln2_b"]]).T
    a["fc1"] = v["tok_fc1_w"].transpose(1, 0, 2)
    a["fc1b"] = v["tok_fc1_b"].reshape(L * 2, D).T
    a["fc2"] = v["tok_fc2_w"].reshape(L, 2, D, D).transpose(2, 0, 1, 3)
    a["fc2b"] = v["tok_fc2_b"].T
    a["normwb"] = np.stack([v["tok_norm_w"], v["tok_norm_b"]], 1)
    a["attg"] = np.stack([v["attn_ln_gamma"], v["attn_ln_beta"]], 1)
    a["win"] = v["attn_Win"]
    a["binb"] = np.broadcast_to(v["attn_bin_"], (D, D))
    a["wout"] = v["attn_Wout"]
    a["boutc"] = v["attn_bout"][:, None]
    for n, k in (("lre", "attn_Lambda_re"), ("lim", "attn_Lambda_im"), ("bm", "attn_Bmat"), ("cre", "attn_C_re"),
                 ("cim", "attn_C_im")):
        a[n] = v[k].reshape(CG, D).T
    a["dvec"] = v["attn_Dvec"][:, None]
    a["w1"] = v["ffn_W1"].transpose(1, 0, 2)
    a["b1c"] = v["ffn_b1"].reshape(2 * EXPERTS, D).T
    a["w2"] = v["ffn_W2"].reshape(EXPERTS, 2, D, D).transpose(2, 0, 1, 3)
    a["b2"] = v["ffn_b2"]
    a["wg"] = v["ffn_Wg"]
    a["bgb"] = np.broadcast_to(v["ffn_bg"], (D, EXPERTS))
    f = np.float32
    j = (TOK - 1) - np.arange(GEN)
    a["om"] = np.broadcast_to(np.where(j >= 0, j, -j - 1).astype(f), (D, GEN))
    a["ident"] = np.eye(D, dtype=f)
    a["anti"] = np.eye(D, dtype=f)[::-1]
    a["cen"] = (np.eye(D) - 1.0 / D).astype(f)
    a["mean"] = np.full((D, D), 1.0 / D, f)
    r = np.arange(D)
    a["gsel"] = (r[:, None] == (r // 32 * 32 + HD)[None, :]).astype(f)
    a["esel"] = np.broadcast_to((1 - np.eye(EXPERTS))[:, :, None], (EXPERTS, EXPERTS, D)).astype(f)
    a["rank"] = np.broadcast_to(np.arange(EXPERTS, 0, -1).astype(f), (D, EXPERTS))
    return {k: np.ascontiguousarray(a[k]) for k in _INS}


def kernel(**inputs):
    import numpy as np
    import concourse.bacc as bacc
    from concourse.bass_utils import run_bass_kernel_spmd

    arrays = layouts(inputs, np)
    batch = inputs["x"].shape[0]
    nc = bacc.Bacc("TRN2", target_bir_lowering=False, num_devices=1)
    args = {k: nc.dram_tensor(k, a.shape, mybir.dt.from_np(a.dtype), kind="ExternalInput").ap()
            for k, a in arrays.items()}
    args["out"] = nc.dram_tensor("out", (batch, TOK, P), F32, kind="ExternalOutput").ap()
    build(nc, **args)
    r = run_bass_kernel_spmd(nc, [arrays], core_ids=[0])
    return r.results[0]["out"]
```

```python
from contextlib import ExitStack

import concourse.bass as bass
from concourse import mybir

F32 = mybir.dt.float32
F16 = mybir.dt.float16
BF16 = mybir.dt.bfloat16
ALU = mybir.AluOpType
ACT = mybir.ActivationFunctionType
AX_X = mybir.AxisListType.X

P = 128
TOK = 197
PATCH = TOK - 1
IMG = 2
N = IMG * TOK
DEPTH = 4
HEADS = 8
HD = P // HEADS
KCH = 6
EXPERTS = 8
TILES = ((0, 128), (128, TOK - 128))
LAST0 = TOK - 128
EPS = 1e-5
CHUNKS = 32
CW = P // CHUNKS
GEN = 2 * TOK - 1
STATE = 64
CG = CHUNKS // 2
NEG = -1e30
ONE_ROW = 96


FIRST = 1


def shift(it, per, k):
    return it * per + k + FIRST


def start(nc, sems, ahead=()):
    with nc.Block() as blk:
        @blk.gpsimd
        def _(pool):
            for sem in sems:
                pool.sem_inc(sem, FIRST)
            for sem, value in ahead:
                pool.sem_inc(sem, value)


class Banks:

    def __init__(self, steps):
        self.use, count = {}, [0, 0]
        for n, step in enumerate(steps):
            b = n % 2
            self.use[step] = (b, count[b])
            count[b] += 1
        self.per = count


ROUNDS = 2 * DEPTH
NORM_SET = "natural_log_exp_and_others"


def timed(*parts):
    out = [(t0 + (t1 - t0) * (n + 0.5) / len(steps), k, step) for k, (t0, t1, steps) in enumerate(parts)
           for n, step in enumerate(steps)]
    return [step for _, _, step in sorted(out, key=lambda x: x[:2])]


def of(p, *steps):
    return [(step, p) for step in steps]


def probs(p):
    return [("c", p, 0), ("c", p, 1), ("c", p, 2), ("c", p, 3), ("w", p, 0), ("c", p, 4), ("c", p, 5), ("w", p, 1),
            ("c", p, 6), ("c", p, 7), ("w", p, 2), ("o", p, 0), ("w", p, 3), ("o", p, 1)]


def maxima(p):
    return [("b", p, n) for n in range(8)]


END = ("sqn", "varn", "ho", "xcz", "varz", "yz", "u")
TO_MLP = ("den", "on", "proj", "sq2", "var2", "y2")
MLP = [(step, p) for step in ("fc1", "gelu", "fc2") for p in range(2)]


def steps(text):
    words = [word.split("-") for word in text.split()]
    return [(w[0], *map(int, w[1:])) for w in words]


ORDER = steps("""
    c-0-0 c-0-1 c-0-2 c-0-3 sq1-1 w-0-0 sq1-0 c-0-4 c-0-5 w-0-1 var1-0 c-0-6 c-0-7 w-0-2 var1-1 y1-0 o-0-0 q-0
    w-0-3 o-0-1 c-1-0 k-0 c-1-1 v-0 c-1-2 y1-1 c-1-3 den-0 w-1-0 on-0 q-1 k-1 c-1-4 c-1-5 w-1-1 c-1-6 v-1 c-1-7
    b-0-0 w-1-2 o-1-0 b-0-1 w-1-3 b-0-2 o-1-1 proj-0 b-0-3 b-0-4 den-1 sq2-0 b-0-5 on-1 b-0-6 b-0-7 var2-0
    proj-1 b-1-0 sq2-1 neg-0 b-1-1 y2-0 var2-1 b-1-2 b-1-3 fc1-0 y2-1 b-1-4 gelu-0 b-1-5 fc1-1 b-1-6 gelu-1
    b-1-7 fc2-0 fc2-1 neg-1""")
ORDER_END = steps("""
    sqn-0 c-0-0 c-0-1 varn-0 sqn-1 ho-0 c-0-2 c-0-3 w-0-0 varn-1 xcz-0 c-0-4 c-0-5 w-0-1 varz-0 ho-1 xcz-1 c-0-6
    c-0-7 w-0-2 varz-1 yz-0 yz-1 o-0-0 u-0 w-0-3 o-0-1 emb-0 u-1 sq1-0 c-1-0 c-1-1 var1-0 y1-0 emb-1 c-1-2 q-0
    c-1-3 k-0 w-1-0 sq1-1 c-1-4 den-0 c-1-5 v-0 on-0 var1-1 w-1-1 c-1-6 c-1-7 y1-1 w-1-2 o-1-0 q-1 proj-0 b-0-0
    sq2-0 b-0-1 k-1 b-0-2 w-1-3 var2-0 o-1-1 b-0-3 b-0-4 den-1 y2-0 b-0-5 v-1 on-1 b-0-6 fc1-0 b-0-7 gelu-0
    proj-1 sq2-1 b-1-0 b-1-1 var2-1 b-1-2 b-1-3 fc2-0 neg-0 y2-1 b-1-4 b-1-5 fc1-1 b-1-6 b-1-7 gelu-1 fc2-1
    neg-1""")
BODY = [(r, x) for r in range(ROUNDS) for x in (ORDER_END if r < 2 else ORDER)]
LAST_0 = timed((0.02, 0.5, of(0, *END)), (0.05, 0.55, of(1, *END)), (0.0, 0.3, probs(0)), (0.3, 0.6, probs(1)),
               (0.4, 0.7, of(0, *TO_MLP)), (0.65, 0.85, of(1, *TO_MLP)), (0.86, 1.0, MLP))
LAST_1 = timed((0.0, 0.9, of(0, *END)), (0.1, 1.0, of(1, *END)))
LAST = [(0, x) for x in LAST_0] + [(1, x) for x in LAST_1]

DENSE = {"varn": ("varn",), "xcz": ("xcz",), "varz": ("varz",), "u": ("u",), "emb": ("emb",), "var1": ("var1",),
         "q": ("q",), "k": ("k",), "v": ("v",), "den": ("den0", "den1"), "proj": ("proj",),
         "var2": ("var2",), "fc1": ("fc1a", "fc1b"), "neg": ("neg",), "fc2": ("fc2",)}
COUNTED = {
    "sq": {"sqn": 1, "xcz": 1, "sq1": 1, "sq2": 1},
    "rstd": {"varn": 1, "varz": 1, "var1": 1, "var2": 1},
    "y": {"ho": 1, "yz": 1, "y1": 1, "y2": 1},
    "hi": {"q": 1, "k": 1},
    "v": {"v": 1},
    "split": {"k": 32},
    "stacks": {"k": 48},
    "b": {"b": 1},
    "c": {"c": 1},
    "w": {"w": 1},
    "o": {"o": 1},
    "neg": {"neg": 16},
    "rden": {"den": 2},
    "on": {"on": 1},
    "ho": {"ho": 1},
    "ho_out": {"ho": 16},
    "u": {"u": 1},
    "u_out": {"u": 32},
    "cls": {"emb": 1},
}


BY_PAIR = ("split", "stacks", "neg", "ho_out", "u_out")


def dense(steps):
    return [(r, d, x[1]) for r, x in steps for d in DENSE.get(x[0], ())]


def counts(steps):
    out = {}
    for name, adds in COUNTED.items():
        total, at = [0, 0], {}
        for r, x in steps:
            p = x[1] if name in BY_PAIR else 0
            total[p] += adds.get(x[0], 0)
            at[(r, x)] = total[p]
        out[name] = (at, total[0])
    return out


TAIL_FRONT = ("yT", "out", "h2", "xc", "var", "h3", "logit", "route", "hotT")
TAIL_BACK = ("h4", "xcf", "varf", "yf", "back")
TAIL_USES = ("yT", "out", "xc", "var", "logit", "hotT", "xcf", "varf", "back")


def experts(q):
    n = 2 * EXPERTS
    out = []
    for k in range(n + 2):
        out += [("exp", q, k)] * (k < n) + [("w2", q, k - 2)] * (k >= 2)
    return out + [("b2", q)]


def tail_half(q, *chain):
    return [("half", q)] + timed((0.0, 1.0, experts(q)), (0.0, 0.95, of(1 - q, *chain)))


TAIL_FIRST = of(0, *TAIL_FRONT) + tail_half(0, *TAIL_FRONT)
TAIL_BODY = tail_half(1, *(TAIL_BACK + TAIL_FRONT)) + tail_half(0, *(TAIL_BACK + TAIL_FRONT))
TAIL_LAST = tail_half(1, *TAIL_BACK) + [("half", 0)] + of(1, *TAIL_BACK)
TAIL_BANK = {x: x[2] % 2 for x in TAIL_BODY if x[0] == "exp"}
TAIL_BANK.update({x: 2 + n % 2 for n, x in enumerate(x for x in TAIL_BODY if x[0] in TAIL_USES)})
TAIL_COUNTED = {"h2": {"h2": 1}, "sq": {"xc": 1, "xcf": 1}, "rstd": {"var": 1, "varf": 1}, "route": {"route": 5},
                "w2": {"w2": 1}, "moe": {"b2": 1}, "h4": {"h4": 1}, "back": {"back": 1}}


def tail_count(steps):
    adds = {name: (lambda x, by=by: by.get(x[0], 0)) for name, by in TAIL_COUNTED.items()}
    for b in range(4):
        adds[b] = lambda x, b=b: int(TAIL_BANK.get(x) == b)
    for q in range(2):
        adds[f"rows{q}"] = lambda x, q=q: 48 * (x == ("yT", q))
        adds[f"out{q}"] = lambda x, q=q: 32 * (x == ("back", q))
    out = {}
    for name, add in adds.items():
        total, at = 0, {}
        for x in steps:
            total += add(x)
            at[x] = total
        out[name] = (at, total)
    return out


def build(nc, x, conv, convb, clsc, posT, qkv, qkvb, projp, projn, projb, ln1, fc1, fc1b, fc2, fc2b, ln2,
          normwb, attg, win, binb, wout, boutc, lre, lim, bm, cre, cim, dvec, w1, b1c, w2, b2, wg, bgb,
          om, ident, cen, mean, gsel, esel, rank, anti, out):
    B = out.shape[0]
    PAIRS = B // IMG
    GRP = B // 4 if B >= 8 else B
    GROUPS = B // GRP

    with ExitStack() as ctx:
        def sb(name, shape, dt=F32):
            return ctx.enter_context(nc.sbuf_tensor(name, shape, dt))

        def sem(name):
            return ctx.enter_context(nc.semaphore(name))

        split_dram = nc.dram_tensor("split_dram", (2, 2, 2, HD, HEADS, N), F16).ap()
        gen_dram = nc.dram_tensor("gen_dram", (CHUNKS, GEN), F32).ap()
        u_dram = nc.dram_tensor("u_dram", (TOK, B + 4 * IMG, P), F32).ap()
        y_dram = nc.dram_tensor("y_dram", (TOK, B, P), F32).ap()
        ho_dram = nc.dram_tensor("ho_dram", (PAIRS + 4, P, N), F32).ap()

        psA = ctx.enter_context(nc.psum_tensor("psA", [P, 2, 2, 512], F32))
        psD = ctx.enter_context(nc.psum_tensor("psD", [P, 2, 512], F32))
        psO = ctx.enter_context(nc.psum_tensor("psO", [P, 2, 512], F32))

        const_in = sem("const_in")

        conv_s = sb("conv_s", [P, KCH, P])
        qkv_s = sb("qkv_s", [P, DEPTH, 3 * P])
        projp_s = sb("projp_s", [P, DEPTH, 2, P])
        fc1_s = sb("fc1_s", [P, DEPTH, 2 * P])
        fc2_s = sb("fc2_s", [P, DEPTH, 2, P])
        win_s = sb("win_s", [P, P])
        wout_s = sb("wout_s", [P, P])
        cen_s = sb("cen_s", [P, P])
        mean_s = sb("mean_s", [P, P])
        gsel_s = sb("gsel_s", [P, P])
        id_s = sb("id_s", [P, P])
        pos_s = sb("pos_s", [P, TOK])
        binb_s = sb("binb_s", [P, P])
        vecs = {}
        for nm_, src in (("convb", convb), ("clsc", clsc), ("qkvb", qkvb), ("projb", projb), ("ln1", ln1),
                         ("fc1b", fc1b), ("fc2b", fc2b), ("ln2", ln2), ("normwb", normwb), ("attg", attg),
                         ("boutc", boutc), ("lre", lre), ("lim", lim), ("bm", bm), ("cre", cre), ("cim", cim),
                         ("b1c", b1c)):
            vecs[nm_] = (sb(nm_ + "_s", [P, src.shape[1]]), src)
        convb_s, clsc_s, qkvb_s, projb_s, ln1_s, fc1b_s, fc2b_s, ln2_s, normwb_s, attg_s, boutc_s, lre_s, lim_s, \
            bm_s, cre_s, cim_s, b1c_s = [vecs[k][0] for k in vecs]
        loads = [(conv_s, conv), (qkv_s, qkv), (projp_s, projp), (fc1_s, fc1), (fc2_s, fc2), (win_s, win),
                 (wout_s, wout), (cen_s, cen), (mean_s, mean), (gsel_s, gsel), (id_s, ident), (pos_s, posT),
                 (binb_s, binb)] + list(vecs.values())
        bias_s = sb("bias_s", [P, DEPTH, 6])
        eps_s = sb("eps_s", [P, 1])

        with ExitStack() as pre:
            def psb(name, shape, dt=F32):
                return pre.enter_context(nc.sbuf_tensor(name, shape, dt))
            CGS = 4
            projn_s = psb("projn_s", [P, DEPTH, P])
            om_s = psb("om_s", [P, GEN])
            dvec_s = psb("dvec_s", [CHUNKS, 1])
            cb = psb("cb", [P, 2, CG])
            lw = psb("lw", [P, 2, CG * CHUNKS])
            ang = psb("ang", [P, CGS, GEN])
            turn = psb("turn", [P, CGS, GEN])
            red = psb("red", [P, CGS, GEN])
            red2 = psb("red2", [P, CGS, GEN])
            dec = psb("dec", [P, CGS, GEN])
            sn = psb("sn", [P, CGS, GEN])
            hs = psb("hs", [P, CGS, GEN])
            cs = psb("cs", [P, CGS, GEN])
            ec = psb("ec", [P, 2, CGS, GEN])
            es = psb("es", [P, 2, CGS, GEN])
            gen = psb("gen", [CHUNKS, GEN])
            wsum = psb("wsum", [P, KCH + 4 * DEPTH])
            pre_loads = [(projn_s, projn), (om_s, om), (dvec_s, dvec)]

            fold = pre.enter_context(nc.semaphore("fold"))
            shifts_full = pre.enter_context(nc.semaphore("shifts_full"))
            vshift = pre.enter_context(nc.semaphore("vshift"))
            bias_done = pre.enter_context(nc.semaphore("bias_done"))
            centred = pre.enter_context(nc.semaphore("centred"))
            proj_full = pre.enter_context(nc.semaphore("proj_full"))
            winfull = pre.enter_context(nc.semaphore("winfull"))
            chain = pre.enter_context(nc.semaphore("chain"))
            reduced = pre.enter_context(nc.semaphore("reduced"))
            waves = pre.enter_context(nc.semaphore("waves"))
            damped = pre.enter_context(nc.semaphore("damped"))
            summed = pre.enter_context(nc.semaphore("summed"))
            gen_out = pre.enter_context(nc.semaphore("gen_out"))
            gen_done = pre.enter_context(nc.semaphore("gen_done"))
            n_const = 16 * (len(loads) + len(pre_loads))
            blk = pre.enter_context(nc.Block())

            @blk.sync
            def _(sp):
                for t, src in loads + pre_loads:
                    sp.dma_start(t[:], src).then_inc(const_in, 16)
                sp.wait_ge(gen_done, 1)
                sp.dma_start(gen_dram, gen[:, :]).then_inc(gen_out, 16)
                sp.wait_ge(gen_out, 16)

            @blk.tensor
            def _(pe):
                pe.wait_ge(const_in, n_const)
                for l in range(DEPTH):
                    for j in range(3):
                        pe.matmul(psD[:, 0, 8 * l + j:8 * l + j + 1], qkv_s[:, l, j * P:(j + 1) * P],
                                  ln1_s[:, DEPTH + l:DEPTH + l + 1], start=True, stop=True)
                    for j in range(2):
                        last = pe.matmul(psD[:, 0, 8 * l + 3 + j:8 * l + 4 + j], fc1_s[:, l, j * P:(j + 1) * P],
                                         ln2_s[:, DEPTH + l:DEPTH + l + 1], start=True, stop=True)
                last = pe.matmul(psD[:, 0, 128:256], attg_s[:, 1:2].to_broadcast([P, P]), win_s[:, :],
                                 start=True, stop=True)
                last.then_inc(shifts_full, 1)
                pe.wait_ge(vshift, 1)
                for l in range(DEPTH):
                    last = pe.matmul(psD[:, 1, l:l + 1], projn_s[:, l, :], bias_s[:, l, 2:3], start=True, stop=True)
                last.then_inc(proj_full, 1)
                pe.wait_ge(bias_done, 1)
                pe.matmul(psD[:, 1, 8:8 + TOK], cen_s[:, :], pos_s[:, :], start=True, stop=True)
                pe.matmul(psD[:, 1, 256:256 + DEPTH], cen_s[:, :], bias_s[:, :, 5], start=True, stop=True)
                pe.matmul(psD[:, 1, 260:260 + DEPTH], cen_s[:, :], fc2b_s[:, :], start=True,
                          stop=True).then_inc(centred, 1)
                for g in range(CG):
                    n, i = g // CGS % 2, g % CGS
                    pe.wait_ge(damped, 2 * (g // CGS + 1))
                    pe.matmul(psA[0:CHUNKS, 0, 0, 0:GEN], lw[:, 0, g * CHUNKS:(g + 1) * CHUNKS], ec[:, n, i, :],
                              start=(g == 0), stop=False)
                    pe.matmul(psA[0:CHUNKS, 0, 0, 0:GEN], lw[:, 1, g * CHUNKS:(g + 1) * CHUNKS], es[:, n, i, :],
                              start=False, stop=(g == CG - 1)).then_inc(summed, 1)

            @blk.scalar
            def _(act):
                act.wait_ge(const_in, n_const)
                for m in range(CG // CGS):
                    if m >= 1:
                        act.wait_ge(damped, 2 * m)
                    for i in range(CGS):
                        g = CGS * m + i
                        act.activation(dec[:, i, :], om_s[:, :], ACT.Exp, scale=lre_s[:, g:g + 1]).then_inc(waves, 1)
                    act.wait_ge(reduced, m + 1)
                    act.activation(sn[:, :, :], red2[:, :, :], ACT.Sin).then_inc(waves, 1)
                    act.activation(hs[:, :, :], red2[:, :, :], ACT.Sin, scale=0.5).then_inc(waves, 1)

            @blk.vector
            def _(dve):
                steps = [0]

                def then(ins):
                    steps[0] += 1
                    ins.then_inc(chain, 1)
                    dve.wait_ge(chain, steps[0])

                dve.memset(eps_s[:, :], EPS)
                then(dve.memset(lw[:, :, :], 0.0))
                dve.wait_ge(const_in, n_const)
                dve.tensor_scalar(pos_s[:, 1:TOK], pos_s[:, 1:TOK], convb_s[:, 0:1], None, ALU.add)
                dve.tensor_tensor(pos_s[:, 0:1], pos_s[:, 0:1], clsc_s[:, 0:1], ALU.add)
                dve.wait_ge(shifts_full, 1)
                sv = psD[:, 0, 0:8 * DEPTH].rearrange("p (l k) -> p l k", k=8)
                dve.tensor_tensor(bias_s[:, :, 0:3], sv[:, :, 0:3],
                                  qkvb_s[:, :].rearrange("p (l k) -> p l k", k=3), ALU.add)
                dve.tensor_tensor(bias_s[:, :, 3:5], sv[:, :, 3:5],
                                  fc1b_s[:, :].rearrange("p (l k) -> p l k", k=2), ALU.add)
                then(dve.tensor_tensor(binb_s[:, :], psD[:, 0, 128:256], binb_s[:, :], ALU.add))
                dve.tensor_scalar(bias_s[:, :, 0:1], bias_s[:, :, 0:1], float(HD) ** -0.5, None,
                                  ALU.mult).then_inc(vshift, 1)
                for l in range(DEPTH):
                    dve.tensor_scalar(qkv_s[:, l, P:], qkv_s[:, l, P:], ln1_s[:, l:l + 1], None, ALU.mult)
                    dve.tensor_scalar(qkv_s[:, l, 0:P], qkv_s[:, l, 0:P], ln1_s[:, l:l + 1], float(HD) ** -0.5,
                                      ALU.mult, ALU.mult)
                    dve.tensor_scalar(fc1_s[:, l, :], fc1_s[:, l, :], ln2_s[:, l:l + 1], None, ALU.mult)
                dve.tensor_scalar(win_s[:, :], win_s[:, :], attg_s[:, 0:1], None, ALU.mult)
                dve.wait_ge(proj_full, 1)
                dve.tensor_tensor(bias_s[:, :, 5], psD[:, 1, 0:DEPTH], projb_s[:, :], ALU.add).then_inc(bias_done, 1)
                parts = [(conv_s[:, :, :], KCH), (projp_s[:, :, :, :].rearrange("p l g n -> p (l g) n"), 2 * DEPTH),
                         (fc2_s[:, :, :, :].rearrange("p l j n -> p (l j) n"), 2 * DEPTH)]
                k0 = 0
                for w, k in parts:
                    last = dve.tensor_reduce(wsum[:, k0:k0 + k], w, AX_X, ALU.add)
                    k0 += k
                then(last)
                then(dve.tensor_scalar(wsum[:, :], wsum[:, :], 1.0 / P, None, ALU.mult))
                k0 = 0
                for w, k in parts:
                    for i in range(k):
                        dve.tensor_scalar(w[:, i, :], w[:, i, :], wsum[:, k0 + i:k0 + i + 1], None, ALU.subtract)
                    k0 += k
                dve.wait_ge(centred, 1)
                dve.tensor_copy(pos_s[:, :], psD[:, 1, 8:8 + TOK])
                dve.tensor_copy(bias_s[:, :, 5], psD[:, 1, 256:256 + DEPTH])
                dve.tensor_copy(fc2b_s[:, :], psD[:, 1, 260:260 + DEPTH])
                dve.tensor_tensor(cb[:, 0, :], cre_s[:, :], bm_s[:, :], ALU.mult)
                then(dve.tensor_tensor(cb[:, 1, :], cim_s[:, :], bm_s[:, :], ALU.mult))
                for i in range(2):
                    r = slice(STATE * i, STATE * (i + 1))
                    dve.tensor_scalar(lw[r, 0, i::CHUNKS + 2], cb[r, 0, :], 1.0, None, ALU.mult)
                    then(dve.tensor_scalar(lw[r, 1, i::CHUNKS + 2], cb[r, 1, :], -1.0, None, ALU.mult))
                for m in range(CG // CGS):
                    for i in range(CGS):
                        last = dve.tensor_scalar(ang[:, i, :], om_s[:, :], lim_s[:, CGS * m + i:CGS * m + i + 1], None,
                                                 ALU.mult)
                    then(last)
                    then(dve.tensor_scalar(turn[:, :, :], ang[:, :, :], TURNS, MAGIC, ALU.mult, ALU.add))
                    then(dve.tensor_scalar(turn[:, :, :], turn[:, :, :], MAGIC, None, ALU.subtract))
                    then(dve.scalar_tensor_tensor(out=red[:, :, :], in0=turn[:, :, :], scalar=-PI2[0], in1=ang[:, :, :],
                                                  op0=ALU.mult, op1=ALU.add))
                    then(dve.scalar_tensor_tensor(out=red[:, :, :], in0=turn[:, :, :], scalar=-PI2[1], in1=red[:, :, :],
                                                  op0=ALU.mult, op1=ALU.add))
                    then(dve.scalar_tensor_tensor(out=red[:, :, :], in0=turn[:, :, :], scalar=-PI2[2], in1=red[:, :, :],
                                                  op0=ALU.mult, op1=ALU.add))
                    dve.tensor_scalar(red2[:, :, :], red[:, :, :], PI_BELOW, -PI_BELOW, ALU.min,
                                      ALU.max).then_inc(reduced, 1)
                    dve.wait_ge(waves, (CGS + 2) * (m + 1))
                    then(dve.scalar_tensor_tensor(out=cs[:, :, :], in0=hs[:, :, :], scalar=-2.0, in1=hs[:, :, :],
                                                  op0=ALU.mult, op1=ALU.mult))
                    if m >= 2:
                        dve.wait_ge(summed, CGS * (m - 1))
                    dve.scalar_tensor_tensor(out=ec[:, m % 2, :, :], in0=cs[:, :, :], scalar=1.0, in1=dec[:, :, :],
                                             op0=ALU.add, op1=ALU.mult).then_inc(damped, 1)
                    dve.tensor_tensor(es[:, m % 2, :, :], sn[:, :, :], dec[:, :, :], ALU.mult).then_inc(damped, 1)
                dve.wait_ge(summed, CG)
                then(dve.tensor_copy(gen[:, :], psA[0:CHUNKS, 0, 0, 0:GEN]))
                dve.tensor_tensor(gen[:, TOK - 1:TOK], gen[:, TOK - 1:TOK], dvec_s[:, :],
                                  ALU.add).then_inc(gen_done, 1)

        with ExitStack() as st:
            def ssb(name, shape, dt=F32):
                return st.enter_context(nc.sbuf_tensor(name, shape, dt))

            counted = []

            def ssem(name):
                counted.append(st.enter_context(nc.semaphore(name)))
                return counted[-1]

            def four(name, shape, dt=F32):
                return [[ssb(f"{name}{s}{p}", shape, dt) for p in range(2)] for s in range(2)]

            def two(name, shape, dt=F32):
                return [ssb(f"{name}{p}", shape, dt) for p in range(2)]

            h = four("h", [P, N])
            qst = four("qst", [P, HEADS, N], F16)
            kst = four("kst", [P, HEADS, N], F16)
            vals = four("vals", [P, IMG, 2, HEADS, 2 * HD])
            patches = two("patches", [P, KCH, IMG * PATCH])
            sq = two("sq", [P, N])
            lnv = two("lnv", [P, N])
            rstd = two("rstd", [P, N])
            y = two("y", [P, N])
            qsp = two("qsp", [P, 2, N], F16)
            ksp = two("ksp", [P, 2, N], F16)
            nmax = two("nmax", [P, IMG, 2, HEADS], F16)
            idh_s = ssb("idh_s", [P, P], F16)
            nmT = two("nmT", [HEADS, N], F16)
            prob = ssb("prob", [P, 4, 4, TOK])
            osb = two("osb", [P, 2, N])
            lden = two("lden", [P, 2, N])
            rden = two("rden", [P, 2, N])
            on = two("on", [P, 2, N])
            gl = two("gl", [P, 2, N])
            ho = two("ho", [P, N])
            usb = two("usb", [P, IMG, 2, P])

            patches_in = [ssem(f"patches_in{p}") for p in range(2)]
            full = [ssem(f"dense_full{b}") for b in range(2)]
            evac = [ssem(f"dense_evac{b}") for b in range(2)]
            set_up = st.enter_context(nc.semaphore("set_up"))
            ones_set = [[st.enter_context(nc.semaphore(f"ones_set{s}{p}")) for p in range(2)] for s in range(2)]
            cls_done = ssem("cls_done")
            sq_done = ssem("sq_done")
            rstd_done = ssem("rstd_done")
            y_done = ssem("y_done")
            hi_done = ssem("hi_done")
            v_parts = ssem("v_parts")
            split_out = [ssem(f"split_out{p}") for p in range(2)]
            stacks_in = [ssem(f"stacks_in{p}") for p in range(2)]
            keys_full = ssem("keys_full")
            max_done = ssem("max_done")
            neg_in = [ssem(f"neg_in{p}") for p in range(2)]
            probs_full = ssem("probs_full")
            exp_done = ssem("exp_done")
            pv_done = ssem("pv_done")
            o_copied = ssem("o_copied")
            rden_done = ssem("rden_done")
            on_done = ssem("on_done")
            ho_done = ssem("ho_done")
            ho_out = [ssem(f"ho_out{p}") for p in range(2)]
            u_parts = ssem("u_parts")
            u_out = [ssem(f"u_out{p}") for p in range(2)]
            sems = {"sq": sq_done, "rstd": rstd_done, "y": y_done, "hi": hi_done, "v": v_parts, "split": split_out,
                    "stacks": stacks_in, "b": max_done, "c": exp_done, "w": pv_done, "o": o_copied, "neg": neg_in,
                    "rden": rden_done, "on": on_done, "ho": ho_done, "ho_out": ho_out, "u": u_parts,
                    "u_out": u_out, "cls": cls_done}
            ITERS = PAIRS // 4
            body, last_part = Banks(dense(BODY)), Banks(dense(LAST))
            body_counts, last_counts = counts(BODY), counts(LAST)
            units = [[(r, x) for r, x in steps if x[0] in "bc"] for steps in (BODY, LAST)]

            class At:

                def __init__(self, it, last=False):
                    self.it, self.banks = it, last_part if last else body
                    self.counts = last_counts if last else body_counts
                    self.units = units[last]

                def slot(self, r, x):
                    return self.units.index((r, x)) % 2

                def bank(self, r, step, p, more):
                    b, k = self.banks.use[(r, step, p)]
                    return b, shift(self.it, body.per[b], k + more)

            def signal(name, step):
                return sems[name][step[1]] if name in BY_PAIR else sems[name]

            def wait(eng, at, name, r, step):
                eng.wait_ge(signal(name, step), shift(at.it, body_counts[name][1], at.counts[name][0][(r, step)]))

            def wait_before(eng, at, name, r, step, back=1):
                add = COUNTED[name][step[0]]
                k = at.counts[name][0][(r, step)] - back * add
                if k >= 0:
                    eng.wait_ge(signal(name, step), shift(at.it, body_counts[name][1], k))
                else:
                    eng.wait_ge(signal(name, step), shift(at.it, body_counts[name][1], 0))

            def wait_round(eng, at, name, r, step):
                if r:
                    wait(eng, at, name, r - 1, step)
                else:
                    eng.wait_ge(signal(name, step), shift(at.it, body_counts[name][1], 0))

            def ready(eng, at, r, step, p):
                b, v = at.bank(r, step, p, 1)
                eng.wait_ge(full[b], v)
                return psD[:, b, :]

            def result(eng, at, r, step, p):
                b, v = at.bank(r, step, p, 1)
                eng.wait_ge(evac[b], v)

            def free(pe, at, r, step, p, after=()):
                own, k = at.banks.use[(r, step, p)]
                need = {own: k}
                for d in after:
                    b, k = at.banks.use[(r, d, p)]
                    need[b] = max(need.get(b, 0), k + 1)
                for b, k in need.items():
                    pe.wait_ge(evac[b], shift(at.it, body.per[b], k))
                return psD[:, own, :]

            def fulls(ins, at, r, step, p):
                ins.then_inc(full[at.bank(r, step, p, 1)[0]], 1)

            def evacs(ins, at, r, step, p):
                ins.then_inc(evac[at.bank(r, step, p, 1)[0]], 1)

            def mlp_result(eng, at, r, p):
                if r:
                    result(eng, at, r - 1, "fc2", p)
                else:
                    for b in range(2):
                        eng.wait_ge(evac[b], shift(at.it, body.per[b], 0))

            def layer(r, second):
                return (r - second) // 2 % DEPTH

            SQUARE = {"varn": "sqn", "varz": "xcz", "var1": "sq1", "var2": "sq2"}
            start(nc, counted)
            blk = st.enter_context(nc.Block())

            @blk.sync
            def _(sp):
                ho_slots = ho_dram.rearrange("(i s) p n -> i s p n", s=4)
                u_slots = u_dram.rearrange("t (i s b) p -> t i s b p", s=4, b=IMG)
                x_next = x[2:].rearrange("(i s) p k n -> i s p k n", s=4)

                def play(at, r, steps):
                    for x in steps:
                        step, p = x[0], x[1]
                        if step == "ho":
                            wait(sp, at, "ho", r, x)
                            sp.dma_start(ho_slots[bass.ds(at.it, 1), 2 * r + p].rearrange("a p n -> (a p) n"),
                                         ho[p][:, :]).then_inc(ho_out[p], 16)
                        elif step == "u":
                            for t, (t0, tn) in enumerate(TILES):
                                if t == 0:
                                    wait(sp, at, "u", r, x)
                                else:
                                    result(sp, at, r, "u", p)
                                sp.dma_start(u_slots[t0:t0 + tn, bass.ds(at.it, 1), 2 * r + p].rearrange(
                                    "t a b p -> t (a b) p"), usb[p][0:tn, :, t, :]).then_inc(u_out[p], 16)
                        elif step == "emb":
                            ready(sp, at, r, "emb", p)
                            sp.dma_start(patches[p][:, :, :], x_next[bass.ds(at.it, 1), 2 * r + p].rearrange(
                                "a p k n -> (a p) k n")).then_inc(patches_in[p], 16)
                        elif step in ("q", "k"):
                            j = "qk".index(step)
                            result(sp, at, r, step, p)
                            sp.dma_start(split_dram[p, j].rearrange("s d h n -> (d h) s n"),
                                         (qsp, ksp)[j][p][:, :, :]).then_inc(split_out[p], 16)
                            if step == "k":
                                wait(sp, at, "split", r, x)
                                for part in range(2):
                                    src = split_dram[p, 0, part].rearrange("d h n -> d (h n)")
                                    sp.dma_start(qst[r % 2][p][2 * HD * part:2 * HD * (part + 1), :, :],
                                                 src.unsqueeze(0).to_broadcast([2, HD, HEADS * N])
                                                 ).then_inc(stacks_in[p], 16)
                                src = split_dram[p, 1].rearrange("s d h n -> (s d) (h n)")
                                sp.dma_start(kst[r % 2][p][0:4 * HD, :, :],
                                             src.unsqueeze(0).to_broadcast([2, 2 * HD, HEADS * N])
                                             ).then_inc(stacks_in[p], 16)
                        elif step == "neg":
                            result(sp, at, r, "neg", p)
                            sp.dma_start(qst[r % 2][p][ONE_ROW:ONE_ROW + 1, :, :],
                                         nmT[p][:, :]).then_inc(neg_in[p], 16)

                for p in range(2):
                    sp.dma_start(patches[p][:, :, :], x[p]).then_inc(patches_in[p], 16)
                with sp.Fori(0, ITERS) as it:
                    for r in range(ROUNDS):
                        play(At(it), r, ORDER_END if r < 2 else ORDER)
                at = At(ITERS, last=True)
                play(at, 0, LAST_0)
                play(at, 1, LAST_1)
                for p in range(2):
                    sp.wait_ge(ho_out[p], shift(0, 0, 16 * (PAIRS // 2 + 2)))
                    sp.wait_ge(u_out[p], shift(0, 0, 32 * (PAIRS // 2 + 2)))
                    sp.wait_ge(patches_in[p], shift(0, 0, 16 * (PAIRS // 2 + 1)))

            @blk.tensor
            def _(pe):
                pe.wait_ge(set_up, 19)

                def scores(at, r, kind, p, n):
                    s = r % 2 if kind == "b" else 1 - r % 2
                    m = at.units.index((r, (kind, p, n)))
                    slot = at.slot(r, (kind, p, n))
                    if m >= 2:
                        r0, x0 = at.units[m - 2]
                        wait(pe, at, x0[0], r0, x0)
                    else:
                        pe.wait_ge(max_done, shift(at.it, body_counts["b"][1], 0))
                    if kind == "b":
                        b, t, g = n // 4, n // 2 % 2, n % 2
                        sta, mov, rows = qst[s][p], kst[s][p], ONE_ROW
                    else:
                        b, g, t = n // 4, n // 2 % 2, n % 2
                        sta, mov, rows = kst[s][p], qst[s][p], ONE_ROW + 1
                    t0, tn = TILES[t]
                    for j in range(4):
                        last = pe.matmul(psA[0:tn, slot, j // 2, (j % 2) * TOK:(j % 2 + 1) * TOK],
                                         sta[0:rows, 4 * g + j, b * TOK + t0:b * TOK + t0 + tn],
                                         mov[0:rows, 4 * g + j, b * TOK:(b + 1) * TOK], start=True, stop=True)
                    last.then_inc(keys_full if kind == "b" else probs_full, 1)

                def weighted(at, r, p, n):
                    b, g, s = n // 2, n % 2, 1 - r % 2
                    wait(pe, at, "c", r, ("c", p, 2 * n + 1))
                    if b == 0:
                        wait_before(pe, at, "o", r, ("o", p, g), 2)
                    for t, (t0, tn) in enumerate(TILES):
                        for j in range(4):
                            last = pe.matmul(psO[32 * j:32 * j + 32, g, b * TOK:(b + 1) * TOK],
                                             vals[s][p][0:tn, b, t, 4 * g + j, :], prob[0:tn, (2 * n + t) % 4, j, :],
                                             start=(t == 0), stop=(t == 1))
                    last.then_inc(pv_done, 1)

                def product(at, r, step, p, weights, moving, after=()):
                    ps = free(pe, at, r, step, p, after)
                    for i, (w, m) in enumerate(zip(weights, moving)):
                        last = pe.matmul(ps[:, 0:m.shape[1]], w, m, start=(i == 0), stop=(i == len(weights) - 1))
                    fulls(last, at, r, step, p)

                def by_token(at, r, step, p, weights):
                    ps = free(pe, at, r, step, p)
                    for b in range(IMG):
                        for t, (t0, tn) in enumerate(TILES):
                            last = pe.matmul(ps[0:tn, (2 * b + t) * P:(2 * b + t + 1) * P],
                                             y[p][:, b * TOK + t0:b * TOK + t0 + tn], weights, start=True, stop=True)
                    fulls(last, at, r, step, p)

                def play(at, r, steps):
                    l1, l2 = layer(r, 0), layer(r, 1)
                    for x in steps:
                        step, p = x[0], x[1]
                        if step in ("b", "c"):
                            if x[2] == 0 and step == "b":
                                wait(pe, at, "stacks", r, ("k", p))
                            elif x[2] == 0:
                                wait_round(pe, at, "neg", r, ("neg", p))
                            scores(at, r, step, p, x[2])
                        elif step == "w":
                            weighted(at, r, p, x[2])
                        elif step == "emb":
                            pe.wait_ge(patches_in[p], shift(at.it, 32, 16 * (r + 1)))
                            product(at, r, "emb", p, [conv_s[:, k, :] for k in range(KCH)],
                                    [patches[p][:, k, :] for k in range(KCH)])
                        elif step in SQUARE:
                            wait(pe, at, "sq", r, (SQUARE[step], p))
                            product(at, r, step, p, [mean_s[:, :]], [sq[p][:, :]])
                        elif step == "xcz":
                            wait(pe, at, "ho", r, ("ho", p))
                            product(at, r, "xcz", p, [cen_s[:, :]], [ho[p][:, :]])
                        elif step == "u":
                            wait(pe, at, "y", r, ("yz", p))
                            by_token(at, r, "u", p, win_s[:, :])
                        elif step in ("q", "k"):
                            wait(pe, at, "y", r, ("y1", p))
                            j = "qk".index(step)
                            product(at, r, step, p, [qkv_s[:, l1, j * P:(j + 1) * P]], [y[p][:, :]])
                        elif step == "v":
                            by_token(at, r, "v", p, qkv_s[:, l1, 2 * P:])
                        elif step == "den":
                            wait(pe, at, "o", r, ("o", p, 1))
                            for g in range(2):
                                product(at, r, f"den{g}", p, [gsel_s[:, :]], [osb[p][:, g, :]])
                        elif step == "proj":
                            wait(pe, at, "on", r, ("on", p))
                            product(at, r, "proj", p, [projp_s[:, l2, g, :] for g in range(2)],
                                    [on[p][:, g, :] for g in range(2)])
                        elif step == "fc1":
                            wait(pe, at, "y", r, ("y2", p))
                            for j, d in enumerate(("fc1a", "fc1b")):
                                product(at, r, d, p, [fc1_s[:, l2, j * P:(j + 1) * P]], [y[p][:, :]])
                        elif step == "neg":
                            wait(pe, at, "b", r, ("b", p, 7))
                            ps = free(pe, at, r, "neg", p)
                            for b in range(IMG):
                                for t, (t0, tn) in enumerate(TILES):
                                    c0 = b * TOK + t0
                                    last = pe.matmul(ps[0:HEADS, c0:c0 + tn], nmax[p][0:tn, b, t, :], idh_s[0:tn, 0:tn],
                                                     start=True, stop=True)
                            fulls(last, at, r, "neg", p)
                        elif step == "fc2":
                            product(at, r, "fc2", p, [fc2_s[:, l2, j, :] for j in range(2)],
                                    [gl[p][:, j, :] for j in range(2)], ("fc1a", "fc1b"))

                with pe.Fori(0, ITERS) as it:
                    for r in range(ROUNDS):
                        play(At(it), r, ORDER_END if r < 2 else ORDER)
                at = At(ITERS, last=True)
                play(at, 0, LAST_0)
                play(at, 1, LAST_1)

            @blk.scalar
            def _(act):
                act.preload_act_table_set(NORM_SET)
                act.wait_ge(set_up, 19)

                def square(p, source):
                    act.activation(sq[p][:, :], source, ACT.Square).then_inc(sq_done, 1)

                def inverse(at, r, step, p):
                    ps = ready(act, at, r, step, p)
                    evacs(act.activation(lnv[p][:, :], ps[:, 0:N], ACT.Ln, bias=eps_s[:, 0:1]), at, r, step, p)
                    result(act, at, r, step, p)
                    act.activation(rstd[p][:, :], lnv[p][:, :], ACT.Exp, scale=-0.5).then_inc(rstd_done, 1)

                def play(at, r, steps):
                    s, l1, l2 = r % 2, layer(r, 0), layer(r, 1)
                    for x in steps:
                        step, p = x[0], x[1]
                        if step == "c":
                            n = x[2]
                            tn = TILES[n % 2][1]
                            act.wait_ge(probs_full, shift(at.it, body_counts["c"][1], at.counts["c"][0][(r, x)]))
                            wait_before(act, at, "w", r, ("w", p, n // 2), 2)
                            act.activation(prob[0:tn, n % 4, :, :].rearrange("p (a c) n -> p a c n", c=2),
                                           psA[0:tn, at.slot(r, x), :, 0:2 * TOK].rearrange("p a (c n) -> p a c n", c=2),
                                           ACT.Exp).then_inc(exp_done, 1)
                        elif step == "sqn":
                            mlp_result(act, at, r, p)
                            square(p, h[s][p][:, :])
                        elif step == "xcz":
                            result(act, at, r, "xcz", p)
                            square(p, y[p][:, :])
                        elif step == "sq1":
                            if r < 2:
                                result(act, at, r, "emb", p)
                                wait(act, at, "cls", r, ("emb", p))
                            else:
                                mlp_result(act, at, r, p)
                            square(p, h[s][p][:, :])
                        elif step == "sq2":
                            result(act, at, r, "proj", p)
                            square(p, h[1 - s][p][:, :])
                        elif step in SQUARE:
                            inverse(at, r, step, p)
                        elif step in ("q", "k"):
                            j = "qk".index(step)
                            ps = ready(act, at, r, step, p)
                            wait_before(act, at, "split", r, ("k", p))
                            act.activation((qsp, ksp)[j][p][:, 0, :], ps[:, 0:N], ACT.Identity,
                                           bias=bias_s[:, l1, j:j + 1]).then_inc(hi_done, 1)
                        elif step == "den":
                            for g in range(2):
                                ps = ready(act, at, r, f"den{g}", p)
                                evacs(act.activation(lden[p][:, g, :], ps[:, 0:N], ACT.Ln), at, r, f"den{g}", p)
                            for g in range(2):
                                result(act, at, r, f"den{g}", p)
                                act.activation(rden[p][:, g, :], lden[p][:, g, :], ACT.Exp,
                                               scale=-1.0).then_inc(rden_done, 1)
                        elif step == "neg":
                            ps = ready(act, at, r, "neg", p)
                            wait_before(act, at, "neg", r, ("neg", p))
                            evacs(act.activation(nmT[p][:, :], ps[0:HEADS, 0:N], ACT.Copy), at, r, "neg", p)
                        elif step == "gelu":
                            for j, d in enumerate(("fc1a", "fc1b")):
                                ps = ready(act, at, r, d, p)
                                evacs(act.activation(gl[p][:, j, :], ps[:, 0:N], ACT.Gelu, bias=bias_s[:, l2, 3 + j:4 + j]),
                                      at, r, d, p)
                            if p == 1:
                                act.preload_act_table_set(NORM_SET)

                with act.Fori(0, ITERS) as it:
                    for r in range(ROUNDS):
                        play(At(it), r, ORDER_END if r < 2 else ORDER)
                at = At(ITERS, last=True)
                play(at, 0, LAST_0)
                play(at, 1, LAST_1)

            def stack_rows(eng, s, p):
                eng.memset(kst[s][p][:, :, :], 1.0).then_inc(ones_set[s][p], 1)
                eng.wait_ge(ones_set[s][p], 1)
                eng.memset(kst[s][p][0:ONE_ROW, :, :], 0.0).then_inc(set_up, 1)

            @blk.gpsimd
            def _(pool):
                for s, p in ((0, 0), (0, 1), (1, 0)):
                    stack_rows(pool, s, p)

            @blk.vector
            def _(dve):
                for s in range(2):
                    for p in range(2):
                        dve.memset(h[s][p][:, :], 0.0).then_inc(set_up, 1)
                        dve.memset(qst[s][p][:, :, :], 0.0).then_inc(set_up, 1)
                        dve.memset(vals[s][p][:, :, :, :, :], 1.0).then_inc(set_up, 1)
                stack_rows(dve, 1, 1)
                for p in range(2):
                    dve.memset(nmax[p][:, :, :, :], 0.0).then_inc(set_up, 1)
                dve.tensor_copy(idh_s[:, :], id_s[:, :]).then_inc(set_up, 1)
                dve.wait_ge(set_up, 19)

                def scaled(at, r, step, p, source):
                    wait(dve, at, "rstd", r, ({"ho": "varn", "yz": "varz", "y1": "var1", "y2": "var2"}[step], p))
                    dve.tensor_tensor(y[p][:, :], source, rstd[p][:, :], ALU.mult).then_inc(y_done, 1)

                def add_to_h(at, r, s, step, p, bias):
                    ps = ready(dve, at, r, step, p)
                    evacs(dve.scalar_tensor_tensor(out=h[s][p][:, :], in0=ps[:, 0:N], scalar=bias, in1=h[s][p][:, :],
                                                   op0=ALU.add, op1=ALU.add), at, r, step, p)

                def play(at, r, steps):
                    s, l1, l2 = r % 2, layer(r, 0), layer(r, 1)
                    for x in steps:
                        step, p = x[0], x[1]
                        if step == "b":
                            n = x[2]
                            b, t, g = n // 4, n // 2 % 2, n % 2
                            tn = TILES[t][1]
                            dve.wait_ge(keys_full, shift(at.it, body_counts["b"][1], at.counts["b"][0][(r, x)]))
                            dve.tensor_reduce(nmax[p][0:tn, b, t, 4 * g:4 * g + 4].rearrange("p (a c) -> p a c", c=2),
                                              psA[0:tn, at.slot(r, x), :, 0:2 * TOK].rearrange("p a (c n) -> p a c n", c=2),
                                              AX_X, ALU.max, negate=True).then_inc(max_done, 1)
                        elif step == "o":
                            g = x[2]
                            wait(dve, at, "w", r, ("w", p, g + 2))
                            dve.tensor_copy(osb[p][:, g, :], psO[:, g, 0:N]).then_inc(o_copied, 1)
                        elif step == "emb":
                            ps = ready(dve, at, r, "emb", p)
                            hv = h[s][p][:, :].rearrange("p (b t) -> p b t", b=IMG)
                            for b in range(IMG):
                                last = dve.tensor_copy(hv[:, b, 0:1], pos_s[:, 0:1])
                            last.then_inc(cls_done, 1)
                            for b in range(IMG):
                                last = dve.tensor_tensor(hv[:, b, 1:TOK], ps[:, b * PATCH:(b + 1) * PATCH],
                                                         pos_s[:, 1:TOK], ALU.add)
                            evacs(last, at, r, "emb", p)
                        elif step == "ho":
                            mlp_result(dve, at, r, p)
                            scaled(at, r, "ho", p, h[s][p][:, :])
                            wait(dve, at, "y", r, ("ho", p))
                            wait_before(dve, at, "ho_out", r, ("ho", p))
                            dve.tensor_scalar(ho[p][:, :], y[p][:, :], normwb_s[:, 0:1], normwb_s[:, 1:2], ALU.mult,
                                              ALU.add).then_inc(ho_done, 1)
                        elif step == "xcz":
                            ps = ready(dve, at, r, "xcz", p)
                            evacs(dve.tensor_copy(y[p][:, :], ps[:, 0:N]), at, r, "xcz", p)
                        elif step == "yz":
                            scaled(at, r, "yz", p, y[p][:, :])
                        elif step == "u":
                            ps = ready(dve, at, r, "u", p)
                            wait_before(dve, at, "u_out", r, ("u", p))
                            pv = ps.rearrange("p (b t d) -> p b t d", b=IMG, t=2)
                            for t, (t0, tn) in enumerate(TILES):
                                for b in range(IMG):
                                    last = dve.tensor_tensor(usb[p][0:tn, b, t, :], pv[0:tn, b, t, :], binb_s[0:tn, :],
                                                             ALU.add)
                                if t == 0:
                                    last.then_inc(u_parts, 1)
                            evacs(last, at, r, "u", p)
                        elif step == "y1":
                            scaled(at, r, "y1", p, h[s][p][:, :])
                        elif step == "y2":
                            scaled(at, r, "y2", p, h[1 - s][p][:, :])
                        elif step in ("q", "k"):
                            j = "qk".index(step)
                            ps = ready(dve, at, r, step, p)
                            part = (qsp, ksp)[j][p]
                            wait(dve, at, "hi", r, x)
                            evacs(dve.scalar_tensor_tensor(out=part[:, 1, :], in0=ps[:, 0:N], scalar=bias_s[:, l1, j:j + 1],
                                                           in1=part[:, 0, :], op0=ALU.add, op1=ALU.subtract),
                                  at, r, step, p)
                        elif step == "v":
                            pv = ready(dve, at, r, "v", p).rearrange("p (b t h d) -> p b t h d", b=IMG, t=2, h=HEADS)
                            for t, (t0, tn) in enumerate(TILES):
                                for b in range(IMG):
                                    last = dve.tensor_copy(vals[s][p][0:tn, b, t, :, 0:HD], pv[0:tn, b, t, :, :])
                                if t == 0:
                                    last.then_inc(v_parts, 1)
                            evacs(last, at, r, "v", p)
                        elif step == "on":
                            wait(dve, at, "rden", r, ("den", p))
                            dve.tensor_tensor(on[p][:, :, :], osb[p][:, :, :], rden[p][:, :, :],
                                              ALU.mult).then_inc(on_done, 1)
                        elif step == "proj":
                            add_to_h(at, r, 1 - s, "proj", p, bias_s[:, l2, 5:6])
                        elif step == "fc2":
                            add_to_h(at, r, 1 - s, "fc2", p, fc2b_s[:, l2:l2 + 1])

                with dve.Fori(0, ITERS) as it:
                    for r in range(ROUNDS):
                        play(At(it), r, ORDER_END if r < 2 else ORDER)
                at = At(ITERS, last=True)
                play(at, 0, LAST_0)
                play(at, 1, LAST_1)

        with ExitStack() as st:
            def ssb(name, shape, dt=F32):
                return st.enter_context(nc.sbuf_tensor(name, shape, dt))

            counted = []

            def ssem(name):
                counted.append(st.enter_context(nc.semaphore(name)))
                return counted[-1]

            BUFS = 2 if GROUPS % 2 == 0 else 1
            toep = [ssb(f"toep{t}", [tn, CHUNKS, TOK]) for t, (t0, tn) in enumerate(TILES)]
            uin = [[ssb(f"uin{b}{t}", [tn, GRP, P]) for t, (t0, tn) in enumerate(TILES)] for b in range(BUFS)]
            yout = [ssb(f"yout{t}", [tn, GRP, P]) for t, (t0, tn) in enumerate(TILES)]
            toep_in = st.enter_context(nc.semaphore("toep_in"))
            uin_in = [st.enter_context(nc.semaphore(f"uin_in{b}")) for b in range(BUFS)]
            conv_full = ssem("conv_full")
            conv_act = ssem("conv_act")
            conv_dve = ssem("conv_dve")
            yout_out = [ssem(f"yout_out{t}") for t in range(2)]
            CB = 4
            STEPS = 2 * CHUNKS // CB

            def done(it, g, k):
                return shift(it, BUFS * STEPS // 2, g * STEPS // 2 + k)

            def filled(it, g, n):
                return shift(it, BUFS * STEPS, (BUFS + g) * STEPS + n + 1)

            start(nc, counted, [(conv_full, BUFS * STEPS)])
            blk = st.enter_context(nc.Block())

            @blk.sync
            def _(sp):
                for t, (t0, tn) in enumerate(TILES):
                    g0 = gen_dram[:, :]
                    src = bass.AP(tensor=g0.tensor, offset=t0, ap=[[1, tn], [GEN, CHUNKS], [1, TOK]])
                    sp.dma_start(toep[t][:, :, :], src).then_inc(toep_in, 16)
                with sp.Fori(0, GROUPS // BUFS) as it:
                    for b in range(BUFS):
                        for t, (t0, tn) in enumerate(TILES):
                            sp.wait_ge(conv_act, done(it, b, STEPS // 4 * (t + 1)))
                            sp.wait_ge(conv_dve, done(it, b, STEPS // 4 * (t + 1)))
                            sp.dma_start(y_dram[t0:t0 + tn, bass.ds(BUFS * GRP * it + GRP * b, GRP), :],
                                         yout[t][:, :, :]).then_inc(yout_out[t], 16)
                for t in range(2):
                    sp.wait_ge(yout_out[t], shift(GROUPS, 16, 0))

            @blk.gpsimd
            def _(pool):
                with pool.Fori(0, GROUPS // BUFS) as it:
                    for b in range(BUFS):
                        pool.wait_ge(conv_full, shift(it, BUFS * STEPS, (b + 1) * STEPS))
                        for t, (t0, tn) in enumerate(TILES):
                            pool.dma_start(uin[b][t][:, :, :],
                                           u_dram[t0:t0 + tn, bass.ds(BUFS * GRP * it + GRP * b + 4 * IMG, GRP), :]
                                           ).then_inc(uin_in[b], 16)

            @blk.tensor
            def _(pe):
                pe.wait_ge(toep_in, 32)
                with pe.Fori(0, GROUPS // BUFS) as it:
                    for g, n in [(g, n) for g in range(BUFS) for n in range(STEPS)]:
                        if n == 0:
                            pe.wait_ge(uin_in[g], it * 32 + 32)
                        t, c0 = n // (STEPS // 2), n % (STEPS // 2) * CB
                        t0, tn = TILES[t]
                        pe.wait_ge((conv_act, conv_dve)[n % 2], done(it, g, n // 2))
                        for c in range(CB):
                            for s, (s0, sn) in enumerate(TILES):
                                last = pe.matmul(psD[0:tn, n % 2, c * GRP * CW:(c + 1) * GRP * CW],
                                                 toep[s][:, c0 + c, t0:t0 + tn],
                                                 uin[g][s][:, :, CW * (c0 + c):CW * (c0 + c + 1)],
                                                 start=(s == 0), stop=(s == 1))
                        last.then_inc(conv_full, 1)

            def conv_view(n):
                t, c0 = n // (STEPS // 2), n % (STEPS // 2) * CB
                tn = TILES[t][1]
                dst = yout[t][:, :, CW * c0:CW * (c0 + CB)].rearrange("p b (c r) -> p c b r", c=CB)
                src = psD[0:tn, n % 2, 0:CB * GRP * CW].rearrange("p (c b r) -> p c b r", c=CB, r=CW)
                return dst, src

            @blk.scalar
            def _(act):
                with act.Fori(0, GROUPS // BUFS) as it:
                    for g, n in [(g, n) for g in range(BUFS) for n in range(0, STEPS, 2)]:
                        if n % (STEPS // 2) == 0:
                            act.wait_ge(yout_out[n // (STEPS // 2)], shift(it, 16 * BUFS, 16 * g))
                        dst, src = conv_view(n)
                        act.wait_ge(conv_full, filled(it, g, n))
                        act.activation(dst, src, ACT.Copy).then_inc(conv_act, 1)

            @blk.vector
            def _(dve):
                with dve.Fori(0, GROUPS // BUFS) as it:
                    for g, n in [(g, n) for g in range(BUFS) for n in range(1, STEPS, 2)]:
                        if n % (STEPS // 2) == 1:
                            dve.wait_ge(yout_out[n // (STEPS // 2)], shift(it, 16 * BUFS, 16 * g))
                        dst, src = conv_view(n)
                        dve.wait_ge(conv_full, filled(it, g, n))
                        dve.tensor_copy(dst, src).then_inc(conv_dve, 1)

        with ExitStack() as st:
            def ssb(name, shape, dt=F32):
                return st.enter_context(nc.sbuf_tensor(name, shape, dt))

            counted = []

            def ssem(name):
                counted.append(st.enter_context(nc.semaphore(name)))
                return counted[-1]

            def two(name, shape, dt=F32):
                return [ssb(f"{name}_{q}", shape, dt) for q in range(2)]

            w1_s = ssb("w1_s", [P, EXPERTS, 2 * P])
            w2_s = ssb("w2_s", [P, EXPERTS, 2, P])
            b2_s = ssb("b2_s", [EXPERTS, P])
            wg_s = ssb("wg_s", [P, EXPERTS])
            bgb_s = ssb("bgb_s", [P, EXPERTS])
            esel_s = ssb("esel_s", [EXPERTS, EXPERTS, P])
            closed = ssb("closed", [EXPERTS, EXPERTS, P], BF16)
            rank_s = ssb("rank_s", [P, EXPERTS])
            anti_s = ssb("anti_s", [P, P])
            yin = two("yin", [P, IMG, 2, P])
            hoin = two("hoin", [P, N])
            yT = two("yT", [P, N])
            gel = two("gel", [P, N])
            h2 = two("h2", [P, N])
            sq = two("sq3", [P, N])
            lnv = two("lnv3", [P, N])
            rstd = two("rstd3", [P, N])
            h3 = two("h3", [P, N])
            logit = two("logit", [P, 2 * IMG, EXPERTS])
            top = two("top", [P, 2 * IMG])
            cand = two("cand", [P, 2 * IMG, EXPERTS])
            first = two("first", [P, 2 * IMG])
            hot = two("hot", [P, 2 * IMG, EXPERTS])
            hotT = two("hotT", [EXPERTS, N])
            hotb = two("hotb", [EXPERTS, N], BF16)
            hid = ssb("hid", [P, 4, N])
            h4 = two("h4", [P, N])
            yf = two("yf", [P, N])
            osb3 = two("osb3", [P, IMG, 2, P])

            w_in = st.enter_context(nc.semaphore("w_in"))
            closed_done = st.enter_context(nc.semaphore("closed_done"))
            full = [ssem(f"tail_full{b}") for b in range(4)]
            evac = [ssem(f"tail_evac{b}") for b in range(4)]
            rows_in = [ssem(f"rows_in{q}") for q in range(2)]
            out_done = [ssem(f"out_done{q}") for q in range(2)]
            h2_done = ssem("h2_done")
            sq_done = ssem("sq3_done")
            rstd_done = ssem("rstd3_done")
            route = ssem("route")
            w2_done = ssem("w2_done")
            moe_full = ssem("moe_full")
            h4_done = ssem("h4_done")
            back_part = ssem("back_part")
            sems = {"h2": h2_done, "sq": sq_done, "rstd": rstd_done, "route": route, "w2": w2_done,
                    "moe": moe_full, "h4": h4_done, "back": back_part,
                    "rows0": rows_in[0], "rows1": rows_in[1], "out0": out_done[0], "out1": out_done[1]}
            wl = [(w1_s, w1), (w2_s, w2), (b2_s, b2), (wg_s, wg), (bgb_s, bgb), (esel_s, esel), (rank_s, rank), (anti_s, anti)]
            ITERS = PAIRS // 2 - 1
            banks = [psD[:, 0, :], psD[:, 1, :], psA[:, 0, 0, :], psA[:, 1, 0, :]]
            tail_counts = [tail_count(part) for part in (TAIL_FIRST, TAIL_BODY, TAIL_LAST)]

            class Part:

                def __init__(self, part, it):
                    self.counts, self.part, self.it = tail_counts[part], part, it

                def value(self, name, x, more=0):
                    k = self.counts[name][0][x] + more
                    if self.part == 0:
                        return shift(0, 0, k)
                    return shift(self.it, tail_counts[1][name][1], tail_counts[0][name][1] + k)

            def wait(eng, at, name, x, more=0):
                eng.wait_ge(sems[name], at.value(name, x, more))

            def ready(eng, at, x):
                b = TAIL_BANK[x]
                eng.wait_ge(full[b], at.value(b, x))
                return banks[b]

            def result(eng, at, x):
                b = TAIL_BANK[x]
                eng.wait_ge(evac[b], at.value(b, x))

            def free(pe, at, x):
                b = TAIL_BANK[x]
                pe.wait_ge(evac[b], at.value(b, x, -1))
                return banks[b]

            def fulls(ins, x):
                ins.then_inc(full[TAIL_BANK[x]], 1)

            def evacs(ins, x):
                ins.then_inc(evac[TAIL_BANK[x]], 1)

            FULL = ((0, 128), (LAST0, 128))
            start(nc, counted)
            blk = st.enter_context(nc.Block())

            @blk.sync
            def _(sp):
                for t, src in wl:
                    sp.dma_start(t[:], src).then_inc(w_in, 16)
                y_pairs = y_dram.rearrange("t (i s b) p -> t i s b p", s=2, b=IMG)
                ho_pairs = ho_dram.rearrange("(i s) p n -> i s p n", s=2)

                def load(q, y_rows, ho_rows):
                    for t, (t0, tn) in enumerate(TILES):
                        sp.dma_start(yin[q][0:tn, :, t, :],
                                     y_rows[t0:t0 + tn].rearrange("t a b p -> t (a b) p")).then_inc(rows_in[q], 16)
                    sp.dma_start(hoin[q][:, :], ho_rows.rearrange("a p n -> (a p) n")).then_inc(rows_in[q], 16)

                def store(at, q, out_rows):
                    for t, (t0, tn) in enumerate(TILES):
                        if t == 0:
                            wait(sp, at, "back", ("back", q))
                        else:
                            result(sp, at, ("back", q))
                        sp.dma_start(out_rows[:, t0:t0 + tn].rearrange("b t d -> t b d"),
                                     osb3[q][0:tn, :, t, :]).then_inc(out_done[q], 16)

                for q in range(2):
                    load(q, y_pairs[:, 0:1, q], ho_pairs[2:3, q])
                y_next, ho_next = y_pairs[:, 1:], ho_pairs[3:]
                with sp.Fori(0, ITERS) as it:
                    at = Part(1, it)
                    for q in range(2):
                        wait(sp, at, "h2", ("h2", q), -1)
                        load(q, y_next[:, bass.ds(it, 1), q], ho_next[bass.ds(it, 1), q])
                        store(at, q, out[bass.ds(2 * IMG * it + IMG * q, IMG)])
                at = Part(2, ITERS)
                for q in range(2):
                    store(at, q, out[2 * IMG * ITERS + IMG * q:2 * IMG * ITERS + IMG * (q + 1)])
                for q in range(2):
                    sp.wait_ge(out_done[q], shift(0, 0, 16 * PAIRS))

            @blk.tensor
            def _(pe):
                pe.wait_ge(w_in, 16 * len(wl))
                pe.wait_ge(closed_done, 1)

                def product(at, x, weights, moving):
                    fulls(pe.matmul(free(pe, at, x)[:, 0:N], weights, moving, start=True, stop=True), x)

                def play(at, steps):
                    for x in steps:
                        step, q = x[0], x[1]
                        if step == "yT":
                            pe.wait_ge(rows_in[q], at.value(f"rows{q}", x))
                            ps = free(pe, at, x)
                            for b in range(IMG):
                                for t, (t0, tn) in enumerate(TILES):
                                    c0 = (b + 1) * TOK - t0 - tn
                                    last = pe.matmul(ps[:, c0:c0 + tn], yin[q][0:tn, b, t, :], anti_s[0:tn, P - tn:P],
                                                     start=True, stop=True)
                            fulls(last, x)
                        elif step == "out":
                            result(pe, at, ("yT", q))
                            product(at, x, wout_s[:, :], yT[q][:, :])
                        elif step == "xc":
                            wait(pe, at, "h2", ("h2", q))
                            product(at, x, cen_s[:, :], h2[q][:, :])
                        elif step == "xcf":
                            wait(pe, at, "h4", ("h4", q))
                            product(at, x, cen_s[:, :], h4[q][:, :])
                        elif step in ("var", "varf"):
                            wait(pe, at, "sq", (("xc", "xcf")[step == "varf"], q))
                            product(at, x, mean_s[:, :], sq[q][:, :])
                        elif step == "logit":
                            result(pe, at, ("xc", q))
                            ps = free(pe, at, x)
                            for b in range(IMG):
                                for t, (t0, tn) in enumerate(FULL):
                                    c0 = b * TOK + t0
                                    last = pe.matmul(ps[:, (2 * b + t) * EXPERTS:(2 * b + t + 1) * EXPERTS],
                                                     h3[q][:, c0:c0 + tn], wg_s[:, :], start=True, stop=True)
                            fulls(last, x)
                        elif step == "hotT":
                            wait(pe, at, "route", ("route", q))
                            ps = free(pe, at, x)
                            for b in range(IMG):
                                for t, (t0, tn) in enumerate(FULL):
                                    c0 = b * TOK + t0
                                    last = pe.matmul(ps[0:EXPERTS, c0:c0 + tn], hot[q][:, 2 * b + t, :], id_s[:, :],
                                                     start=True, stop=True)
                            fulls(last, x)
                        elif step == "exp":
                            e, j = x[2] // 2, x[2] % 2
                            if x[2] == 0:
                                b = TAIL_BANK[("hotT", q)]
                                pe.wait_ge(evac[b], at.value(b, ("half", q)))
                            ps = free(pe, at, x)
                            pe.matmul(ps[:, 0:N], w1_s[:, e, j * P:(j + 1) * P], h3[q][:, :], start=True, stop=False)
                            fulls(pe.matmul(ps[:, 0:N], closed[:, e, :], hotb[q][:, :], start=False, stop=True), x)
                        elif step == "w2":
                            n = x[2]
                            if n == 0:
                                wait(pe, at, "h4", ("half", q))
                            result(pe, at, ("exp", q, n))
                            pe.matmul(psO[:, q, 0:N], w2_s[:, n // 2, n % 2, :], hid[:, n % 4, :], start=(n == 0),
                                      stop=False).then_inc(w2_done, 1)
                        elif step == "b2":
                            pe.matmul(psO[:, q, 0:N], b2_s[:, :], hotT[q][:, :], start=False,
                                      stop=True).then_inc(moe_full, 1)
                        elif step == "back":
                            result(pe, at, ("xcf", q))
                            ps = free(pe, at, x)
                            for b in range(IMG):
                                for t, (t0, tn) in enumerate(TILES):
                                    c0 = b * TOK + t0
                                    last = pe.matmul(ps[0:tn, (2 * b + t) * P:(2 * b + t + 1) * P],
                                                     yf[q][:, c0:c0 + tn], id_s[:, :], start=True, stop=True)
                            fulls(last, x)

                play(Part(0, 0), TAIL_FIRST)
                with pe.Fori(0, ITERS) as it:
                    play(Part(1, it), TAIL_BODY)
                play(Part(2, ITERS), TAIL_LAST)

            @blk.scalar
            def _(act):
                act.wait_ge(w_in, 16 * len(wl))
                act.preload_act_table_set(NORM_SET)

                def play(at, steps):
                    for x in steps:
                        step, q = x[0], x[1]
                        if step == "out":
                            evacs(act.activation(gel[q][:, :], ready(act, at, x)[:, 0:N], ACT.Gelu,
                                                 bias=boutc_s[:, 0:1]), x)
                            act.preload_act_table_set(NORM_SET)
                        elif step in ("xc", "xcf"):
                            act.activation(sq[q][:, :], ready(act, at, x)[:, 0:N], ACT.Square).then_inc(sq_done, 1)
                        elif step in ("var", "varf"):
                            evacs(act.activation(lnv[q][:, :], ready(act, at, x)[:, 0:N], ACT.Ln, bias=eps_s[:, 0:1]), x)
                            result(act, at, x)
                            act.activation(rstd[q][:, :], lnv[q][:, :], ACT.Exp, scale=-0.5).then_inc(rstd_done, 1)
                        elif step == "exp" and x[2] % 2 == 0:
                            n = x[2]
                            ps = ready(act, at, x)
                            wait(act, at, "w2", ("w2", q, 0), max(n - 3, 0) - 1)
                            evacs(act.activation(hid[:, n % 4, :], ps[:, 0:N], ACT.Relu, bias=b1c_s[:, n:n + 1]), x)

                play(Part(0, 0), TAIL_FIRST)
                with act.Fori(0, ITERS) as it:
                    play(Part(1, it), TAIL_BODY)
                play(Part(2, ITERS), TAIL_LAST)

            @blk.vector
            def _(dve):
                dve.wait_ge(w_in, 16 * len(wl))
                dve.tensor_scalar(closed[:, :, :], esel_s[:, :, :], NEG, None, ALU.mult).then_inc(closed_done, 1)
                dve.wait_ge(closed_done, 1)

                def play(at, steps):
                    for x in steps:
                        step, q = x[0], x[1]
                        if step == "yT":
                            evacs(dve.tensor_copy(yT[q][:, :], ready(dve, at, x)[:, 0:N]), x)
                        elif step == "h2":
                            result(dve, at, ("out", q))
                            dve.scalar_tensor_tensor(out=h2[q][:, :], in0=hoin[q][:, :], scalar=2.0, in1=gel[q][:, :],
                                                     op0=ALU.mult, op1=ALU.add).then_inc(h2_done, 1)
                        elif step == "h3":
                            wait(dve, at, "rstd", ("var", q))
                            evacs(dve.tensor_tensor(h3[q][:, :], ready(dve, at, ("xc", q))[:, 0:N], rstd[q][:, :],
                                                    ALU.mult), ("xc", q))
                        elif step == "route":
                            ps = ready(dve, at, ("logit", q))
                            lg, tp, cd, fi = logit[q][:, :, :], top[q][:, :], cand[q][:, :, :], first[q][:, :]
                            sh = [P, 2 * IMG, EXPERTS]
                            evacs(dve.tensor_tensor(lg, ps[:, 0:2 * IMG * EXPERTS].rearrange("p (t e) -> p t e", e=EXPERTS),
                                                    bgb_s[:, :].unsqueeze(1).to_broadcast(sh), ALU.add), ("logit", q))
                            result(dve, at, ("logit", q))
                            dve.tensor_reduce(tp, lg, AX_X, ALU.max).then_inc(route, 1)
                            wait(dve, at, "route", x, -4)
                            dve.tensor_tensor(cd, lg, tp.unsqueeze(2).to_broadcast(sh), ALU.is_equal).then_inc(route, 1)
                            wait(dve, at, "route", x, -3)
                            dve.tensor_tensor(cd, cd, rank_s[:, :].unsqueeze(1).to_broadcast(sh), ALU.mult).then_inc(route, 1)
                            wait(dve, at, "route", x, -2)
                            dve.tensor_reduce(fi, cd, AX_X, ALU.max).then_inc(route, 1)
                            wait(dve, at, "route", x, -1)
                            dve.tensor_tensor(hot[q][:, :, :], cd, fi.unsqueeze(2).to_broadcast(sh),
                                              ALU.is_equal).then_inc(route, 1)
                        elif step == "hotT":
                            ps = ready(dve, at, x)
                            dve.tensor_copy(hotb[q][:, :], ps[0:EXPERTS, 0:N])
                            evacs(dve.tensor_copy(hotT[q][:, :], ps[0:EXPERTS, 0:N]), x)
                        elif step == "exp" and x[2] % 2 == 1:
                            n = x[2]
                            ps = ready(dve, at, x)
                            wait(dve, at, "w2", ("w2", q, 0), max(n - 3, 0) - 1)
                            evacs(dve.tensor_scalar(hid[:, n % 4, :], ps[:, 0:N], b1c_s[:, n:n + 1], 0.0, ALU.add,
                                                    ALU.max), x)
                        elif step == "h4":
                            wait(dve, at, "moe", ("half", 1 - q))
                            dve.tensor_tensor(h4[q][:, :], psO[:, q, 0:N], h3[q][:, :], ALU.add).then_inc(h4_done, 1)
                        elif step == "yf":
                            wait(dve, at, "rstd", ("varf", q))
                            evacs(dve.tensor_tensor(yf[q][:, :], ready(dve, at, ("xcf", q))[:, 0:N], rstd[q][:, :],
                                                    ALU.mult), ("xcf", q))
                        elif step == "back":
                            ps = ready(dve, at, x)
                            dve.wait_ge(out_done[q], at.value(f"out{q}", x, -32))
                            pv = ps.rearrange("p (b t d) -> p b t d", b=IMG, t=2)
                            for t, (t0, tn) in enumerate(TILES):
                                for b in range(IMG):
                                    last = dve.tensor_copy(osb3[q][0:tn, b, t, :], pv[0:tn, b, t, :])
                                if t == 0:
                                    last.then_inc(back_part, 1)
                            evacs(last, x)

                play(Part(0, 0), TAIL_FIRST)
                with dve.Fori(0, ITERS) as it:
                    play(Part(1, it), TAIL_BODY)
                play(Part(2, ITERS), TAIL_LAST)

TURNS = 0.15915494309189535
MAGIC = 12582912.0
PI2 = (6.28125, 0.0019350051879882812, 3.0199159819567e-07)
PI_BELOW = 3.1415925

_INS = ["x", "conv", "convb", "clsc", "posT", "qkv", "qkvb", "projp", "projn", "projb", "ln1", "fc1", "fc1b", "fc2",
        "fc2b", "ln2", "normwb", "attg", "win", "binb", "wout", "boutc", "lre", "lim", "bm", "cre", "cim", "dvec",
        "w1", "b1c", "w2", "b2", "wg", "bgb", "om", "ident", "cen", "mean", "gsel", "esel", "rank", "anti"]


def layouts(i, np):
    L, D = DEPTH, P
    v = {k.replace("L0_", ""): np.asarray(a) for k, a in i.items()}
    a = {}
    x = v["x"]
    b = x.shape[0]
    xp = x.reshape(b // 2, 2, 3, 14, 16, 14, 16).transpose(0, 2, 4, 6, 1, 3, 5).reshape(b // 2, KCH, D, 2 * PATCH)
    xp = xp.transpose(0, 2, 1, 3)
    a["x"] = np.concatenate([xp, xp[:2]], axis=0)
    a["conv"] = v["tok_conv_w"].reshape(KCH, D, D).transpose(1, 0, 2)
    a["convb"] = v["tok_conv_b"][:, None]
    a["clsc"] = v["tok_cls_token"].reshape(D, 1)
    a["posT"] = v["tok_pos_embed"][0].T
    def apart(w):
        w = w.reshape(w.shape[:-1] + (3, HEADS, HD)).copy()
        w[..., :2, :, :] = w[..., :2, :, :].swapaxes(-1, -2).reshape(w[..., :2, :, :].shape)
        return w.reshape(w.shape[:-3] + (3 * D,))

    a["qkv"] = apart(v["tok_qkv_w"]).transpose(1, 0, 2)
    a["qkvb"] = apart(v["tok_qkv_b"]).reshape(L * 3, D).T
    pj = v["tok_proj_w"]
    pp = np.zeros((L, 2, 4, 32, D), pj.dtype)
    pp[:, :, :, :HD] = pj.reshape(L, 2, 4, HD, D)
    a["projp"] = pp.reshape(L, 2, D, D).transpose(2, 0, 1, 3)
    a["projn"] = pj.transpose(1, 0, 2)
    a["projb"] = v["tok_proj_b"].T
    a["ln1"] = np.concatenate([v["tok_ln1_w"], v["tok_ln1_b"]]).T
    a["ln2"] = np.concatenate([v["tok_ln2_w"], v["tok_ln2_b"]]).T
    a["fc1"] = v["tok_fc1_w"].transpose(1, 0, 2)
    a["fc1b"] = v["tok_fc1_b"].reshape(L * 2, D).T
    a["fc2"] = v["tok_fc2_w"].reshape(L, 2, D, D).transpose(2, 0, 1, 3)
    a["fc2b"] = v["tok_fc2_b"].T
    a["normwb"] = np.stack([v["tok_norm_w"], v["tok_norm_b"]], 1)
    a["attg"] = np.stack([v["attn_ln_gamma"], v["attn_ln_beta"]], 1)
    a["win"] = v["attn_Win"]
    a["binb"] = np.broadcast_to(v["attn_bin_"], (D, D))
    a["wout"] = v["attn_Wout"]
    a["boutc"] = v["attn_bout"][:, None]
    for n, k in (("lre", "attn_Lambda_re"), ("lim", "attn_Lambda_im"), ("bm", "attn_Bmat"), ("cre", "attn_C_re"),
                 ("cim", "attn_C_im")):
        a[n] = v[k].reshape(CG, D).T
    a["dvec"] = v["attn_Dvec"][:, None]
    a["w1"] = v["ffn_W1"].transpose(1, 0, 2)
    a["b1c"] = v["ffn_b1"].reshape(2 * EXPERTS, D).T
    a["w2"] = v["ffn_W2"].reshape(EXPERTS, 2, D, D).transpose(2, 0, 1, 3)
    a["b2"] = v["ffn_b2"]
    a["wg"] = v["ffn_Wg"]
    a["bgb"] = np.broadcast_to(v["ffn_bg"], (D, EXPERTS))
    f = np.float32
    j = (TOK - 1) - np.arange(GEN)
    a["om"] = np.broadcast_to(np.where(j >= 0, j, -j - 1).astype(f), (D, GEN))
    a["ident"] = np.eye(D, dtype=f)
    a["anti"] = np.eye(D, dtype=f)[::-1]
    a["cen"] = (np.eye(D) - 1.0 / D).astype(f)
    a["mean"] = np.full((D, D), 1.0 / D, f)
    r = np.arange(D)
    a["gsel"] = (r[:, None] == (r // 32 * 32 + HD)[None, :]).astype(f)
    a["esel"] = np.broadcast_to((1 - np.eye(EXPERTS))[:, :, None], (EXPERTS, EXPERTS, D)).astype(f)
    a["rank"] = np.broadcast_to(np.arange(EXPERTS, 0, -1).astype(f), (D, EXPERTS))
    return {k: np.ascontiguousarray(a[k]) for k in _INS}


def kernel(**inputs):
    import numpy as np
    import concourse.bacc as bacc
    from concourse.bass_utils import run_bass_kernel_spmd

    arrays = layouts(inputs, np)
    batch = inputs["x"].shape[0]
    nc = bacc.Bacc("TRN2", target_bir_lowering=False, num_devices=1)
    args = {k: nc.dram_tensor(k, a.shape, mybir.dt.from_np(a.dtype), kind="ExternalInput").ap()
            for k, a in arrays.items()}
    args["out"] = nc.dram_tensor("out", (batch, TOK, P), F32, kind="ExternalOutput").ap()
    build(nc, **args)
    r = run_bass_kernel_spmd(nc, [arrays], core_ids=[0])
    return r.results[0]["out"]
```
